# Optimizing a Trainium2 kernel written in Bass

```python
import numpy as np
import jax
import jax.numpy as jnp

def _softmax(x, axis=-1):
    return jax.nn.softmax(x, axis=axis)

def _gelu(x):
    return jax.nn.gelu(x, approximate=True)

def _silu(x):
    return jax.nn.silu(x)

def _sigmoid(x):
    return jax.nn.sigmoid(x)

def _layernorm(x, axis=-1, eps=1e-05):
    m = jnp.mean(x, axis=axis, keepdims=True)
    v = jnp.var(x, axis=axis, keepdims=True)
    return (x - m) / jnp.sqrt(v + eps)

def _scatter_add(tgt, idx, src, axis=0):
    return tgt.at[idx].add(src)

def _segment_sum(src, seg, n):
    return jax.ops.segment_sum(src, seg, n)
kernel_name = 'mk_xattn_ffn_d4_seqx_r4_4ef9a9'

def setup_inputs(seed: int=0):
    np.random.seed(seed)
    _w = jnp.asarray

    def _rec_inputs():
        import jax
        import jax.numpy as jnp
        _rk = jax.random.key(seed)
        x = 0.0003765 + 1 * jax.random.normal(jax.random.fold_in(_rk, 1), (16, 128, 256), jnp.float32)
        _lenS = 128 - jax.random.randint(jax.random.fold_in(_rk, 7), (16,), 0, max(1, 128 // 4) + 1, jnp.int32)
        _lenS2 = 128 - jax.random.randint(jax.random.fold_in(_rk, 8), (16,), 0, max(1, 128 // 4) + 1, jnp.int32)
        _ctx_1024P = jax.random.normal(jax.random.fold_in(_rk, 11), (16, 16, 256), jnp.float32)
        _ctx_1024c = jax.random.dirichlet(jax.random.fold_in(_rk, 511), 0.3 * jnp.ones((16,), jnp.float32), (16, 128))
        _ctx_1024t = jnp.einsum('bsk,bkd->bsd', _ctx_1024c, _ctx_1024P)
        _ctx_1024t = _ctx_1024t * jax.lax.rsqrt(jnp.mean(jnp.square(_ctx_1024t)) + 1e-12) * 0.953939
        ctx_1024 = -0.000292821 + 1.00034 * (_ctx_1024t + 0.3 * jax.random.normal(jax.random.fold_in(_rk, 611), (16, 128, 256), jnp.float32))
        _validS = jnp.arange(128)[None, :] < _lenS[:, None]
        _validS2 = jnp.arange(128)[None, :] < _lenS2[:, None]
        _causal = jnp.tril(jnp.ones((128, 128), dtype=bool))
        mask_Bx1xSxS2_ik1 = jnp.where(jnp.broadcast_to(_validS2[:, None, None, :], (16, 1, 128, 128)), 1, 0).astype(jnp.int32)
        mask_BxS2_bf1 = jnp.ones((16, 128), dtype=bool)
        mask_Bx1x1xS2_ik0 = jnp.where(jnp.broadcast_to(_validS2[:, None, None, :], (16, 1, 1, 128)), 0, 1).astype(jnp.int32)
        return (x, ctx_1024, mask_Bx1xSxS2_ik1, mask_BxS2_bf1, mask_Bx1x1xS2_ik0)
    x, ctx_1024, mask_Bx1xSxS2_ik1, mask_BxS2_bf1, mask_Bx1x1xS2_ik0 = _rec_inputs()

    def _L0_xattn_setup():
        import jax, jax.numpy as jnp
        import numpy as np
        B, L, E, H = (2, 512, 256, 16)
        D = E // H
        key = jax.random.key(seed)
        ks = jax.random.split(key, 6)
        values = jax.random.normal(ks[0], (B, L, E), dtype=jnp.float32)
        keys = jax.random.normal(ks[1], (B, L, E), dtype=jnp.float32)
        query = jax.random.normal(ks[2], (B, L, E), dtype=jnp.float32)
        mask = jax.random.randint(ks[3], (B, 1, L, L), 0, 2, dtype=jnp.int32)
        W_out = jax.random.normal(ks[4], (E, E), dtype=jnp.float32) * 0.02
        b_out = jax.random.normal(ks[5], (E,), dtype=jnp.float32) * 0.02
        return {'values': values, 'keys': keys, 'query': query, 'mask': mask, 'W_out': W_out, 'b_out': b_out}
    _L0_xattn_all = _L0_xattn_setup()
    _L0_xattn_in = {k: v for k, v in _L0_xattn_all.items() if k in ('W_out', 'b_out')}
    del _L0_xattn_all

    def _L0_ffn_setup():
        import jax, jax.numpy as jnp
        import numpy as np
        S, B, H, F, E, K = (512, 2, 256, 512, 8, 2)

        def _moe_forward(hidden_states, router_w, w1, b1, w2, b2):
            s, b, h = hidden_states.shape
            T = s * b
            x = hidden_states.reshape(T, h)
            logits = jnp.einsum('th,eh->te', x, router_w)
            topk_logits, topk_idx = jax.lax.top_k(logits, K)
            probs = jax.nn.softmax(topk_logits, axis=-1)
            combine = jnp.zeros((T, E), dtype=x.dtype)
            combine = combine.at[jnp.arange(T)[:, None], topk_idx].add(probs.astype(x.dtype))
            hmid = jnp.einsum('th,efh->etf', x, w1) + b1[:, None, :]
            hmid = jax.nn.gelu(hmid, approximate=False)
            y = jnp.einsum('etf,ehf->eth', hmid, w2) + b2[:, None, :]
            out = jnp.einsum('eth,te->th', y, combine)
            return out.reshape(s, b, h)
        key = jax.random.key(seed)
        ks = jax.random.split(key, 6)
        std = 0.02
        return {'hidden_states': jax.random.normal(ks[0], (S, B, H), dtype=jnp.float32), 'router_w': jax.random.normal(ks[1], (E, H), dtype=jnp.float32) * std, 'w1': jax.random.normal(ks[2], (E, F, H), dtype=jnp.float32) * (1.0 / np.sqrt(H)), 'b1': jnp.zeros((E, F), dtype=jnp.float32), 'w2': jax.random.normal(ks[3], (E, H, F), dtype=jnp.float32) * (1.0 / np.sqrt(F)), 'b2': jnp.zeros((E, H), dtype=jnp.float32)}
    _L0_ffn_all = _L0_ffn_setup()
    _L0_ffn_in = {k: v for k, v in _L0_ffn_all.items() if k in ('router_w', 'w1', 'b1', 'w2', 'b2')}
    del _L0_ffn_all

    def _L1_xattn_setup():
        import jax, jax.numpy as jnp
        import numpy as np
        HEADS = 16
        CAUSAL = True
        NEG_BIAS = 999999.0
        key = jax.random.key(seed)
        k1, k2, k3 = jax.random.split(key, 3)
        B, Sq, Sk, C = (2, 512, 512, 256)
        return {'queries': jax.random.normal(k1, (B, Sq, C), dtype=jnp.float32), 'keys': jax.random.normal(k2, (B, Sk, C), dtype=jnp.float32), 'values': jax.random.normal(k3, (B, Sk, C), dtype=jnp.float32), 'queries_mask': jnp.ones((B, Sq), dtype=bool), 'values_mask': jnp.ones((B, Sk), dtype=bool)}
    _L1_xattn_all = _L1_xattn_setup()
    _L1_xattn_in = {k: v for k, v in _L1_xattn_all.items() if k in ()}
    del _L1_xattn_all

    def _L1_ffn_setup():
        import jax, jax.numpy as jnp
        import numpy as np
        BLOCK = 32
        W_BITS = 4
        ACT_BITS = 16

        def act_qdq(x):
            qmax = 2.0 ** (ACT_BITS - 1) - 1.0
            scale = jnp.maximum(jnp.max(jnp.abs(x)) / qmax, 1e-12)
            return jnp.clip(jnp.round(x / scale), -qmax - 1.0, qmax) * scale

        def fixed_qdq_u16(x):
            scale = 1.0 / 65536.0
            return jnp.clip(jnp.round(x / scale), 0.0, 65535.0) * scale

        def lpbq_dequant(w):
            O, I = w.shape
            qmax = 2.0 ** (W_BITS - 1) - 1.0
            wb = w.reshape(O, I // BLOCK, BLOCK)
            s = jnp.maximum(jnp.max(jnp.abs(wb), axis=-1, keepdims=True) / qmax, 1e-12)
            wq = jnp.clip(jnp.round(wb / s), -qmax - 1.0, qmax) * s
            return wq.reshape(O, I)
        key = jax.random.key(seed)
        k1, k2, k3, k4 = jax.random.split(key, 4)
        B, S, H, I = (2, 1024, 256, 768)
        x = jax.random.normal(k1, (B, S, H), jnp.float32)
        w_gate = jax.random.normal(k2, (I, H), jnp.float32) * 0.02
        w_up = jax.random.normal(k3, (I, H), jnp.float32) * 0.02
        w_down = jax.random.normal(k4, (H, I), jnp.float32) * 0.02
        return {'x': x, 'w_gate': w_gate, 'w_up': w_up, 'w_down': w_down}
    _L1_ffn_all = _L1_ffn_setup()
    _L1_ffn_in = {k: v for k, v in _L1_ffn_all.items() if k in ('w_gate', 'w_up', 'w_down')}
    del _L1_ffn_all

    def _L2_xattn_setup():
        import jax, jax.numpy as jnp
        import numpy as np
        D_MODEL = 256
        NUM_HEADS = 16
        NEG_BIG = 10000000000.0
        key = jax.random.key(seed)
        ks = jax.random.split(key, 7)
        B, S, D = (4, 512, D_MODEL)
        sc = 1.0 / np.sqrt(D)
        return {'q': jax.random.normal(ks[0], (B, S, D), jnp.float32), 'k': jax.random.normal(ks[1], (B, S, D), jnp.float32), 'v': jax.random.normal(ks[2], (B, S, D), jnp.float32), 'Wq': jax.random.normal(ks[3], (D, D), jnp.float32) * sc, 'bq': jnp.zeros((D,), jnp.float32), 'Wo': jax.random.normal(ks[4], (D, D), jnp.float32) * sc, 'bo': jnp.zeros((D,), jnp.float32)}
    _L2_xattn_all = _L2_xattn_setup()
    _L2_xattn_in = {k: v for k, v in _L2_xattn_all.items() if k in ('Wq', 'bq', 'Wo', 'bo')}
    del _L2_xattn_all

    def _L2_ffn_setup():
        import jax, jax.numpy as jnp
        import numpy as np
        B, S, IN, OUT, E, R = (8, 1024, 256, 256, 8, 8)
        LORA_ALPHA = 16
        SCALING = LORA_ALPHA / R
        key = jax.random.key(seed)
        k = jax.random.split(key, 6)
        x = jax.random.normal(k[0], (B, S, IN), dtype=jnp.float32)
        base_w = jax.random.normal(k[1], (OUT, IN), dtype=jnp.float32) * 0.02
        base_b = jnp.zeros((OUT,), dtype=jnp.float32)
        lora_A = jax.random.normal(k[2], (IN, R), dtype=jnp.float32) * 0.02
        lora_B = jax.random.normal(k[3], (E, R, OUT), dtype=jnp.float32) * 0.02
        router_w = jax.random.normal(k[4], (E, IN), dtype=jnp.float32) * 0.02
        router_b = jnp.zeros((E,), dtype=jnp.float32)
        return {'x': x, 'base_w': base_w, 'base_b': base_b, 'lora_A': lora_A, 'lora_B': lora_B, 'router_w': router_w, 'router_b': router_b}
    _L2_ffn_all = _L2_ffn_setup()
    _L2_ffn_in = {k: v for k, v in _L2_ffn_all.items() if k in ('base_w', 'base_b', 'lora_A', 'lora_B', 'router_w', 'router_b')}
    del _L2_ffn_all

    def _L3_xattn_setup():
        import jax, jax.numpy as jnp
        import numpy as np
        B, S, E, H = (2, 512, 256, 16)
        DH = E // H
        key = jax.random.key(seed)
        ks = jax.random.split(key, 12)
        std = 1.0 / np.sqrt(E)
        inp = {'query': jax.random.normal(ks[0], (B, S, E), jnp.float32), 'key': jax.random.normal(ks[1], (B, S, E), jnp.float32), 'value': jax.random.normal(ks[2], (B, S, E), jnp.float32), 'mask': jax.random.randint(ks[3], (B, 1, 1, S), 0, 2, jnp.int32), 'Wq': jax.random.normal(ks[4], (E, E), jnp.float32) * std, 'bq': jnp.zeros((E,), jnp.float32), 'Wk': jax.random.normal(ks[5], (E, E), jnp.float32) * std, 'bk': jnp.zeros((E,), jnp.float32), 'Wv': jax.random.normal(ks[6], (E, E), jnp.float32) * std, 'bv': jnp.zeros((E,), jnp.float32), 'Wo': jax.random.normal(ks[7], (E, E), jnp.float32) * std, 'bo': jnp.zeros((E,), jnp.float32)}
        return inp
    _L3_xattn_all = _L3_xattn_setup()
    _L3_xattn_in = {k: v for k, v in _L3_xattn_all.items() if k in ('Wq', 'bq', 'Wk', 'bk', 'Wv', 'bv', 'Wo', 'bo')}
    del _L3_xattn_all

    def _L3_ffn_setup():
        import jax, jax.numpy as jnp
        import numpy as np
        DIM = 256
        INTER = 128
        E = 32
        TOPK = 4
        GROUPS = 8
        TOPK_GROUPS = 4
        SHARED_INTER = 2 * INTER
        ROUTE_SCALE = 1.0
        B, S = (8, 1024)

        def _gate(xf, gw, gb):
            T = xf.shape[0]
            scores = jax.nn.softmax((xf @ gw + gb).astype(jnp.float32), axis=-1)
            original_scores = scores
            scores_g = scores.reshape(T, GROUPS, E // GROUPS)
            group_scores = jnp.sum(jax.lax.top_k(scores_g, 2)[0], axis=-1)
            gidx = jax.lax.top_k(group_scores, TOPK_GROUPS)[1]
            keep = jnp.zeros((T, GROUPS), bool).at[jnp.arange(T)[:, None], gidx].set(True)
            masked = jnp.where(keep[:, :, None], scores_g, -jnp.inf).reshape(T, E)
            indices = jax.lax.top_k(masked, TOPK)[1]
            weights = jnp.take_along_axis(original_scores, indices, axis=1) * ROUTE_SCALE
            return (weights.astype(xf.dtype), indices)
        key = jax.random.key(seed)
        ks = jax.random.split(key, 16)

        def xav(k, shape):
            fan_in, fan_out = (shape[-2], shape[-1])
            lim = np.sqrt(6.0 / (fan_in + fan_out))
            return jax.random.uniform(k, shape, jnp.float32, -lim, lim)
        return {'x': jax.random.normal(ks[0], (B, S, DIM), jnp.float32), 'gw': xav(ks[1], (DIM, E)), 'gb': jnp.zeros((E,), jnp.float32), 'w1': xav(ks[2], (E, DIM, INTER)), 'b1': jnp.zeros((E, INTER), jnp.float32), 'w3': xav(ks[3], (E, DIM, INTER)), 'b3': jnp.zeros((E, INTER), jnp.float32), 'w2': xav(ks[4], (E, INTER, DIM)), 'b2': jnp.zeros((E, DIM), jnp.float32), 'sw1': xav(ks[5], (DIM, SHARED_INTER)), 'sb1': jnp.zeros((SHARED_INTER,), jnp.float32), 'sw3': xav(ks[6], (DIM, SHARED_INTER)), 'sb3': jnp.zeros((SHARED_INTER,), jnp.float32), 'sw2': xav(ks[7], (SHARED_INTER, DIM)), 'sb2': jnp.zeros((DIM,), jnp.float32)}
    _L3_ffn_all = _L3_ffn_setup()
    _L3_ffn_in = {k: v for k, v in _L3_ffn_all.items() if k in ('gw', 'gb', 'w1', 'b1', 'w3', 'b3', 'w2', 'b2', 'sw1', 'sb1', 'sw3', 'sb3', 'sw2', 'sb2')}
    del _L3_ffn_all
    return {'x': x, 'ctx_1024': ctx_1024, 'mask_Bx1xSxS2_ik1': mask_Bx1xSxS2_ik1, 'mask_BxS2_bf1': mask_BxS2_bf1, 'mask_Bx1x1xS2_ik0': mask_Bx1x1xS2_ik0, 'L0_xattn_W_out': _L0_xattn_in['W_out'], 'L0_xattn_b_out': _L0_xattn_in['b_out'], 'L0_ffn_router_w': _L0_ffn_in['router_w'], 'L0_ffn_w1': _L0_ffn_in['w1'], 'L0_ffn_b1': _L0_ffn_in['b1'], 'L0_ffn_w2': _L0_ffn_in['w2'], 'L0_ffn_b2': _L0_ffn_in['b2'], 'L1_ffn_w_gate': _L1_ffn_in['w_gate'], 'L1_ffn_w_up': _L1_ffn_in['w_up'], 'L1_ffn_w_down': _L1_ffn_in['w_down'], 'L2_xattn_Wq': _L2_xattn_in['Wq'], 'L2_xattn_bq': _L2_xattn_in['bq'], 'L2_xattn_Wo': _L2_xattn_in['Wo'], 'L2_xattn_bo': _L2_xattn_in['bo'], 'L2_ffn_base_w': _L2_ffn_in['base_w'], 'L2_ffn_base_b': _L2_ffn_in['base_b'], 'L2_ffn_lora_A': _L2_ffn_in['lora_A'], 'L2_ffn_lora_B': _L2_ffn_in['lora_B'], 'L2_ffn_router_w': _L2_ffn_in['router_w'], 'L2_ffn_router_b': _L2_ffn_in['router_b'], 'L3_xattn_Wq': _L3_xattn_in['Wq'], 'L3_xattn_bq': _L3_xattn_in['bq'], 'L3_xattn_Wk': _L3_xattn_in['Wk'], 'L3_xattn_bk': _L3_xattn_in['bk'], 'L3_xattn_Wv': _L3_xattn_in['Wv'], 'L3_xattn_bv': _L3_xattn_in['bv'], 'L3_xattn_Wo': _L3_xattn_in['Wo'], 'L3_xattn_bo': _L3_xattn_in['bo'], 'L3_ffn_gw': _L3_ffn_in['gw'], 'L3_ffn_gb': _L3_ffn_in['gb'], 'L3_ffn_w1': _L3_ffn_in['w1'], 'L3_ffn_b1': _L3_ffn_in['b1'], 'L3_ffn_w3': _L3_ffn_in['w3'], 'L3_ffn_b3': _L3_ffn_in['b3'], 'L3_ffn_w2': _L3_ffn_in['w2'], 'L3_ffn_b2': _L3_ffn_in['b2'], 'L3_ffn_sw1': _L3_ffn_in['sw1'], 'L3_ffn_sb1': _L3_ffn_in['sb1'], 'L3_ffn_sw3': _L3_ffn_in['sw3'], 'L3_ffn_sb3': _L3_ffn_in['sb3'], 'L3_ffn_sw2': _L3_ffn_in['sw2'], 'L3_ffn_sb2': _L3_ffn_in['sb2']}

def reference(x, ctx_1024, mask_Bx1xSxS2_ik1, mask_BxS2_bf1, mask_Bx1x1xS2_ik0, L0_xattn_W_out, L0_xattn_b_out, L0_ffn_router_w, L0_ffn_w1, L0_ffn_b1, L0_ffn_w2, L0_ffn_b2, L1_ffn_w_gate, L1_ffn_w_up, L1_ffn_w_down, L2_xattn_Wq, L2_xattn_bq, L2_xattn_Wo, L2_xattn_bo, L2_ffn_base_w, L2_ffn_base_b, L2_ffn_lora_A, L2_ffn_lora_B, L2_ffn_router_w, L2_ffn_router_b, L3_xattn_Wq, L3_xattn_bq, L3_xattn_Wk, L3_xattn_bk, L3_xattn_Wv, L3_xattn_bv, L3_xattn_Wo, L3_xattn_bo, L3_ffn_gw, L3_ffn_gb, L3_ffn_w1, L3_ffn_b1, L3_ffn_w3, L3_ffn_b3, L3_ffn_w2, L3_ffn_b2, L3_ffn_sw1, L3_ffn_sb1, L3_ffn_sw3, L3_ffn_sb3, L3_ffn_sw2, L3_ffn_sb2):
    import jax
    import jax.numpy as jnp

    def _L0_xattn_ref(values, keys, query, mask, W_out, b_out):
        import jax, jax.numpy as jnp
        import numpy as np
        B, L, E, H = (2, 512, 256, 16)
        D = E // H
        b, l, e = query.shape
        v = values.reshape(b, l, H, D)
        k = keys.reshape(b, l, H, D)
        q = query.reshape(b, l, H, D)
        scores = jnp.einsum('bqhd,bkhd->bhqk', q, k)
        scores = jnp.where(mask == 0, jnp.float32(-1e+20), scores)
        attn = jax.nn.softmax(scores / jnp.float32(E ** 0.5), axis=3)
        out = jnp.einsum('bhqk,bkhd->bqhd', attn, v).reshape(b, l, e)
        out = out @ W_out.T + b_out
        return out

    def _L0_ffn_ref(hidden_states, router_w, w1, b1, w2, b2):
        import jax, jax.numpy as jnp
        import numpy as np
        S, B, H, F, E, K = (512, 2, 256, 512, 8, 2)

        def _moe_forward(hidden_states, router_w, w1, b1, w2, b2):
            s, b, h = hidden_states.shape
            T = s * b
            x = hidden_states.reshape(T, h)
            logits = jnp.einsum('th,eh->te', x, router_w)
            topk_logits, topk_idx = jax.lax.top_k(logits, K)
            probs = jax.nn.softmax(topk_logits, axis=-1)
            combine = jnp.zeros((T, E), dtype=x.dtype)
            combine = combine.at[jnp.arange(T)[:, None], topk_idx].add(probs.astype(x.dtype))
            hmid = jnp.einsum('th,efh->etf', x, w1) + b1[:, None, :]
            hmid = jax.nn.gelu(hmid, approximate=False)
            y = jnp.einsum('etf,ehf->eth', hmid, w2) + b2[:, None, :]
            out = jnp.einsum('eth,te->th', y, combine)
            return out.reshape(s, b, h)
        return _moe_forward(hidden_states, router_w, w1, b1, w2, b2)

    def _L1_xattn_ref(queries, keys, values, queries_mask, values_mask):
        import jax, jax.numpy as jnp
        import numpy as np
        HEADS = 16
        CAUSAL = True
        NEG_BIAS = 999999.0
        B, Sq, C = queries.shape
        Sk = keys.shape[1]
        H = HEADS
        d = C // H
        q = queries.reshape(B, Sq, H, d).transpose(2, 0, 1, 3)
        k = keys.reshape(B, Sk, H, d).transpose(2, 0, 1, 3)
        v = values.reshape(B, Sk, H, d).transpose(2, 0, 1, 3)
        scale = jnp.sqrt(jnp.float32(d))
        scores = jnp.einsum('hbqd,hbkd->hbqk', q, k) / scale
        mask = values_mask[None, :, None, :]
        if CAUSAL:
            causal = jnp.arange(Sq)[:, None] >= jnp.arange(Sk)[None, :]
            mask = jnp.logical_and(mask, causal[None, None])
        weights = jax.nn.softmax(scores - NEG_BIAS * mask.astype(jnp.float32), axis=-1)
        out = jnp.einsum('hbqk,hbkd->hbqd', weights, v)
        out = out.transpose(1, 2, 0, 3).reshape(B, Sq, C)
        return jnp.where(queries_mask[:, :, None], out, jnp.zeros_like(out))

    def _L1_ffn_ref(x, w_gate, w_up, w_down):
        import jax, jax.numpy as jnp
        import numpy as np
        BLOCK = 32
        W_BITS = 4
        ACT_BITS = 16

        def act_qdq(x):
            qmax = 2.0 ** (ACT_BITS - 1) - 1.0
            scale = jnp.maximum(jnp.max(jnp.abs(x)) / qmax, 1e-12)
            return jnp.clip(jnp.round(x / scale), -qmax - 1.0, qmax) * scale

        def fixed_qdq_u16(x):
            scale = 1.0 / 65536.0
            return jnp.clip(jnp.round(x / scale), 0.0, 65535.0) * scale

        def lpbq_dequant(w):
            O, I = w.shape
            qmax = 2.0 ** (W_BITS - 1) - 1.0
            wb = w.reshape(O, I // BLOCK, BLOCK)
            s = jnp.maximum(jnp.max(jnp.abs(wb), axis=-1, keepdims=True) / qmax, 1e-12)
            wq = jnp.clip(jnp.round(wb / s), -qmax - 1.0, qmax) * s
            return wq.reshape(O, I)
        x = act_qdq(x)
        up = act_qdq(x @ lpbq_dequant(w_up).T)
        gate = act_qdq(x @ lpbq_dequant(w_gate).T)
        sig = fixed_qdq_u16(jax.nn.sigmoid(gate))
        gate = act_qdq(gate * sig)
        o = act_qdq(gate * up)
        return o @ lpbq_dequant(w_down).T

    def _L2_xattn_ref(q, k, v, Wq, bq, Wo, bo):
        import jax, jax.numpy as jnp
        import numpy as np
        D_MODEL = 256
        NUM_HEADS = 16
        NEG_BIG = 10000000000.0
        B, S, D = q.shape
        H = NUM_HEADS
        hd = D // H

        def proj_split(x):
            y = x @ Wq + bq
            return y.reshape(B, -1, H, hd).transpose(0, 2, 1, 3)
        qh, kh, vh = (proj_split(q), proj_split(k), proj_split(v))
        scale = jnp.sqrt(jnp.asarray(hd, jnp.float32))
        scores = jnp.einsum('bhqd,bhkd->bhqk', qh, kh) / scale
        i = jnp.arange(S)[:, None]
        j = jnp.arange(S)[None, :]
        mask = (i >= j).astype(scores.dtype)
        scores = scores * mask - jnp.asarray(NEG_BIG, scores.dtype) * (1.0 - mask)
        weights = jax.nn.softmax(scores, axis=-1)
        attn = jnp.einsum('bhqk,bhkd->bhqd', weights, vh)
        concat = attn.transpose(0, 2, 1, 3).reshape(B, S, D)
        return concat @ Wo + bo

    def _L2_ffn_ref(x, base_w, base_b, lora_A, lora_B, router_w, router_b):
        import jax, jax.numpy as jnp
        import numpy as np
        B, S, IN, OUT, E, R = (8, 1024, 256, 256, 8, 8)
        LORA_ALPHA = 16
        SCALING = LORA_ALPHA / R
        result = jnp.einsum('bsd,od->bso', x, base_w) + base_b
        logits = jnp.einsum('bsd,ed->bse', x, router_w) + router_b
        gating = jax.nn.softmax(logits, axis=-1).astype(jnp.bfloat16)
        mid = jnp.einsum('bsd,dr->bsr', x, lora_A)
        lora_out = jnp.einsum('bsr,erd,bse->bsd', mid, lora_B, gating.astype(jnp.float32))
        return result + lora_out * SCALING

    def _L3_xattn_ref(query, key, value, mask, Wq, bq, Wk, bk, Wv, bv, Wo, bo):
        import jax, jax.numpy as jnp
        import numpy as np
        B, S, E, H = (2, 512, 256, 16)
        DH = E // H
        b = query.shape[0]

        def split_heads(x):
            return x.reshape(b, -1, H, DH).transpose(0, 2, 1, 3)
        q = split_heads(query @ Wq + bq)
        k = split_heads(key @ Wk + bk)
        v = split_heads(value @ Wv + bv)
        scores = jnp.einsum('bhqd,bhkd->bhqk', q, k) / np.sqrt(DH).astype(np.float32)
        scores = jnp.where(mask == 0, jnp.float32(-1000000000.0), scores)
        attn = jax.nn.softmax(scores, axis=-1)
        out = jnp.einsum('bhqk,bhkd->bhqd', attn, v)
        out = out.transpose(0, 2, 1, 3).reshape(b, -1, E)
        return out @ Wo + bo

    def _L3_ffn_ref(x, gw, gb, w1, b1, w3, b3, w2, b2, sw1, sb1, sw3, sb3, sw2, sb2):
        import jax, jax.numpy as jnp
        import numpy as np
        DIM = 256
        INTER = 128
        E = 32
        TOPK = 4
        GROUPS = 8
        TOPK_GROUPS = 4
        SHARED_INTER = 2 * INTER
        ROUTE_SCALE = 1.0
        B, S = (8, 1024)

        def _gate(xf, gw, gb):
            T = xf.shape[0]
            scores = jax.nn.softmax((xf @ gw + gb).astype(jnp.float32), axis=-1)
            original_scores = scores
            scores_g = scores.reshape(T, GROUPS, E // GROUPS)
            group_scores = jnp.sum(jax.lax.top_k(scores_g, 2)[0], axis=-1)
            gidx = jax.lax.top_k(group_scores, TOPK_GROUPS)[1]
            keep = jnp.zeros((T, GROUPS), bool).at[jnp.arange(T)[:, None], gidx].set(True)
            masked = jnp.where(keep[:, :, None], scores_g, -jnp.inf).reshape(T, E)
            indices = jax.lax.top_k(masked, TOPK)[1]
            weights = jnp.take_along_axis(original_scores, indices, axis=1) * ROUTE_SCALE
            return (weights.astype(xf.dtype), indices)
        shape = x.shape
        xf = x.reshape(-1, DIM)
        T = xf.shape[0]
        weights, indices = _gate(xf, gw, gb)
        cw = jnp.zeros((T, E), xf.dtype).at[jnp.arange(T)[:, None], indices].add(weights)

        def body(y, p):
            w1e, b1e, w3e, b3e, w2e, b2e, we = p
            h = jax.nn.silu(xf @ w1e + b1e) * (xf @ w3e + b3e)
            return (y + we[:, None] * (h @ w2e + b2e), None)
        y0 = jnp.zeros_like(xf)
        y, _ = jax.lax.scan(body, y0, (w1, b1, w3, b3, w2, b2, cw.T))
        z = jax.nn.silu(xf @ sw1 + sb1) * (xf @ sw3 + sb3) @ sw2 + sb2
        return (y + z).reshape(shape)
    x = x + _L0_xattn_ref(ctx_1024, ctx_1024, _layernorm(x, axis=-1), mask_Bx1xSxS2_ik1, L0_xattn_W_out, L0_xattn_b_out)
    x = x + _L0_ffn_ref(_layernorm(x, axis=-1), L0_ffn_router_w, L0_ffn_w1, L0_ffn_b1, L0_ffn_w2, L0_ffn_b2)
    x = x + _L1_xattn_ref(_layernorm(x, axis=-1), ctx_1024, ctx_1024, mask_BxS2_bf1, mask_BxS2_bf1)
    x = x + _L1_ffn_ref(_layernorm(x, axis=-1), L1_ffn_w_gate, L1_ffn_w_up, L1_ffn_w_down)
    x = x + _L2_xattn_ref(_layernorm(x, axis=-1), ctx_1024, ctx_1024, L2_xattn_Wq, L2_xattn_bq, L2_xattn_Wo, L2_xattn_bo)
    x = x + _L2_ffn_ref(_layernorm(x, axis=-1), L2_ffn_base_w, L2_ffn_base_b, L2_ffn_lora_A, L2_ffn_lora_B, L2_ffn_router_w, L2_ffn_router_b)
    x = x + _L3_xattn_ref(_layernorm(x, axis=-1), ctx_1024, ctx_1024, mask_Bx1x1xS2_ik0, L3_xattn_Wq, L3_xattn_bq, L3_xattn_Wk, L3_xattn_bk, L3_xattn_Wv, L3_xattn_bv, L3_xattn_Wo, L3_xattn_bo)
    x = x + _L3_ffn_ref(_layernorm(x, axis=-1), L3_ffn_gw, L3_ffn_gb, L3_ffn_w1, L3_ffn_b1, L3_ffn_w3, L3_ffn_b3, L3_ffn_w2, L3_ffn_b2, L3_ffn_sw1, L3_ffn_sb1, L3_ffn_sw3, L3_ffn_sb3, L3_ffn_sw2, L3_ffn_sb2)
    return x

_drawn_inputs = setup_inputs


def setup_inputs(seed=0):
    import zlib

    import numpy as np

    out = dict(_drawn_inputs(seed))
    spreads = {'L0_ffn_b1': (0.0, 0.1),
     'L0_ffn_b2': (0.0, 0.1),
     'L2_xattn_bq': (0.0, 0.1),
     'L2_xattn_bo': (0.0, 0.1),
     'L2_ffn_base_b': (0.0, 0.1),
     'L2_ffn_router_b': (0.0, 0.8),
     'L3_xattn_bq': (0.0, 0.408),
     'L3_xattn_bk': (0.0, 2.0),
     'L3_xattn_bv': (0.0, 0.1),
     'L3_xattn_bo': (0.0, 0.1),
     'L3_ffn_gb': (0.0, 0.461),
     'L3_ffn_b1': (0.0, 0.8),
     'L3_ffn_b3': (0.0, 0.8),
     'L3_ffn_b2': (0.0, 0.491),
     'L3_ffn_sb1': (0.0, 0.281),
     'L3_ffn_sb3': (0.0, 0.292),
     'L3_ffn_sb2': (0.0, 0.1)}
    factors = {'L2_ffn_lora_A': 5.782, 'L2_ffn_lora_B': 5.834, 'L2_ffn_router_w': 8.0}
    for name, (base, spread) in spreads.items():
        noise = np.random.default_rng([zlib.crc32(name.encode()), seed]).standard_normal(out[name].shape)
        drawn = base * np.exp(spread * noise) if base else spread * noise
        out[name] = jnp.asarray(drawn.astype(out[name].dtype))
    for name, factor in factors.items():
        out[name] = (out[name] * factor).astype(out[name].dtype)
    return out
```

```python
import numpy as np
from contextlib import ExitStack

import concourse.bass as bass
from concourse import mybir

F32 = mybir.dt.float32
I32 = mybir.dt.int32
U32 = mybir.dt.uint32
U8 = mybir.dt.uint8
BF16 = mybir.dt.bfloat16
ALU = mybir.AluOpType
ACT = mybir.ActivationFunctionType
AXIS = mybir.AxisListType

B, S, D = 16, 128, 256
P = 128
KD = D // P
H, DH = 16, 16
T4 = 4
HB = P // T4
EPS = 1e-5
MASKED = -1e30


def one(i):
    return bass.ds(i, 1)


def row(t, i):
    return t[:, one(i), :].rearrange("p o d -> p (o d)")


def col(t, i):
    return t[:, one(i)]


class Chain:

    def __init__(self, eng, sem):
        self.eng, self.sem, self.n = eng, sem, 0

    def do(self, ins):
        self.n += 1
        ins.then_inc(self.sem, 1)
        self.eng.wait_ge(self.sem, self.n)


class Pool:

    def __init__(self, nc, stack, layer):
        self.nc, self.stack, self.layer, self.sems = nc, stack, layer, []
        stack.callback(self.clear)

    def sb(self, name, shape, dtype=F32):
        return self.stack.enter_context(self.nc.sbuf_tensor(f"{self.layer}_{name}", shape, dtype))

    def sem(self, name):
        self.sems.append(self.stack.enter_context(self.nc.semaphore(f"{self.layer}_{name}")))
        return self.sems[-1]

    def clear(self):
        if self.sems:
            with self.nc.Block() as block:

                @block.gpsimd
                def _(pool):
                    for s in self.sems:
                        pool.sem_clear(s)


def constants(nc, x_dram, X, ident, below):
    with ExitStack() as stack:
        m = Pool(nc, stack, "const")
        loaded, filled, made = m.sem("loaded"), m.sem("filled"), m.sem("made")
        with nc.Block() as block:

            @block.sync
            def _(sp):
                sp.dma_start(X[:, :, :], x_dram.rearrange("b p d -> p b d")).then_inc(loaded, 16)
                sp.wait_ge(loaded, 16)

            @block.gpsimd
            def _(pool):
                nc.gpsimd.memset(ident[:, :], 1.0).then_inc(filled, 1)
                nc.gpsimd.memset(below[:, :], 1.0).then_inc(filled, 1)
                pool.wait_ge(filled, 2)
                nc.gpsimd.affine_select(out=ident[:, :], in_=ident[:, :], compare_op=ALU.is_equal, fill=0.0,
                                        base=0, pattern=[[-1, P]], channel_multiplier=1).then_inc(made, 1)
                nc.gpsimd.affine_select(out=below[:, :], in_=below[:, :], compare_op=ALU.is_ge, fill=0.0,
                                        base=0, pattern=[[-1, P]], channel_multiplier=1).then_inc(made, 1)
                pool.wait_ge(made, 2)


def norm_statistics(nc, layer, X, mean, rstd, scale, loads, zeros=(), ones=()):
    with ExitStack() as stack:
        m = Pool(nc, stack, layer + "_stats")
        raw = m.sb("raw", [P, B, 6])
        t = [m.sb(f"t{k}", [P, B]) for k in range(5)]
        halves, chain, var_ready, root_ready = (m.sem(n) for n in ("halves", "chain", "var_ready", "root_ready"))
        filled, loaded = m.sem("filled"), m.sem("loaded")
        even, odd = raw[:, :, 0:3], raw[:, :, 3:6]
        with nc.Block() as block:

            @block.gpsimd
            def _(pool):
                for z in zeros:
                    nc.gpsimd.memset(z, 0.0).then_inc(filled, 1)
                for z in ones:
                    nc.gpsimd.memset(z, 1.0).then_inc(filled, 1)
                if zeros or ones:
                    pool.wait_ge(filled, len(zeros) + len(ones))

            @block.sync
            def _(sp):
                if zeros or ones:
                    sp.wait_ge(filled, len(zeros) + len(ones))
                for dst, src in loads:
                    sp.dma_start(dst, src).then_inc(loaded, 16)
                if loads:
                    sp.wait_ge(loaded, 16 * len(loads))

            @block.vector
            def _(dve):
                with dve.Fori(0, B) as b:
                    nc.vector.bn_stats(out=row(raw, b), in_=row(X, b)).then_inc(halves, 1)
                dve.wait_ge(halves, B)
                c = Chain(dve, chain)
                me, mo = even[:, :, 1:2].rearrange("p b o -> p (b o)"), odd[:, :, 1:2].rearrange("p b o -> p (b o)")
                ve, vo = even[:, :, 2:3].rearrange("p b o -> p (b o)"), odd[:, :, 2:3].rearrange("p b o -> p (b o)")
                c.do(nc.vector.tensor_tensor(t[0][:, :], me, mo, ALU.add))
                c.do(nc.vector.tensor_tensor(t[1][:, :], me, mo, ALU.subtract))
                c.do(nc.vector.tensor_scalar(mean[:, :], t[0][:, :], 0.5, None, ALU.mult))
                c.do(nc.vector.tensor_tensor(t[2][:, :], ve, vo, ALU.add))
                c.do(nc.vector.scalar_tensor_tensor(t[3][:, :], t[1][:, :], 0.25, t[1][:, :], ALU.mult, ALU.mult))
                c.do(nc.vector.scalar_tensor_tensor(t[0][:, :], t[2][:, :], 1.0 / D, t[3][:, :], ALU.mult, ALU.add))
                nc.vector.tensor_scalar(t[1][:, :], t[0][:, :], EPS, None, ALU.add).then_inc(var_ready, 1)
                dve.wait_ge(root_ready, 1)
                c.do(nc.vector.reciprocal(t[3][:, :], t[2][:, :]))
                c.do(nc.vector.tensor_tensor(t[0][:, :], t[3][:, :], t[3][:, :], ALU.mult))
                c.do(nc.vector.tensor_tensor(t[4][:, :], t[0][:, :], t[1][:, :], ALU.mult))
                c.do(nc.vector.tensor_scalar(t[0][:, :], t[4][:, :], -0.5, 1.5, ALU.mult, ALU.add))
                c.do(nc.vector.scalar_tensor_tensor(rstd[:, :], t[3][:, :], float(scale), t[0][:, :], ALU.mult, ALU.mult))

            @block.scalar
            def _(act):
                act.wait_ge(var_ready, 1)
                nc.scalar.activation(t[2][:, :], t[1][:, :], ACT.Sqrt).then_inc(root_ready, 1)


def attention(nc, layer, X, ident, below, ctx, ctxT, scale, mask_kind, mask=None, wq=None, bq=None, wk=None,
              bk=None, wv=None, bv=None, wo=None, bo=None):
    proj = wq is not None
    oproj = wo is not None
    with ExitStack() as stack:
        m = Pool(nc, stack, layer)
        mean, rstd = m.sb("mean", [P, B]), m.sb("rstd", [P, B])
        XN = D if proj else H * HB
        xn = m.sb("xn", [P, 2, XN])
        qT, kT = m.sb("qT", [P, 2, T4, P]), m.sb("kT", [P, 2, T4, P])
        vraw = m.sb("vraw", [P, 2, D])
        vx = m.sb("vx", [P, 2, H, DH + 1])
        NB = 1 if mask_kind == "causal" else B
        bias = m.sb("bias", [P, NB, P])
        t_sb, p_sb = m.sb("t", [P, T4, T4 * P]), m.sb("p", [P, T4, T4 * P])
        mx = m.sb("mx", [P, T4, T4])
        pT = m.sb("pT", [P, 2, T4, P])
        rec, o_n = m.sb("rec", [P, H]), m.sb("o_n", [P, D])
        loads, zeros, ones = [], [], [vx[:, :, :, DH:DH + 1]]
        if not proj:
            zeros.append(xn[:, :, :])
        if oproj:
            wo_sb = m.sb("wo", [P, KD, D])
            bo_sb = m.sb("bo", [P, D])
            oT = m.sb("oT", [P, KD, P])
            loads += [(wo_sb[:, :, :], wo.rearrange("(k p) n -> p k n", p=P)), (bo_sb[:, :], bo.partition_broadcast(P))]
        if proj:
            xT, cT = m.sb("xT", [P, 2, KD, P]), m.sb("cT", [P, 2, KD, P])
            wq_sb, wk_sb = m.sb("wq", [P, KD, H, HB]), m.sb("wk", [P, KD, H, HB])
            wv_sb, bv_sb = m.sb("wv", [P, KD, D]), m.sb("bv", [P, D])
            bq_sb, bk_sb, bqs = m.sb("bq", [P, T4]), m.sb("bk", [P, T4]), m.sb("bqs", [P, T4])
            zeros += [wq_sb[:, :, :, :], wk_sb[:, :, :, :], bq_sb[:, :], bk_sb[:, :]]
            for w_sb, w in ((wq_sb, wq), (wk_sb, wk)):
                loads += [(w_sb[:, k, :, 0:DH], w[k * P:(k + 1) * P, :].rearrange("p (h d) -> p h d", h=H)) for k in range(KD)]
            for b_sb, b in ((bq_sb, bq), (bk_sb, bk)):
                loads += [(b_sb[j * HB:j * HB + DH, :], b[j, :, :]) for j in range(T4)]
            loads += [(wv_sb[:, :, :], wv.rearrange("(k p) n -> p k n", p=P)), (bv_sb[:, :], bv.partition_broadcast(P))]
        if mask_kind == "int_qk":
            mask_in = m.sb("mask_in", [P, B, P], I32)
            loads.append((mask_in[:, :, :], mask.rearrange("b o q k -> (o q) b k")))
        elif mask_kind == "int_k":
            mask_in = m.sb("mask_in", [P, B, P], I32)
            loads.append((mask_in[:, :, :].rearrange("p b k -> p (b k)"), mask.rearrange("b x y k -> (x y b k)").partition_broadcast(P)))
        elif mask_kind == "inverted":
            mask_in, mask_q = m.sb("mask_in", [P, B, P], U8), m.sb("mask_q", [P, B], U8)
            qm = m.sb("qm", [P, B])
            inv = m.sb("inv", [P, P])
            loads += [(mask_in[:, :, :].rearrange("p b k -> p (b k)"), mask[0].rearrange("b k -> (b k)").partition_broadcast(P)),
                      (mask_q[:, :], mask[1])]
        norm_statistics(nc, layer, X, mean, rstd, 1.0 if proj else scale, loads, zeros, ones)

        PS = stack.enter_context(nc.psum_tensor(f"{layer}_ps", [P, 8, 512], F32))
        ps_s = PS[:, 0:4, :]
        ps_t = [PS[:, 4, :], PS[:, 5, :]]
        ps_v = PS[:, 6, 0:H * (DH + 1)].rearrange("p (h d) -> p h d", h=H)
        ps_q = PS[:, 7, :]

        prepared = m.sem("prepared")
        ctx_in = [m.sem("ctx_in0"), m.sem("ctx_in1")]
        xn_ready, x_done, x_copied = m.sem("xn_ready"), m.sem("x_done"), m.sem("x_copied")
        q_done, q_ready, k_done, k_ready = m.sem("q_done"), m.sem("q_ready"), m.sem("k_done"), m.sem("k_ready")
        v_done, v_ready = m.sem("v_done"), m.sem("v_ready")
        s_done, biased, maxed, shifted, exped = (m.sem(n) for n in ("s_done", "biased", "maxed", "shifted", "exped"))
        pT_done, pT_copied, av_done, inverted, normed = (m.sem(n) for n in ("pT_done", "pT_copied", "av_done", "inverted", "normed"))
        oT_done, oT_copied, o_done, bo_added, resid_done = (m.sem(n) for n in ("oT_done", "oT_copied", "o_done", "bo_added", "resid_done"))
        DMAS = 2 if proj else 5
        LAST = B - 1

        with nc.Block() as block:

            @block.vector
            def _(dve):
                c = Chain(dve, prepared)
                if mask_kind in ("int_qk", "int_k"):
                    c.do(nc.vector.tensor_scalar(bias[:, :, :], mask_in[:, :, :], 0.0, MASKED, ALU.is_equal, ALU.mult))
                elif mask_kind == "causal":
                    c.do(nc.vector.tensor_scalar(bias[:, 0, :], below[:, :], 0.0, MASKED, ALU.is_equal, ALU.mult))
                else:
                    c.do(nc.vector.tensor_scalar(inv[:, :], below[:, :], -999999.0, None, ALU.mult))
                    c.do(nc.vector.tensor_tensor(bias[:, :, :], mask_in[:, :, :], inv[:, :].unsqueeze(1).to_broadcast([P, B, P]), ALU.mult))
                    c.do(nc.vector.tensor_copy(qm[:, :], mask_q[:, :]))
                if proj:
                    c.do(nc.vector.tensor_scalar(bqs[:, :], bq_sb[:, :], scale, None, ALU.mult))

        def body(engine, run):
            run(-2, 0, True, False, False, False)
            run(-1, 1, True, True, False, False)
            run(0, 0, True, True, True, False)
            run(1, 1, True, True, True, True)
            with engine.Fori(1, (B - 2) // 2) as j:
                run(2 * j, 0, True, True, True, True)
                run(2 * j + 1, 1, True, True, True, True)
            run(LAST - 1, 0, False, True, True, True)
            run(LAST, 1, False, False, True, True)
            run(LAST + 1, 0, False, False, False, True)

        def known(i):
            return isinstance(i, int)

        with nc.Block() as block:

            @block.sync
            def _(sp):
                def run(i, u, queries, scores, values, output):
                    if queries:
                        k = i + 2
                        if not known(i) or k >= 2:
                            if proj:
                                sp.wait_ge(v_done, k - 1)
                            else:
                                sp.wait_ge(s_done, T4 * (k - 1))
                                sp.wait_ge(v_ready, k - 1)
                        if proj:
                            for d in range(KD):
                                sp.dma_start(cT[:, u, d, :], ctxT[one(k), d * P:(d + 1) * P, :].rearrange("o p s -> (o p) s"))\
                                  .then_inc(ctx_in[u], 16)
                        else:
                            for j in range(T4):
                                sp.dma_start(kT[j * HB:j * HB + DH, u, :, :],
                                             ctxT[one(k), :, :].rearrange("o (t j d) s -> j d (o t) s", j=T4, d=DH)[j])\
                                  .then_inc(ctx_in[u], 16)
                            sp.dma_start(vraw[:, u, :], ctx[one(k), :, :].rearrange("o s d -> (o s) d")).then_inc(ctx_in[u], 16)
                body(sp, run)

            @block.gpsimd
            def _(pool):
                def run(i, u, queries, scores, values, output):
                    if queries and oproj:
                        k = i + 2
                        pool.wait_ge(xn_ready, k + 1)
                        nc.gpsimd.tensor_tensor(row(X, k), row(X, k), bo_sb[:, :], ALU.add).then_inc(bo_added, 1)
                    if scores:
                        k, w = i + 1, 1 - u
                        if not proj:
                            loads_seen = 16 * DMAS * ((k - w) // 2 + 1) if known(i) else None
                            if known(i):
                                pool.wait_ge(ctx_in[w], loads_seen)
                            else:
                                pool.wait_ge(ctx_in[w], 8 * DMAS * (k - w) + 16 * DMAS)
                            if not known(i) or k >= 2:
                                pool.wait_ge(av_done, T4 * (k - 1))
                            nc.gpsimd.tensor_tensor(vx[:, w, :, 0:DH], vraw[:, w, :].rearrange("p (h d) -> p h d", h=H),
                                                    vx[:, w, :, DH:DH + 1].to_broadcast([P, H, DH]), ALU.mult).then_inc(v_ready, 1)
                        for c in range(T4):
                            pool.wait_ge(maxed, T4 * k + c + 1)
                            tc_ = t_sb[:, c, :].rearrange("p (t s) -> p t s", t=T4)
                            nc.gpsimd.tensor_tensor(tc_, tc_, mx[:, c, :].unsqueeze(2).to_broadcast([P, T4, P]), ALU.subtract)\
                              .then_inc(shifted, 1)
                body(pool, run)

            @block.vector
            def _(dve):
                def run(i, u, queries, scores, values, output):
                    if queries:
                        k = i + 2
                        if not known(i) or k >= 2:
                            dve.wait_ge(x_done, k - 1)
                        dst = xn[:, u, :] if proj else xn[:, u, :].rearrange("p (h e) -> p h e", h=H)[:, :, 0:DH]
                        src = row(X, k) if proj else row(X, k).rearrange("p (h d) -> p h d", h=H)
                        nc.vector.tensor_scalar(dst, src, col(mean, k), col(rstd, k), ALU.subtract, ALU.mult)\
                          .then_inc(xn_ready, 1)
                    if scores:
                        k, w = i + 1, 1 - u

                        def add_bias(c, k=k):
                            dve.wait_ge(s_done, T4 * k + c + 1)
                            if not known(i) or k >= 1:
                                dve.wait_ge(exped, T4 * (k - 1) + c + 1)
                            b = bias[:, 0, :] if NB == 1 else row(bias, k)
                            nc.vector.tensor_tensor(t_sb[:, c, :].rearrange("p (t s) -> p t s", t=T4),
                                                    ps_s[:, c, :].rearrange("p (t s) -> p t s", t=T4),
                                                    b.unsqueeze(1).to_broadcast([P, T4, P]), ALU.add).then_inc(biased, 1)

                        def maximum(c, k=k):
                            dve.wait_ge(biased, T4 * k + c + 1)
                            nc.vector.tensor_reduce(mx[:, c, :], t_sb[:, c, :].rearrange("p (t s) -> p t s", t=T4),
                                                    AXIS.X, ALU.max).then_inc(maxed, 1)
                        add_bias(0)
                        add_bias(1)
                        maximum(0)
                        add_bias(2)
                        maximum(1)
                        add_bias(3)
                    if output and oproj:
                        k = i - 1
                        dve.wait_ge(o_done, k + 1)
                        dve.wait_ge(bo_added, k + 1)
                        nc.vector.tensor_tensor(row(X, k), row(X, k), ps_t[1][:, 0:D], ALU.add).then_inc(resid_done, 1)
                    if queries and proj:
                        k = i + 2
                        dve.wait_ge(q_done, k + 1)
                        if not known(i) or k >= 2:
                            dve.wait_ge(s_done, T4 * (k - 1))
                        nc.vector.scalar_tensor_tensor(qT[:, u, :, :], ps_q.rearrange("p (t s) -> p t s", t=T4), float(scale),
                                                       bqs[:, :].unsqueeze(2).to_broadcast([P, T4, P]), ALU.mult, ALU.add)\
                          .then_inc(q_ready, 1)
                    if scores:
                        maximum(2)
                        maximum(3)
                        if proj:
                            dve.wait_ge(v_done, k_of(i, 1) + 1)
                            if not known(i) or i + 1 >= 2:
                                dve.wait_ge(av_done, T4 * i)
                            nc.vector.tensor_tensor(vx[:, 1 - u, :, 0:DH], ps_q[:, 0:D].rearrange("p (h d) -> p h d", h=H),
                                                    bv_sb[:, :].rearrange("p (h d) -> p h d", h=H), ALU.add).then_inc(v_ready, 1)
                    if values:
                        k = i
                        dve.wait_ge(av_done, T4 * (k + 1))
                        nc.vector.reciprocal(rec[:, :], ps_v[:, :, DH:DH + 1].rearrange("p h o -> p (h o)")).then_inc(inverted, 1)
                        if oproj and (not known(i) or k >= 1):
                            dve.wait_ge(oT_done, k)
                        dve.wait_ge(inverted, k + 1)
                        nc.vector.tensor_tensor(o_n[:, :].rearrange("p (h d) -> p h d", h=H), ps_v[:, :, 0:DH],
                                                rec[:, :].unsqueeze(2).to_broadcast([P, H, DH]), ALU.mult).then_inc(normed, 1)
                        if not oproj:
                            dve.wait_ge(normed, k + 1)
                            nc.vector.scalar_tensor_tensor(row(X, k), o_n[:, :], col(qm, k), row(X, k), ALU.mult, ALU.add)\
                              .then_inc(resid_done, 1)

                def k_of(i, d):
                    return i + d
                body(dve, run)

            @block.scalar
            def _(act):
                def run(i, u, queries, scores, values, output):
                    if queries:
                        k = i + 2
                        act.wait_ge(x_done, k + 1)
                        if proj:
                            if not known(i) or k >= 2:
                                act.wait_ge(q_done, k - 1)
                            nc.scalar.activation(xT[:, u, :, :], ps_q[:, 0:D].rearrange("p (k s) -> p k s", k=KD), ACT.Copy)\
                              .then_inc(x_copied, 1)
                        else:
                            if not known(i) or k >= 2:
                                act.wait_ge(s_done, T4 * (k - 1))
                            nc.scalar.activation(qT[:, u, :, :], ps_q.rearrange("p (t s) -> p t s", t=T4), ACT.Copy)\
                              .then_inc(q_ready, 1)
                    if output and oproj:
                        k = i - 1
                        act.wait_ge(oT_done, k + 1)
                        if not known(i) or k >= 1:
                            act.wait_ge(o_done, k)
                        nc.scalar.activation(oT[:, :, :], ps_t[0][:, 0:D].rearrange("p (k s) -> p k s", k=KD), ACT.Copy)\
                          .then_inc(oT_copied, 1)

                    def copy_pT(c):
                        n = T4 * i + c
                        act.wait_ge(pT_done, n + 1)
                        if not known(i) or n >= 2:
                            act.wait_ge(av_done, n - 1)
                        nc.scalar.activation(pT[:, c % 2, :, :], ps_t[c % 2].rearrange("p (t s) -> p t s", t=T4), ACT.Copy)\
                          .then_inc(pT_copied, 1)
                    if values:
                        copy_pT(0)
                        copy_pT(1)
                    if queries and proj:
                        k = i + 2
                        act.wait_ge(k_done, k + 1)
                        if not known(i) or k >= 2:
                            act.wait_ge(s_done, T4 * (k - 1))
                        for t in range(T4):
                            last = nc.scalar.activation(kT[:, u, t, :], ps_q[:, t * P:(t + 1) * P], ACT.Identity, bias=bk_sb[:, t:t + 1])
                        last.then_inc(k_ready, 1)
                    if values:
                        copy_pT(2)
                        copy_pT(3)
                    if scores:
                        k = i + 1
                        for c in range(T4):
                            act.wait_ge(shifted, T4 * k + c + 1)
                            if not known(i) or k >= 1:
                                act.wait_ge(pT_done, T4 * (k - 1) + c + 1)
                            nc.scalar.activation(p_sb[:, c, :], t_sb[:, c, :], ACT.Exp).then_inc(exped, 1)
                body(act, run)

            @block.tensor
            def _(pe):
                def project(w, src, u, done):
                    for t in range(T4):
                        for d in range(KD):
                            last = nc.tensor.matmul(ps_q[:, t * P:(t + 1) * P], w[:, d, T4 * t:T4 * t + T4, :].rearrange("p h e -> p (h e)"),
                                                    src[:, u, d, :], start=(d == 0), stop=(d == KD - 1))
                    last.then_inc(done, 1)

                def run(i, u, queries, scores, values, output):
                    if queries:
                        k = i + 2
                        pe.wait_ge(xn_ready, k + 1)
                        if not known(i) or k >= 1:
                            if not proj:
                                pe.wait_ge(q_ready, k)
                            elif not known(i) or k >= 2:
                                pe.wait_ge(v_ready, k - 1)
                            else:
                                pe.wait_ge(k_ready, 1)
                        for t in range(XN // P):
                            last = nc.tensor.transpose(ps_q[:, t * P:(t + 1) * P], xn[:, u, t * P:(t + 1) * P], ident[:, :])
                        last.then_inc(x_done, 1)
                    if output and oproj:
                        k = i - 1
                        pe.wait_ge(normed, k + 1)
                        pe.wait_ge(pT_copied, T4 * k + 3)
                        for d in range(KD):
                            last = nc.tensor.transpose(ps_t[0][:, d * P:(d + 1) * P], o_n[:, d * P:(d + 1) * P], ident[:, :])
                        last.then_inc(oT_done, 1)
                    if scores:
                        k, w = i + 1, 1 - u
                        pe.wait_ge(q_ready, k + 1)
                        if proj:
                            pe.wait_ge(k_ready, k + 1)
                        elif known(i):
                            pe.wait_ge(ctx_in[w], 16 * DMAS * ((k - w) // 2 + 1))
                        else:
                            pe.wait_ge(ctx_in[w], 8 * DMAS * (k - w) + 16 * DMAS)
                        for t in range(T4):
                            for j in range(T4):
                                if t == 0 and (not known(i) or k >= 1):
                                    pe.wait_ge(biased, T4 * (k - 1) + j + 1)
                                at = slice(j * HB, j * HB + DH)
                                last = nc.tensor.matmul(ps_s[:, j, t * P:(t + 1) * P], qT[at, w, t, :], kT[at, w, t, :], start=True, stop=True)
                                if t == T4 - 1:
                                    last.then_inc(s_done, 1)
                    if output and oproj:
                        k = i - 1
                        pe.wait_ge(oT_copied, k + 1)
                        pe.wait_ge(pT_copied, T4 * k + 4)
                        for d in range(KD):
                            last = nc.tensor.matmul(ps_t[1][:, 0:D], oT[:, d, :], wo_sb[:, d, :], start=(d == 0), stop=(d == KD - 1))
                        last.then_inc(o_done, 1)
                    if queries and proj:
                        pe.wait_ge(x_copied, i + 3)
                        project(wq_sb, xT, u, q_done)

                    def transpose_p(c):
                        n = T4 * i + c
                        pe.wait_ge(exped, n + 1)
                        if c >= 2:
                            pe.wait_ge(pT_copied, n - 1)
                        elif not known(i) or i >= 1:
                            if not oproj:
                                pe.wait_ge(pT_copied, n - 1)
                            else:
                                pe.wait_ge(oT_copied if c == 0 else resid_done, i)
                        for t in range(T4):
                            last = nc.tensor.transpose(ps_t[c % 2][:, t * P:(t + 1) * P], p_sb[:, c, t * P:(t + 1) * P], ident[:, :])
                        last.then_inc(pT_done, 1)

                    def apply_v(c):
                        pe.wait_ge(pT_copied, T4 * i + c + 1)
                        if c == 0:
                            pe.wait_ge(v_ready, i + 1)
                            if not known(i) or i >= 1:
                                pe.wait_ge(normed, i)
                        for t in range(T4):
                            h = T4 * t + c
                            last = nc.tensor.matmul(ps_v[:, h, :], pT[:, c % 2, t, :], vx[:, u, h, :], start=True, stop=True)
                        last.then_inc(av_done, 1)
                    if values:
                        transpose_p(0)
                        transpose_p(1)
                    if queries and proj:
                        pe.wait_ge(q_ready, i + 3)
                        if known(i):
                            pe.wait_ge(ctx_in[u], 16 * DMAS * ((i + 2 - u) // 2 + 1))
                        else:
                            pe.wait_ge(ctx_in[u], 8 * DMAS * (i + 2 - u) + 16 * DMAS)
                        project(wk_sb, cT, u, k_done)
                    if values:
                        apply_v(0)
                        transpose_p(2)
                        apply_v(1)
                        transpose_p(3)
                    if scores and proj:
                        k, w = i + 1, 1 - u
                        pe.wait_ge(k_ready, k + 2 if queries else B)
                        for d in range(KD):
                            last = nc.tensor.matmul(ps_q[:, 0:D], cT[:, w, d, :], wv_sb[:, d, :], start=(d == 0), stop=(d == KD - 1))
                        last.then_inc(v_done, 1)
                    if values:
                        apply_v(2)
                        apply_v(3)
                body(pe, run)


def store(nc, X, out):
    with ExitStack() as stack:
        stored = stack.enter_context(nc.semaphore("stored"))
        with nc.Block() as block:

            @block.sync
            def _(sp):
                sp.dma_start(out.rearrange("b p d -> p b d"), X[:, :, :]).then_inc(stored, 16)
                sp.wait_ge(stored, 16)


def norm_and_product(nc, layer, X, ident, mean, rstd, small, logits, XT=None, base=None, small_bias=None, base_bias=None):
    N = small.shape[2]
    with ExitStack() as stack:
        m = Pool(nc, stack, layer + "_np")
        xn, xs = m.sb("xn", [P, 2, D]), m.sb("xs", [P, 2, KD, P])
        PS = stack.enter_context(nc.psum_tensor(f"{layer}_np_ps", [P, 8, 512], F32))
        xn_ready, x_done, x_copied, kept = m.sem("xn_ready"), m.sem("x_done"), m.sem("x_copied"), m.sem("kept")
        l_done, l_read, b_done, b_added, bias_added = (m.sem(n) for n in ("l_done", "l_read", "b_done", "b_added", "bias_added"))

        def body(engine, run):
            run(-1, 1, True, False)
            run(0, 0, True, True)
            run(1, 1, True, True)
            with engine.Fori(1, B // 2 - 1) as j:
                run(2 * j, 0, True, True)
                run(2 * j + 1, 1, True, True)
            run(B - 2, 0, True, True)
            run(B - 1, 1, False, True)

        def known(i):
            return isinstance(i, int)

        with nc.Block() as block:

            @block.vector
            def _(dve):
                def run(i, u, ahead, now):
                    if ahead:
                        k = i + 1
                        if not known(i) or k >= 2:
                            dve.wait_ge(x_done, k - 1)
                        nc.vector.tensor_scalar(xn[:, 1 - u, :], row(X, k), col(mean, k), col(rstd, k), ALU.subtract, ALU.mult)\
                          .then_inc(xn_ready, 1)
                    if now:
                        if XT is not None:
                            dve.wait_ge(x_copied, i + 1)
                            nc.vector.tensor_copy(XT[:, :, one(i), :].rearrange("p k o s -> p k (o s)"), xs[:, u, :, :]).then_inc(kept, 1)
                        dve.wait_ge(l_done, i + 1)
                        if small_bias is None:
                            nc.vector.tensor_copy(row(logits, i), PS[:, 2 + u, 0:N]).then_inc(l_read, 1)
                        else:
                            nc.vector.tensor_tensor(row(logits, i), PS[:, 2 + u, 0:N], small_bias[:, :], ALU.add).then_inc(l_read, 1)
                        if base is not None:
                            dve.wait_ge(b_done, i + 1)
                            dve.wait_ge(bias_added, i + 1)
                            nc.vector.tensor_tensor(row(X, i), row(X, i), PS[:, 4 + u, 0:D], ALU.add).then_inc(b_added, 1)
                body(dve, run)

            @block.gpsimd
            def _(pool):
                if base is not None:
                    def run(i, u, ahead, now):
                        if ahead:
                            pool.wait_ge(xn_ready, i + 2)
                            nc.gpsimd.tensor_tensor(row(X, i + 1), row(X, i + 1), base_bias[:, :], ALU.add).then_inc(bias_added, 1)
                    body(pool, run)

            @block.scalar
            def _(act):
                def run(i, u, ahead, now):
                    if ahead:
                        k, w = i + 1, 1 - u
                        act.wait_ge(x_done, k + 1)
                        if not known(i) or k >= 2:
                            act.wait_ge(l_done, k - 1)
                            if base is not None:
                                act.wait_ge(b_done, k - 1)
                            if XT is not None:
                                act.wait_ge(kept, k - 1)
                        nc.scalar.activation(xs[:, w, :, :], PS[:, w, 0:D].rearrange("p (k s) -> p k s", k=KD), ACT.Copy)\
                          .then_inc(x_copied, 1)
                body(act, run)

            @block.tensor
            def _(pe):
                def run(i, u, ahead, now):
                    if ahead:
                        k, w = i + 1, 1 - u
                        pe.wait_ge(xn_ready, k + 1)
                        if not known(i) or k >= 2:
                            pe.wait_ge(x_copied, k - 1)
                        for d in range(KD):
                            last = nc.tensor.transpose(PS[:, w, d * P:(d + 1) * P], xn[:, w, d * P:(d + 1) * P], ident[:, :])
                        last.then_inc(x_done, 1)
                    if now:
                        pe.wait_ge(x_copied, i + 1)
                        if not known(i) or i >= 2:
                            pe.wait_ge(l_read, i - 1)
                        for d in range(KD):
                            last = nc.tensor.matmul(PS[:, 2 + u, 0:N], xs[:, u, d, :], small[:, d, :], start=(d == 0), stop=(d == KD - 1))
                        last.then_inc(l_done, 1)
                        if base is not None:
                            if not known(i) or i >= 2:
                                pe.wait_ge(b_added, i - 1)
                            for d in range(KD):
                                last = nc.tensor.matmul(PS[:, 4 + u, 0:D], xs[:, u, d, :], base[:, d, :], start=(d == 0), stop=(d == KD - 1))
                            last.then_inc(b_done, 1)
                body(pe, run)


def add_product(nc, layer, X, ident, coef, rows, K):
    with ExitStack() as stack:
        m = Pool(nc, stack, layer + "_ap")
        cs, cT = m.sb("cs", [P, 2, P]), m.sb("cT", [K, 2, P])
        cleared = m.sem("cleared")
        PS = stack.enter_context(nc.psum_tensor(f"{layer}_ap_ps", [P, 8, 512], F32))
        staged, t_done, t_copied, r_done, added = (m.sem(n) for n in ("staged", "t_done", "t_copied", "r_done", "added"))

        def body(engine, run):
            run(-1, 1, True, False)
            run(0, 0, True, True)
            run(1, 1, True, True)
            with engine.Fori(1, B // 2 - 1) as j:
                run(2 * j, 0, True, True)
                run(2 * j + 1, 1, True, True)
            run(B - 2, 0, True, True)
            run(B - 1, 1, False, True)

        def known(i):
            return isinstance(i, int)

        with nc.Block() as block:

            @block.gpsimd
            def _(pool):
                nc.gpsimd.memset(cs[:, :, :], 0.0).then_inc(cleared, 1)

            @block.vector
            def _(dve):
                dve.wait_ge(cleared, 1)

                def run(i, u, ahead, now):
                    if ahead:
                        k = i + 1
                        if not known(i) or k >= 2:
                            dve.wait_ge(t_done, k - 1)
                        nc.vector.tensor_copy(cs[:, 1 - u, 0:K], coef[:, one(k), 0:K].rearrange("p o k -> p (o k)")).then_inc(staged, 1)
                    if now:
                        dve.wait_ge(r_done, i + 1)
                        nc.vector.tensor_tensor(row(X, i), row(X, i), PS[:, 2 + u, 0:D], ALU.add).then_inc(added, 1)
                body(dve, run)

            @block.scalar
            def _(act):
                def run(i, u, ahead, now):
                    if ahead:
                        k, w = i + 1, 1 - u
                        act.wait_ge(t_done, k + 1)
                        if not known(i) or k >= 2:
                            act.wait_ge(r_done, k - 1)
                        nc.scalar.activation(cT[:, w, :], PS[0:K, w, 0:P], ACT.Copy).then_inc(t_copied, 1)
                body(act, run)

            @block.tensor
            def _(pe):
                def run(i, u, ahead, now):
                    if ahead:
                        k, w = i + 1, 1 - u
                        pe.wait_ge(staged, k + 1)
                        if not known(i) or k >= 2:
                            pe.wait_ge(t_copied, k - 1)
                        nc.tensor.transpose(PS[:, w, 0:P], cs[:, w, :], ident[:, :]).then_inc(t_done, 1)
                    if now:
                        pe.wait_ge(t_copied, i + 1)
                        if not known(i) or i >= 2:
                            pe.wait_ge(added, i - 1)
                        nc.tensor.matmul(PS[:, 2 + u, 0:D], cT[:, u, :], rows[0:K, :], start=True, stop=True).then_inc(r_done, 1)
                body(pe, run)


def spread(t, n):
    return t.unsqueeze(2).to_broadcast([P, B, n])


def select_top(nc, c, combine, numbers, hit, index, values, count, E):
    for j in range(count):
        c.do(nc.vector.tensor_tensor(hit, numbers, spread(index[:, :, j], E), ALU.is_equal))
        if values is not None:
            c.do(nc.vector.tensor_tensor(hit, hit, spread(values[:, :, j], E), ALU.mult))
        if j == 0:
            c.do(nc.vector.tensor_copy(combine, hit))
        else:
            c.do(nc.vector.tensor_tensor(combine, combine, hit, ALU.add))


def top_picks(nc, c, values8, index8, index_f, source):
    for b in range(B):
        last = nc.vector.max(values8[:, b, :], source[:, b, :])
        if b == B - 1:
            c.do(last)
        else:
            last.then_inc(c.sem, 1)
            c.n += 1
    for b in range(B):
        last = nc.vector.max_index(index8[:, b, :], values8[:, b, :], source[:, b, :])
        if b == B - 1:
            c.do(last)
        else:
            last.then_inc(c.sem, 1)
            c.n += 1
    c.do(nc.vector.tensor_copy(index_f[:, :, :], index8[:, :, :]))


def route_top2(nc, layer, logits, combine, E):
    with ExitStack() as stack:
        m = Pool(nc, stack, layer + "_route")
        n_i, n_f = m.sb("n_i", [P, B, E], I32), m.sb("n_f", [P, B, E])
        v8, i8, i8f, hit = m.sb("v8", [P, B, 8]), m.sb("i8", [P, B, 8], U32), m.sb("i8f", [P, B, 8]), m.sb("hit", [P, B, E])
        gap, e, p = m.sb("gap", [P, B]), m.sb("e", [P, B]), m.sb("p", [P, B, 2])
        numbered, chain, gap_ready, e_ready = (m.sem(n) for n in ("numbered", "chain", "gap_ready", "e_ready"))
        with nc.Block() as block:

            @block.gpsimd
            def _(pool):
                nc.gpsimd.iota(n_i[:, :, :], pattern=[[0, B], [1, E]], base=0, channel_multiplier=0).then_inc(numbered, 1)

            @block.scalar
            def _(act):
                act.wait_ge(gap_ready, 1)
                nc.scalar.activation(e[:, :], gap[:, :], ACT.Exp).then_inc(e_ready, 1)

            @block.vector
            def _(dve):
                c = Chain(dve, chain)
                dve.wait_ge(numbered, 1)
                c.do(nc.vector.tensor_copy(n_f[:, :, :], n_i[:, :, :]))
                top_picks(nc, c, v8, i8, i8f, logits)
                nc.vector.tensor_tensor(gap[:, :], v8[:, :, 1], v8[:, :, 0], ALU.subtract).then_inc(gap_ready, 1)
                dve.wait_ge(e_ready, 1)
                c.do(nc.vector.tensor_scalar(gap[:, :], e[:, :], 1.0, None, ALU.add))
                c.do(nc.vector.reciprocal(p[:, :, 0], gap[:, :]))
                c.do(nc.vector.tensor_tensor(p[:, :, 1], p[:, :, 0], e[:, :], ALU.mult))
                select_top(nc, c, combine[:, :, 0:E], n_f[:, :, :], hit[:, :, :], i8f, p, 2, E)


def softmax_rows(nc, c, dve, act_ready, e_ready, scores, top, N):
    c.do(nc.vector.tensor_reduce(top, scores, AXIS.X, ALU.max))
    nc.vector.tensor_tensor(scores, scores, spread(top, N), ALU.subtract).then_inc(act_ready, 1)
    dve.wait_ge(e_ready, 1)
    c.do(nc.vector.tensor_reduce(top, scores, AXIS.X, ALU.add))
    c.do(nc.vector.reciprocal(top, top))
    c.do(nc.vector.tensor_tensor(scores, scores, spread(top, N), ALU.mult))


def route_grouped(nc, layer, logits, combine, E, GROUPS, TOP_GROUPS, TOP):
    G = E // GROUPS
    assert G == 4 and GROUPS == 8
    with ExitStack() as stack:
        m = Pool(nc, stack, layer + "_route")
        n_i, n_f = m.sb("n_i", [P, B, E], I32), m.sb("n_f", [P, B, E])
        v8, i8, i8f, hit = m.sb("v8", [P, B, 8]), m.sb("i8", [P, B, 8], U32), m.sb("i8f", [P, B, 8]), m.sb("hit", [P, B, E])
        top, masked = m.sb("top", [P, B]), m.sb("masked", [P, B, E])
        hi, lo = m.sb("hi", [P, 2, B, GROUPS]), m.sb("lo", [P, 2, B, GROUPS])
        gs, keep = m.sb("gs", [P, B, GROUPS]), m.sb("keep", [P, B, GROUPS])
        numbered, chain, act_ready, e_ready = (m.sem(n) for n in ("numbered", "chain", "act_ready", "e_ready"))
        with nc.Block() as block:

            @block.gpsimd
            def _(pool):
                nc.gpsimd.iota(n_i[:, :, :], pattern=[[0, B], [1, E]], base=0, channel_multiplier=0).then_inc(numbered, 1)
                pool.wait_ge(numbered, 1)
                nc.gpsimd.memset(combine[:, :, E:], 1.0).then_inc(numbered, 1)

            @block.scalar
            def _(act):
                act.wait_ge(act_ready, 1)
                nc.scalar.activation(logits[:, :, :], logits[:, :, :], ACT.Exp).then_inc(e_ready, 1)

            @block.vector
            def _(dve):
                c = Chain(dve, chain)
                dve.wait_ge(numbered, 2)
                c.do(nc.vector.tensor_copy(n_f[:, :, :], n_i[:, :, :]))
                softmax_rows(nc, c, dve, act_ready, e_ready, logits[:, :, :], top[:, :], E)
                s = logits[:, :, :].rearrange("p b (g m) -> p b g m", m=G)
                for k in range(2):
                    c.do(nc.vector.tensor_tensor(hi[:, k], s[:, :, :, 2 * k], s[:, :, :, 2 * k + 1], ALU.max))
                    c.do(nc.vector.tensor_tensor(lo[:, k], s[:, :, :, 2 * k], s[:, :, :, 2 * k + 1], ALU.min))
                c.do(nc.vector.tensor_tensor(gs[:, :, :], hi[:, 0], hi[:, 1], ALU.max))
                c.do(nc.vector.tensor_tensor(keep[:, :, :], hi[:, 0], hi[:, 1], ALU.min))
                c.do(nc.vector.tensor_tensor(hi[:, 0], lo[:, 0], lo[:, 1], ALU.max))
                c.do(nc.vector.tensor_tensor(hi[:, 1], hi[:, 0], keep[:, :, :], ALU.max))
                c.do(nc.vector.tensor_tensor(gs[:, :, :], gs[:, :, :], hi[:, 1], ALU.add))
                top_picks(nc, c, v8, i8, i8f, gs)
                select_top(nc, c, keep[:, :, :], n_f[:, :, 0:GROUPS], hit[:, :, 0:GROUPS], i8f, None, TOP_GROUPS, GROUPS)
                m4 = masked[:, :, :].rearrange("p b (g m) -> p b g m", m=G)
                c.do(nc.vector.tensor_scalar(gs[:, :, :], keep[:, :, :], 1.0, -MASKED, ALU.subtract, ALU.mult))
                c.do(nc.vector.tensor_tensor(m4, s, keep[:, :, :].unsqueeze(3).to_broadcast([P, B, GROUPS, G]), ALU.mult))
                c.do(nc.vector.tensor_tensor(m4, m4, gs[:, :, :].unsqueeze(3).to_broadcast([P, B, GROUPS, G]), ALU.add))
                top_picks(nc, c, v8, i8, i8f, masked)
                select_top(nc, c, combine[:, :, 0:E], n_f[:, :, :], hit[:, :, :], i8f, v8, TOP, E)


def experts(nc, layer, X, XT, combine, blob, E, F, gated):
    FT = F // P
    HID = FT * (2 if gated else 1)
    NT = 512
    UNITS = B * P // NT
    SUB = NT // P
    W1, BI = KD * F * (2 if gated else 1), HID
    with ExitStack() as stack:
        m = Pool(nc, stack, layer + "_ex")
        wb = m.sb("w", [P, 2, blob.shape[2]])
        h = m.sb("h", [P, 2, FT, NT])
        sg = m.sb("sg", [P, 2, NT]) if gated else None
        PS = stack.enter_context(nc.psum_tensor(f"{layer}_ex_ps", [P, 8, 512], F32))
        w_in = [m.sem("w_in0"), m.sem("w_in1")]
        h_done, act_done, h_ready, y_done, added = (m.sem(n) for n in ("h_done", "act_done", "h_ready", "y_done", "added"))

        def hidden_bank(n, f):
            return HID * (n % 2) + f if gated else f

        def w1(u, f, d):
            return wb[:, u, (f * KD + d) * P:(f * KD + d + 1) * P]

        def bias(u, f):
            return wb[:, u, W1 + f:W1 + f + 1]

        def w2(u, f):
            return wb[:, u, W1 + BI + f * D:W1 + BI + (f + 1) * D]

        def xt(d, n):
            return XT[:, d, SUB * n:SUB * (n + 1), :].rearrange("p b s -> p (b s)")

        def body(engine, run):
            run(0, 0, True, False)
            run(1, 1, False, False)
            with engine.Fori(1, E // 2 - 1) as j:
                run(2 * j, 0, False, False)
                run(2 * j + 1, 1, False, False)
            run(E - 2, 0, False, False)
            run(E - 1, 1, False, True)

        def known(e):
            return isinstance(e, int)

        def loads_seen(e, u):
            return 8 * (e - u) + 16

        with nc.Block() as block:

            @block.sync
            def _(sp):
                def run(e, u, first, last):
                    if not known(e) or e >= 2:
                        sp.wait_ge(y_done, 2 * UNITS * (e - 1))
                    sp.dma_start(wb[:, u, :], blob[one(e), :, :].rearrange("o p n -> (o p) n")).then_inc(w_in[u], 16)
                body(sp, run)

            @block.tensor
            def _(pe):
                def hidden(e, u, n):
                    g = UNITS * e + n
                    if n == 0:
                        pe.wait_ge(w_in[u], loads_seen(e, u))
                    for f in range(HID):
                        if gated:
                            if not known(e) or g >= 2:
                                pe.wait_ge(act_done if f < FT else h_ready, g - 1)
                        elif not known(e) or g >= 1:
                            pe.wait_ge(h_ready, FT * (g - 1) + f + 1)
                        for d in range(KD):
                            last = nc.tensor.matmul(PS[:, hidden_bank(n, f), :], w1(u, f, d), xt(d, n), start=(d == 0), stop=(d == KD - 1))
                        last.then_inc(h_done, 1)

                def outputs(e, u, n):
                    g = UNITS * e + n
                    pe.wait_ge(h_ready, FT * (g + 1))
                    for s in range(SUB):
                        if s % 2 == 0 and (not known(e) or g >= 2):
                            pe.wait_ge(added, 2 * (g - 2) + s // 2 + 1)
                        for f in range(FT):
                            last = nc.tensor.matmul(PS[:, 4 + 2 * (n % 2) + s // 2, (s % 2) * D:(s % 2 + 1) * D],
                                                    h[:, n % 2, f, s * P:(s + 1) * P], w2(u, f), start=(f == 0), stop=(f == FT - 1))
                        if s % 2:
                            last.then_inc(y_done, 1)

                def run(e, u, first, last):
                    if first:
                        hidden(e, u, 0)
                    for n in range(UNITS):
                        if n < UNITS - 1:
                            hidden(e, u, n + 1)
                        elif not last:
                            hidden(e + 1, 1 - u, 0)
                        outputs(e, u, n)
                body(pe, run)

            @block.scalar
            def _(act):
                def run(e, u, first, last):
                    for n in range(UNITS):
                        g = UNITS * e + n
                        for f in range(FT):
                            act.wait_ge(h_done, HID * g + f + 1)
                            if gated:
                                if not known(e) or g >= 2:
                                    act.wait_ge(h_ready, g - 1)
                                nc.scalar.activation(sg[:, n % 2, :], PS[:, hidden_bank(n, f), :], ACT.Silu, bias=bias(u, f))\
                                  .then_inc(act_done, 1)
                            else:
                                if f == 0 and (not known(e) or g >= 2):
                                    act.wait_ge(y_done, 2 * (g - 1))
                                nc.scalar.activation(h[:, n % 2, f, :], PS[:, hidden_bank(n, f), :], ACT.Gelu, bias=bias(u, f))\
                                  .then_inc(h_ready, 1)
                body(act, run)

            @block.vector
            def _(dve):
                def gate(e, u, n):
                    g = UNITS * e + n
                    dve.wait_ge(h_done, HID * (g + 1))
                    dve.wait_ge(act_done, g + 1)
                    if not known(e) or g >= 2:
                        dve.wait_ge(y_done, 2 * (g - 1))
                    nc.vector.scalar_tensor_tensor(h[:, n % 2, 0, :], PS[:, hidden_bank(n, 1), :], bias(u, 1), sg[:, n % 2, :],
                                                   ALU.add, ALU.mult).then_inc(h_ready, 1)

                def run(e, u, first, last):
                    if gated and first:
                        gate(e, u, 0)
                    for n in range(UNITS):
                        g = UNITS * e + n
                        if gated:
                            if n < UNITS - 1:
                                gate(e, u, n + 1)
                            elif not last:
                                gate(e + 1, 1 - u, 0)
                        for s in range(SUB):
                            b = SUB * n + s
                            if s % 2 == 0:
                                dve.wait_ge(y_done, 2 * g + s // 2 + 1)
                            acc = nc.vector.scalar_tensor_tensor(
                                X[:, b, :], PS[:, 4 + 2 * (n % 2) + s // 2, (s % 2) * D:(s % 2 + 1) * D],
                                combine[:, b, one(e)], X[:, b, :], ALU.mult, ALU.add)
                            if s % 2:
                                acc.then_inc(added, 1)
                body(dve, run)


def mixture(nc, layer, X, ident, router, router_bias, b2, blob, E, F, gated):
    shared = 2 if gated else 0
    with ExitStack() as stack:
        m = Pool(nc, stack, layer)
        mean, rstd = m.sb("mean", [P, B]), m.sb("rstd", [P, B])
        XT = m.sb("XT", [P, KD, B, P])
        logits, combine = m.sb("logits", [P, B, E]), m.sb("combine", [P, B, E + shared])
        rw = m.sb("rw", [P, KD, E])
        rows = b2.shape[0]
        b2_sb = m.sb("b2", [rows, D])
        loads = [(rw[:, :, :], router.rearrange("(k p) e -> p k e", p=P)), (b2_sb[:, :], b2)]
        rb = None
        if router_bias is not None:
            rb = m.sb("rb", [P, E])
            loads.append((rb[:, :], router_bias.partition_broadcast(P)))
        norm_statistics(nc, layer, X, mean, rstd, 1.0, loads)
        norm_and_product(nc, layer, X, ident, mean, rstd, rw, logits, XT=XT, small_bias=rb)
        if gated:
            route_grouped(nc, layer, logits, combine, E, 8, 4, 4)
        else:
            route_top2(nc, layer, logits, combine, E)
        add_product(nc, layer, X, ident, combine, b2_sb, rows)
        experts(nc, layer, X, XT, combine, blob, E + shared, F, gated)


def lora(nc, layer, X, ident, small, small_bias, base, base_bias, loraB, E, R, scaling):
    with ExitStack() as stack:
        m = Pool(nc, stack, layer)
        mean, rstd = m.sb("mean", [P, B]), m.sb("rstd", [P, B])
        sm, bs = m.sb("small", [P, KD, E + R]), m.sb("base", [P, KD, D])
        smb, bsb, lb = m.sb("small_bias", [P, E + R]), m.sb("base_bias", [P, D]), m.sb("loraB", [E * R, D])
        both, gate, gate16 = m.sb("both", [P, B, E + R]), m.sb("gate", [P, B, E]), m.sb("gate16", [P, B, E], BF16)
        top, outer = m.sb("top", [P, B]), m.sb("outer", [P, B, E * R])
        loads = [(sm[:, :, 0:E], small[0].rearrange("(k p) e -> p k e", p=P)),
                 (sm[:, :, E:], small[1].rearrange("(k p) e -> p k e", p=P)),
                 (smb[:, 0:E], small_bias.partition_broadcast(P)),
                 (bs[:, :, :], base.rearrange("(k p) e -> p k e", p=P)),
                 (bsb[:, :], base_bias.partition_broadcast(P)),
                 (lb[:, :], loraB.rearrange("e r n -> (e r) n"))]
        norm_statistics(nc, layer, X, mean, rstd, 1.0, loads, zeros=[smb[:, :]])
        norm_and_product(nc, layer, X, ident, mean, rstd, sm, both, base=bs, small_bias=smb, base_bias=bsb)
        chain, act_ready, e_ready = m.sem("chain"), m.sem("act_ready"), m.sem("e_ready")
        with nc.Block() as block:

            @block.scalar
            def _(act):
                act.wait_ge(act_ready, 1)
                nc.scalar.activation(gate[:, :, :], gate[:, :, :], ACT.Exp).then_inc(e_ready, 1)

            @block.vector
            def _(dve):
                c = Chain(dve, chain)
                c.do(nc.vector.tensor_copy(gate[:, :, :], both[:, :, 0:E]))
                softmax_rows(nc, c, dve, act_ready, e_ready, gate[:, :, :], top[:, :], E)
                c.do(nc.vector.tensor_copy(gate16[:, :, :], gate[:, :, :]))
                c.do(nc.vector.tensor_scalar(gate[:, :, :], gate16[:, :, :], float(scaling), None, ALU.mult))
                for r in range(R):
                    c.do(nc.vector.tensor_tensor(outer[:, :, :].rearrange("p b (e r) -> p b e r", r=R)[:, :, :, r],
                                                 gate[:, :, :], spread(both[:, :, E + r], E), ALU.mult))
        add_product(nc, layer, X, ident, outer, lb, E * R)


MAGIC = 1.5 * 2.0 ** 23
QMAX = 32767.0
WBLOCK, WQMAX = 32, 7.0
SIG = 65536.0


def quantized_ffn(nc, layer, X, ident, w_gate, w_up, w_down, F):
    FT = F // P
    NT = 512
    NN = B * P // NT
    CH = 1024
    NC = FT * B * P // CH
    with ExitStack() as stack:
        m = Pool(nc, stack, layer)
        mean, rstd = m.sb("mean", [P, B]), m.sb("rstd", [P, B])
        G, U = m.sb("G", [P, FT, B * P]), m.sb("U", [P, FT, B * P])
        XQ = m.sb("XQ", [P, KD, B, P])
        wT = [m.sb(f"wT{k}", [P, KD * F]) for k in range(3)]
        big, step, inv = m.sb("big", [P, 5]), m.sb("step", [P, 5]), m.sb("inv", [P, 5])
        part = m.sb("part", [P, 5])
        magic = m.sb("magic", [P, 1])
        found, reduced, scaled, chain = m.sem("found"), m.sem("reduced"), m.sem("scaled"), m.sem("chain")
        RMAX = bass.bass_isa.ReduceOp.absmax

        def all_tokens(pool, k):
            pool.wait_ge(found, k + 1)
            nc.gpsimd.partition_all_reduce(big[:, k:k + 1], part[:, k:k + 1], P, RMAX).then_inc(reduced, 1)

        def steps(dve, c, k, factor):
            dve.wait_ge(reduced, k + 1)
            c.do(nc.vector.tensor_scalar(step[:, k:k + 1], big[:, k:k + 1], factor / QMAX, 1e-12, ALU.mult, ALU.max))
            c.do(nc.vector.reciprocal(inv[:, k:k + 1], step[:, k:k + 1]))
            c.do(nc.vector.tensor_scalar(inv[:, k:k + 1], inv[:, k:k + 1], factor, None, ALU.mult))

        with ExitStack() as early:
            me = Pool(nc, early, layer)
            wn = [me.sb(f"wn{k}", [P, KD * F]) for k in range(3)]
            wa, wi = me.sb("wa", [P, KD * F // WBLOCK]), me.sb("wi", [P, KD * F // WBLOCK])
            XN = me.sb("XN", [P, B, D])
            xq = me.sb("xq", [P, 2, D])
            loads = [(wn[0][:, :].rearrange("p (t n) -> p t n", t=FT), w_gate.rearrange("(t p) n -> p t n", p=P)),
                     (wn[1][:, :].rearrange("p (t n) -> p t n", t=FT), w_up.rearrange("(t p) n -> p t n", p=P)),
                     (wn[2][:, :].rearrange("p (t n) -> p t n", t=KD), w_down.rearrange("(t p) n -> p t n", p=P))]
            norm_statistics(nc, layer, X, mean, rstd, 1.0, loads)

            PS = early.enter_context(nc.psum_tensor(f"{layer}_q_ps", [P, 8, 512], F32))
            normed, w_ready, wt_done, wt_copied = me.sem("normed"), me.sem("w_ready"), me.sem("wt_done"), me.sem("wt_copied")
            rounded, x_done, x_copied = me.sem("rounded"), me.sem("x_done"), me.sem("x_copied")
            with nc.Block() as block:

                @block.gpsimd
                def _(pool):
                    nc.gpsimd.memset(magic[:, :], MAGIC)
                    all_tokens(pool, 0)

                @block.vector
                def _(dve):
                    c = Chain(dve, chain)
                    with dve.Fori(0, B) as b:
                        nc.vector.tensor_scalar(row(XN, b), row(X, b), col(mean, b), col(rstd, b), ALU.subtract, ALU.mult)\
                          .then_inc(normed, 1)
                    dve.wait_ge(normed, B)
                    nc.vector.tensor_reduce(part[:, 0:1], XN[:, :, :].rearrange("p b d -> p (b d)"), AXIS.X, ALU.max,
                                            apply_absolute_value=True).then_inc(found, 1)
                    for k in range(3):
                        w = wn[k][:, :].rearrange("p (a n) -> p a n", n=WBLOCK)
                        NB = KD * F // WBLOCK
                        if k:
                            dve.wait_ge(w_ready, k)
                        c.do(nc.vector.tensor_reduce(wa[:, :], w, AXIS.X, ALU.max, apply_absolute_value=True))
                        c.do(nc.vector.tensor_scalar(wa[:, :], wa[:, :], 1.0 / WQMAX, 1e-12, ALU.mult, ALU.max))
                        c.do(nc.vector.reciprocal(wi[:, :], wa[:, :]))
                        c.do(nc.vector.tensor_tensor(w, w, wi[:, :].unsqueeze(2).to_broadcast([P, NB, WBLOCK]), ALU.mult))
                        c.do(nc.vector.tensor_scalar(w, w, MAGIC, MAGIC, ALU.add, ALU.subtract))
                        c.do(nc.vector.tensor_scalar(w, w, -WQMAX - 1.0, WQMAX, ALU.max, ALU.min))
                        nc.vector.tensor_tensor(w, w, wa[:, :].unsqueeze(2).to_broadcast([P, NB, WBLOCK]), ALU.mult).then_inc(w_ready, 1)
                    steps(dve, c, 0, 1.0)

                @block.tensor
                def _(pe):
                    for k in range(3):
                        pe.wait_ge(w_ready, k + 1)
                        for q in range(KD * FT):
                            g = 3 * k + q // 4
                            if q % 4 == 0 and g >= 8:
                                pe.wait_ge(wt_copied, g - 7)
                            if k < 2:
                                d, f = divmod(q, FT)
                                src = wn[k][:, f * D + d * P:f * D + (d + 1) * P]
                            else:
                                f, o = divmod(q, KD)
                                src = wn[k][:, o * F + f * P:o * F + (f + 1) * P]
                            t = nc.tensor.transpose(PS[:, g % 8, (q % 4) * P:(q % 4 + 1) * P], src, ident[:, :])
                            if q % 4 == 3:
                                t.then_inc(wt_done, 1)

                @block.scalar
                def _(act):
                    for g in range(9):
                        act.wait_ge(wt_done, g + 1)
                        nc.scalar.activation(wT[g // 3][:, (g % 3) * 512:(g % 3 + 1) * 512], PS[:, g % 8, :], ACT.Copy).then_inc(wt_copied, 1)

            with nc.Block() as block:

                @block.vector
                def _(dve):
                    def run(i, u):
                        if not isinstance(i, int):
                            dve.wait_ge(x_done, i - 1)
                        nc.vector.tensor_scalar(row(XN, i), row(XN, i), inv[:, 0:1], MAGIC, ALU.mult, ALU.add).then_inc(rounded, 1)
                        dve.wait_ge(rounded, 3 * i + 1)
                        nc.vector.tensor_scalar(xq[:, u, :], row(XN, i), MAGIC + QMAX, MAGIC - QMAX - 1.0, ALU.min, ALU.max).then_inc(rounded, 1)
                        dve.wait_ge(rounded, 3 * i + 2)
                        nc.vector.tensor_scalar(xq[:, u, :], xq[:, u, :], MAGIC, None, ALU.subtract).then_inc(rounded, 1)
                    run(0, 0)
                    run(1, 1)
                    with dve.Fori(1, B // 2) as j:
                        run(2 * j, 0)
                        run(2 * j + 1, 1)

                @block.tensor
                def _(pe):
                    def run(i, u):
                        pe.wait_ge(rounded, 3 * i + 3)
                        if not isinstance(i, int):
                            pe.wait_ge(x_copied, i - 1)
                        for d in range(KD):
                            last = nc.tensor.transpose(PS[:, u, d * P:(d + 1) * P], xq[:, u, d * P:(d + 1) * P], ident[:, :])
                        last.then_inc(x_done, 1)
                    run(0, 0)
                    run(1, 1)
                    with pe.Fori(1, B // 2) as j:
                        run(2 * j, 0)
                        run(2 * j + 1, 1)

                @block.gpsimd
                def _(pool):
                    pool.nop()

                @block.scalar
                def _(act):
                    for i in range(B):
                        act.wait_ge(x_done, i + 1)
                        nc.scalar.activation(XQ[:, :, i, :], PS[:, i % 2, 0:D].rearrange("p (k s) -> p k s", k=KD), ACT.Copy)\
                          .then_inc(x_copied, 1)

        with ExitStack() as middle:
            mm = Pool(nc, middle, layer)
            BANKS = 6
            PS = middle.enter_context(nc.psum_tensor(f"{layer}_m_ps", [P, 8, 512], F32))
            am, am_all = mm.sb("am", [P, 2, FT]), mm.sb("am_all", [P, 2, FT])
            p_done, p_read, am_done, am_kept = mm.sem("p_done"), mm.sem("p_read"), mm.sem("am_done"), mm.sem("am_kept")
            PER = 2 * FT
            with nc.Block() as block:

                @block.tensor
                def _(pe):
                    def run(n):
                        for q in range(PER):
                            k, f = divmod(q, FT)
                            if not isinstance(n, int) or q >= BANKS:
                                pe.wait_ge(p_read, PER * n + q - BANKS + 1)
                            for d in range(KD):
                                rhs = XQ[:, d, bass.ds(n * (NT // P), NT // P), :].rearrange("p b s -> p (b s)")
                                last = nc.tensor.matmul(PS[:, q % BANKS, :], wT[k][:, d * F + f * P:d * F + (f + 1) * P], rhs,
                                                        start=(d == 0), stop=(d == KD - 1))
                            last.then_inc(p_done, 1)
                    run(0)
                    with pe.Fori(1, NN) as n:
                        run(n)

                @block.vector
                def _(dve):
                    def run(n):
                        for q in range(PER):
                            k, f = divmod(q, FT)
                            dst = (G, U)[k]
                            dve.wait_ge(p_done, PER * n + q + 1)
                            if q == 0 and not isinstance(n, int):
                                dve.wait_ge(am_kept, n)
                            nc.vector.tensor_reduce(am[:, k, f:f + 1], PS[:, q % BANKS, :], AXIS.X, ALU.max,
                                                    apply_absolute_value=True).then_inc(am_done, 1)
                            nc.vector.tensor_scalar(dst[:, f, bass.ds(n * NT, NT)], PS[:, q % BANKS, :], step[:, 0:1], None, ALU.mult)\
                              .then_inc(p_read, 1)
                        dve.wait_ge(am_done, PER * n + PER)
                        if isinstance(n, int):
                            nc.vector.tensor_copy(am_all[:, :, :], am[:, :, :]).then_inc(am_kept, 1)
                        else:
                            nc.vector.tensor_tensor(am_all[:, :, :], am_all[:, :, :], am[:, :, :], ALU.max).then_inc(am_kept, 1)
                    run(0)
                    with dve.Fori(1, NN) as n:
                        run(n)
                    c = Chain(dve, mm.sem("chain1"))
                    dve.wait_ge(am_kept, NN)
                    c.do(nc.vector.tensor_reduce(part[:, 1:3], am_all[:, :, :], AXIS.X, ALU.max))
                    for k in range(2):
                        nc.vector.tensor_scalar(part[:, 1 + k:2 + k], part[:, 1 + k:2 + k], step[:, 0:1], None, ALU.mult).then_inc(found, 1)
                    steps(dve, c, 1, 1.0)
                    steps(dve, c, 2, 1.0)

                @block.gpsimd
                def _(pool):
                    all_tokens(pool, 1)
                    all_tokens(pool, 2)

        def chunk(t, i):
            return t[:, :, :].rearrange("p f s -> p (f s)")[:, bass.ds(i * CH, CH)]

        with ExitStack() as late:
            ml = Pool(nc, late, layer)
            gq, sg = ml.sb("gq", [P, 2, CH]), ml.sb("sg", [P, 2, CH])
            on_grid, clipped, q_ready, sg_ready, sg_clipped, prod = (ml.sem(n) for n in ("on_grid", "clipped", "q_ready", "sg_ready", "sg_clipped", "prod"))
            with nc.Block() as block:

                @block.scalar
                def _(act):
                    with act.Fori(0, NC) as i:
                        nc.scalar.activation(chunk(G, i), chunk(G, i), ACT.Identity, bias=magic[:, :], scale=inv[:, 1:2]).then_inc(on_grid, 1)

                    def run(i, u):
                        act.wait_ge(q_ready, i + 1)
                        if not isinstance(i, int):
                            act.wait_ge(prod, i - 1)
                        nc.scalar.activation(sg[:, u, :], gq[:, u, :], ACT.Sigmoid, scale=step[:, 1:2]).then_inc(sg_ready, 1)
                        act.wait_ge(sg_ready, 2 * i + 1)
                        nc.scalar.activation(sg[:, u, :], sg[:, u, :], ACT.Identity, bias=magic[:, :], scale=SIG).then_inc(sg_ready, 1)
                    run(0, 0)
                    run(1, 1)
                    with act.Fori(1, NC // 2) as j:
                        run(2 * j, 0)
                        run(2 * j + 1, 1)
                    with act.Fori(0, NC) as i:
                        nc.scalar.activation(chunk(U, i), chunk(U, i), ACT.Identity, bias=magic[:, :], scale=inv[:, 2:3]).then_inc(on_grid, 1)

                @block.vector
                def _(dve):
                    def to_integers(i, u):
                        if not isinstance(i, int):
                            dve.wait_ge(prod, i - 1)
                        dve.wait_ge(on_grid, i + 1)
                        nc.vector.tensor_scalar(gq[:, u, :], chunk(G, i), MAGIC + QMAX, MAGIC - QMAX - 1.0, ALU.min, ALU.max)\
                          .then_inc(clipped, 1)
                        dve.wait_ge(clipped, i + 1)
                        nc.vector.tensor_scalar(gq[:, u, :], gq[:, u, :], MAGIC, None, ALU.subtract).then_inc(q_ready, 1)

                    def product(i, u):
                        dve.wait_ge(sg_ready, 2 * i + 2)
                        nc.vector.tensor_scalar(sg[:, u, :], sg[:, u, :], MAGIC + SIG - 1.0, MAGIC, ALU.min, ALU.max).then_inc(sg_clipped, 1)
                        dve.wait_ge(sg_clipped, i + 1)
                        nc.vector.scalar_tensor_tensor(chunk(G, i), sg[:, u, :], MAGIC, gq[:, u, :], ALU.subtract, ALU.mult).then_inc(prod, 1)
                    to_integers(0, 0)
                    to_integers(1, 1)
                    with dve.Fori(1, NC // 2) as j:
                        product(2 * j - 2, 0)
                        to_integers(2 * j, 0)
                        product(2 * j - 1, 1)
                        to_integers(2 * j + 1, 1)
                    product(NC - 2, 0)
                    product(NC - 1, 1)
                    dve.wait_ge(prod, NC)
                    c = Chain(dve, ml.sem("chain3"))
                    c.do(nc.vector.tensor_reduce(part[:, 3:4], G[:, :, :].rearrange("p f s -> p (f s)"), AXIS.X, ALU.max,
                                                 apply_absolute_value=True))
                    nc.vector.tensor_scalar(part[:, 3:4], part[:, 3:4], step[:, 1:2], None, ALU.mult).then_inc(found, 1)
                    steps(dve, c, 3, 1.0 / SIG)
                    c.do(nc.vector.tensor_tensor(inv[:, 3:4], inv[:, 3:4], step[:, 1:2], ALU.mult))

                @block.gpsimd
                def _(pool):
                    all_tokens(pool, 3)

            grid2, low2, int2, up2, prod2 = (ml.sem(n) for n in ("grid2", "low2", "int2", "up2", "prod2"))
            with nc.Block() as block:

                @block.scalar
                def _(act):
                    with act.Fori(0, NC) as i:
                        nc.scalar.activation(chunk(G, i), chunk(G, i), ACT.Identity, bias=magic[:, :], scale=inv[:, 3:4]).then_inc(grid2, 1)

                @block.vector
                def _(dve):
                    with dve.Fori(0, NC) as i:
                        nc.vector.tensor_scalar(chunk(U, i), chunk(U, i), MAGIC + QMAX, MAGIC - QMAX - 1.0, ALU.min, ALU.max).then_inc(up2, 1)
                        dve.wait_ge(grid2, i + 1)
                        nc.vector.tensor_scalar(chunk(G, i), chunk(G, i), MAGIC + QMAX, MAGIC - QMAX - 1.0, ALU.min, ALU.max).then_inc(low2, 1)
                        dve.wait_ge(low2, i + 1)
                        nc.vector.tensor_scalar(chunk(G, i), chunk(G, i), MAGIC, None, ALU.subtract).then_inc(int2, 1)
                        dve.wait_ge(up2, i + 1)
                        dve.wait_ge(int2, i + 1)
                        nc.vector.scalar_tensor_tensor(chunk(G, i), chunk(U, i), MAGIC, chunk(G, i), ALU.subtract, ALU.mult).then_inc(prod2, 1)
                    dve.wait_ge(prod2, NC)
                    c = Chain(dve, ml.sem("chain2"))
                    c.do(nc.vector.tensor_reduce(part[:, 4:5], G[:, :, :].rearrange("p f s -> p (f s)"), AXIS.X, ALU.max,
                                                 apply_absolute_value=True))
                    c.do(nc.vector.tensor_tensor(part[:, 3:4], step[:, 2:3], step[:, 3:4], ALU.mult))
                    nc.vector.tensor_tensor(part[:, 4:5], part[:, 4:5], part[:, 3:4], ALU.mult).then_inc(found, 1)
                    steps(dve, c, 4, 1.0)
                    c.do(nc.vector.tensor_tensor(inv[:, 4:5], inv[:, 4:5], part[:, 3:4], ALU.mult))

                @block.gpsimd
                def _(pool):
                    all_tokens(pool, 4)

            PS = late.enter_context(nc.psum_tensor(f"{layer}_d_ps", [P, 8, 512], F32))
            ob = ml.sb("ob", [P, 2, FT, P])
            grid3, low3, int3, d_done, d_added = (ml.sem(n) for n in ("grid3", "low3", "int3", "d_done", "d_added"))

            def tokens(t, i):
                return t[:, :, bass.ds(i * P, P)]

            with nc.Block() as block:

                @block.scalar
                def _(act):
                    with act.Fori(0, B) as i:
                        nc.scalar.activation(tokens(G, i), tokens(G, i), ACT.Identity, bias=magic[:, :], scale=inv[:, 4:5]).then_inc(grid3, 1)

                @block.vector
                def _(dve):
                    def integers(i, u):
                        if not isinstance(i, int):
                            dve.wait_ge(d_done, i - 1)
                        dve.wait_ge(grid3, i + 1)
                        nc.vector.tensor_scalar(ob[:, u, :, :], tokens(G, i), MAGIC + QMAX, MAGIC - QMAX - 1.0, ALU.min, ALU.max)\
                          .then_inc(low3, 1)
                        dve.wait_ge(low3, i + 1)
                        nc.vector.tensor_scalar(ob[:, u, :, :], ob[:, u, :, :], MAGIC, None, ALU.subtract).then_inc(int3, 1)

                    def add(i, u):
                        dve.wait_ge(d_done, i + 1)
                        nc.vector.scalar_tensor_tensor(row(X, i), PS[:, u, 0:D], step[:, 4:5], row(X, i), ALU.mult, ALU.add)\
                          .then_inc(d_added, 1)
                    integers(0, 0)
                    integers(1, 1)
                    with dve.Fori(1, B // 2) as j:
                        add(2 * j - 2, 0)
                        integers(2 * j, 0)
                        add(2 * j - 1, 1)
                        integers(2 * j + 1, 1)
                    add(B - 2, 0)
                    add(B - 1, 1)

                @block.tensor
                def _(pe):
                    def run(i, u):
                        pe.wait_ge(int3, i + 1)
                        if not isinstance(i, int):
                            pe.wait_ge(d_added, i - 1)
                        for f in range(FT):
                            last = nc.tensor.matmul(PS[:, u, 0:D], ob[:, u, f, :], wT[2][:, f * D:(f + 1) * D], start=(f == 0), stop=(f == FT - 1))
                        last.then_inc(d_done, 1)
                    run(0, 0)
                    run(1, 1)
                    with pe.Fori(1, B // 2) as j:
                        run(2 * j, 0)
                        run(2 * j + 1, 1)
def program(nc, a, out):
    with ExitStack() as stack:
        X = stack.enter_context(nc.sbuf_tensor("X", [P, B, D], F32))
        ident = stack.enter_context(nc.sbuf_tensor("ident", [P, P], F32))
        below = stack.enter_context(nc.sbuf_tensor("below", [P, P], F32))
        constants(nc, a["x"], X, ident, below)
        ctx, ctxT = a["ctx"], a["ctxT"]
        attention(nc, "a0", X, ident, below, ctx, ctxT, 1 / 16, "int_qk", a["mask_qk"], wo=a["L0_woT"], bo=a["L0_bo"])
        mixture(nc, "f0", X, ident, a["L0_router"], None, a["L0_b2"], a["L0_blob"], 8, 512, False)
        attention(nc, "a1", X, ident, below, ctx, ctxT, 1 / 4, "inverted", (a["mask_bool"], a["mask_boolT"]))
        quantized_ffn(nc, "f1", X, ident, a["L1_gate"], a["L1_up"], a["L1_down"], 768)
        attention(nc, "a2", X, ident, below, ctx, ctxT, 1 / 4, "causal", wq=a["L2_wq"], bq=a["L2_bq_heads"], wk=a["L2_wq"], bk=a["L2_bq_heads"],
                  wv=a["L2_wq"], bv=a["L2_bq"], wo=a["L2_wo"], bo=a["L2_bo"])
        lora(nc, "f2", X, ident, (a["L2_router"], a["L2_loraA"]), a["L2_router_b"], a["L2_base"], a["L2_base_b"], a["L2_loraB"], 8, 8, 2.0)
        attention(nc, "a3", X, ident, below, ctx, ctxT, 1 / 4, "int_k", a["mask_k"], wq=a["L3_wq"], bq=a["L3_bq_heads"], wk=a["L3_wk"],
                  bk=a["L3_bk_heads"], wv=a["L3_wv"], bv=a["L3_bv"], wo=a["L3_wo"], bo=a["L3_bo"])
        mixture(nc, "f3", X, ident, a["L3_gw"], a["L3_gb"], a["L3_b2"], a["L3_blob"], 32, 128, True)
        store(nc, X, out)


def blob_of(ins, biases, w2):
    E, F, _ = w2.shape
    parts = [np.transpose(np.asarray(w).reshape(E, KD, P, F // P, P), (0, 2, 3, 1, 4)).reshape(E, P, KD * F) for w in ins]
    parts += [np.transpose(np.asarray(b).reshape(E, F // P, P), (0, 2, 1)) for b in biases]
    parts.append(np.transpose(np.asarray(w2).reshape(E, F // P, P, D), (0, 2, 1, 3)).reshape(E, P, F // P * D))
    return np.concatenate(parts, axis=2)


def by_head(b):
    return np.transpose(np.asarray(b).reshape(T4, T4, DH), (1, 2, 0))


def with_shared(routed, shared, axis):
    halves = np.split(np.asarray(shared), 2, axis=axis - 1)
    return np.concatenate([routed, np.stack(halves)])


def kernel(x, ctx_1024, mask_Bx1xSxS2_ik1, mask_BxS2_bf1, mask_Bx1x1xS2_ik0, **w):
    import concourse.bacc as bacc
    from concourse.bass_utils import run_bass_kernel_spmd

    laid = {
        "x": x, "ctx": ctx_1024, "ctxT": np.transpose(ctx_1024, (0, 2, 1)),
        "mask_qk": mask_Bx1xSxS2_ik1, "mask_k": mask_Bx1x1xS2_ik0,
        "mask_bool": np.ascontiguousarray(mask_BxS2_bf1).view(np.uint8),
        "mask_boolT": np.ascontiguousarray(np.transpose(mask_BxS2_bf1)).view(np.uint8),
        "L0_woT": np.transpose(w["L0_xattn_W_out"]), "L0_bo": w["L0_xattn_b_out"],
        "L1_gate": w["L1_ffn_w_gate"], "L1_up": w["L1_ffn_w_up"], "L1_down": w["L1_ffn_w_down"],
        "L2_wq": w["L2_xattn_Wq"], "L2_bq": w["L2_xattn_bq"], "L2_wo": w["L2_xattn_Wo"], "L2_bo": w["L2_xattn_bo"],
        "L2_base": np.transpose(w["L2_ffn_base_w"]), "L2_base_b": w["L2_ffn_base_b"], "L2_loraA": w["L2_ffn_lora_A"],
        "L2_loraB": w["L2_ffn_lora_B"], "L2_router": np.transpose(w["L2_ffn_router_w"]), "L2_router_b": w["L2_ffn_router_b"],
        "L3_wq": w["L3_xattn_Wq"], "L3_bq_heads": by_head(w["L3_xattn_bq"]), "L3_wk": w["L3_xattn_Wk"],
        "L3_bk_heads": by_head(w["L3_xattn_bk"]), "L2_bq_heads": by_head(w["L2_xattn_bq"]),
        "L3_wv": w["L3_xattn_Wv"], "L3_bv": w["L3_xattn_bv"], "L3_wo": w["L3_xattn_Wo"], "L3_bo": w["L3_xattn_bo"],
        "L3_gw": w["L3_ffn_gw"], "L3_gb": w["L3_ffn_gb"],
        "L3_b2": np.concatenate([w["L3_ffn_b2"], np.reshape(w["L3_ffn_sb2"], (1, D))]),
        "L3_blob": blob_of([with_shared(w["L3_ffn_w1"], w["L3_ffn_sw1"], 2), with_shared(w["L3_ffn_w3"], w["L3_ffn_sw3"], 2)],
                           [with_shared(w["L3_ffn_b1"], w["L3_ffn_sb1"], 1), with_shared(w["L3_ffn_b3"], w["L3_ffn_sb3"], 1)],
                           with_shared(w["L3_ffn_w2"], w["L3_ffn_sw2"], 1)),
        "L0_router": np.transpose(w["L0_ffn_router_w"]), "L0_b2": w["L0_ffn_b2"],
        "L0_blob": blob_of([np.transpose(w["L0_ffn_w1"], (0, 2, 1))], [w["L0_ffn_b1"]], np.transpose(w["L0_ffn_w2"], (0, 2, 1))),
    }
    nc = bacc.Bacc("TRN2", target_bir_lowering=False, num_devices=1)
    arrays, aps = {}, {}
    for name, value in laid.items():
        value = np.ascontiguousarray(value)
        arrays[f"in_{name}"] = value
        aps[name] = nc.dram_tensor(f"in_{name}", value.shape, mybir.dt.from_np(value.dtype), kind="ExternalInput").ap()
    out = nc.dram_tensor("out", x.shape, F32, kind="ExternalOutput").ap()
    program(nc, aps, out)
    return run_bass_kernel_spmd(nc, [arrays], core_ids=[0]).results[0]["out"]
```

```python
import numpy as np
from contextlib import ExitStack

import concourse.bass as bass
from concourse import mybir

F32 = mybir.dt.float32
I32 = mybir.dt.int32
U32 = mybir.dt.uint32
U8 = mybir.dt.uint8
BF16 = mybir.dt.bfloat16
ALU = mybir.AluOpType
ACT = mybir.ActivationFunctionType
AXIS = mybir.AxisListType

B, S, D = 16, 128, 256
P = 128
KD = D // P
H, DH = 16, 16
HT = P // DH
T4 = 4
HP = P // T4
EPS = 1e-5
MASKED = -1e30


def one(i):
    return bass.ds(i, 1)


def row(t, i):
    return t[:, one(i), :].rearrange("p o d -> p (o d)")


def col(t, i):
    return t[:, one(i)]


class Chain:

    def __init__(self, eng, sem):
        self.eng, self.sem, self.n = eng, sem, 0

    def do(self, ins):
        self.n += 1
        ins.then_inc(self.sem, 1)
        self.eng.wait_ge(self.sem, self.n)


class Pool:

    def __init__(self, nc, stack, layer):
        self.nc, self.stack, self.layer, self.sems = nc, stack, layer, []
        stack.callback(self.clear)

    def sb(self, name, shape, dtype=F32):
        return self.stack.enter_context(self.nc.sbuf_tensor(f"{self.layer}_{name}", shape, dtype))

    def sem(self, name):
        self.sems.append(self.stack.enter_context(self.nc.semaphore(f"{self.layer}_{name}")))
        return self.sems[-1]

    def clear(self):
        if self.sems:
            with self.nc.Block() as block:

                @block.gpsimd
                def _(pool):
                    for s in self.sems:
                        pool.sem_clear(s)


def constants(nc, x_dram, parity_dram, X, ident, below, parity):
    with ExitStack() as stack:
        m = Pool(nc, stack, "const")
        loaded, filled, made = m.sem("loaded"), m.sem("filled"), m.sem("made")
        with nc.Block() as block:

            @block.sync
            def _(sp):
                sp.dma_start(X[:, :, :], x_dram.rearrange("b p d -> p b d")).then_inc(loaded, 16)
                sp.dma_start(parity[:, :], parity_dram).then_inc(loaded, 16)
                sp.wait_ge(loaded, 32)

            @block.gpsimd
            def _(pool):
                nc.gpsimd.memset(ident[:, :], 1.0).then_inc(filled, 1)
                nc.gpsimd.memset(below[:, :], 1.0).then_inc(filled, 1)
                pool.wait_ge(filled, 2)
                nc.gpsimd.affine_select(out=ident[:, :], in_=ident[:, :], compare_op=ALU.is_equal, fill=0.0,
                                        base=0, pattern=[[-1, P]], channel_multiplier=1).then_inc(made, 1)
                nc.gpsimd.affine_select(out=below[:, :], in_=below[:, :], compare_op=ALU.is_ge, fill=0.0,
                                        base=0, pattern=[[-1, P]], channel_multiplier=1).then_inc(made, 1)
                pool.wait_ge(made, 2)


def norm_statistics(nc, layer, X, mean, rstd, scale, loads, zeros=(), ones=()):
    with ExitStack() as stack:
        m = Pool(nc, stack, layer + "_stats")
        raw = m.sb("raw", [P, B, 6])
        t = [m.sb(f"t{k}", [P, B]) for k in range(5)]
        halves, chain, var_ready, root_ready = (m.sem(n) for n in ("halves", "chain", "var_ready", "root_ready"))
        filled, loaded = m.sem("filled"), m.sem("loaded")
        even, odd = raw[:, :, 0:3], raw[:, :, 3:6]
        with nc.Block() as block:

            @block.gpsimd
            def _(pool):
                for z in zeros:
                    nc.gpsimd.memset(z, 0.0).then_inc(filled, 1)
                for z in ones:
                    nc.gpsimd.memset(z, 1.0).then_inc(filled, 1)
                if zeros or ones:
                    pool.wait_ge(filled, len(zeros) + len(ones))

            @block.sync
            def _(sp):
                if zeros or ones:
                    sp.wait_ge(filled, len(zeros) + len(ones))
                for dst, src in loads:
                    sp.dma_start(dst, src).then_inc(loaded, 16)
                if loads:
                    sp.wait_ge(loaded, 16 * len(loads))

            @block.vector
            def _(dve):
                with dve.Fori(0, B) as b:
                    nc.vector.bn_stats(out=row(raw, b), in_=row(X, b)).then_inc(halves, 1)
                dve.wait_ge(halves, B)
                c = Chain(dve, chain)
                me, mo = even[:, :, 1:2].rearrange("p b o -> p (b o)"), odd[:, :, 1:2].rearrange("p b o -> p (b o)")
                ve, vo = even[:, :, 2:3].rearrange("p b o -> p (b o)"), odd[:, :, 2:3].rearrange("p b o -> p (b o)")
                c.do(nc.vector.tensor_tensor(t[0][:, :], me, mo, ALU.add))
                c.do(nc.vector.tensor_tensor(t[1][:, :], me, mo, ALU.subtract))
                c.do(nc.vector.tensor_scalar(mean[:, :], t[0][:, :], 0.5, None, ALU.mult))
                c.do(nc.vector.tensor_tensor(t[2][:, :], ve, vo, ALU.add))
                c.do(nc.vector.scalar_tensor_tensor(t[3][:, :], t[1][:, :], 0.25, t[1][:, :], ALU.mult, ALU.mult))
                c.do(nc.vector.scalar_tensor_tensor(t[0][:, :], t[2][:, :], 1.0 / D, t[3][:, :], ALU.mult, ALU.add))
                nc.vector.tensor_scalar(t[1][:, :], t[0][:, :], EPS, None, ALU.add).then_inc(var_ready, 1)
                dve.wait_ge(root_ready, 1)
                c.do(nc.vector.reciprocal(t[3][:, :], t[2][:, :]))
                c.do(nc.vector.tensor_tensor(t[0][:, :], t[3][:, :], t[3][:, :], ALU.mult))
                c.do(nc.vector.tensor_tensor(t[4][:, :], t[0][:, :], t[1][:, :], ALU.mult))
                c.do(nc.vector.tensor_scalar(t[0][:, :], t[4][:, :], -0.5, 1.5, ALU.mult, ALU.add))
                c.do(nc.vector.scalar_tensor_tensor(rstd[:, :], t[3][:, :], float(scale), t[0][:, :], ALU.mult, ALU.mult))

            @block.scalar
            def _(act):
                act.wait_ge(var_ready, 1)
                nc.scalar.activation(t[2][:, :], t[1][:, :], ACT.Sqrt).then_inc(root_ready, 1)


def attention(nc, layer, X, ident, below, parity, ctx, ctxT, scale, mask_kind, mask=None, wq=None, bq=None, wk=None,
              bk=None, wv=None, bv=None, wo=None, bo=None):
    proj = wq is not None
    oproj = wo is not None
    with ExitStack() as stack:
        m = Pool(nc, stack, layer)
        mean, rstd = m.sb("mean", [P, B]), m.sb("rstd", [P, B])
        xn = m.sb("xn", [P, 2, D])
        xo = m.sb("xo", [P, 2, 2 * KD, P])
        kM = m.sb("kM", [P, 2, KD, HT, P])
        vraw = m.sb("vraw", [P, 2, D])
        vx = m.sb("vx", [P, 2, H, DH + 1])
        NB = 1 if mask_kind == "causal" else B
        bias = m.sb("bias", [P, NB, P])
        t_sb, p_sb = m.sb("t", [P, T4, T4 * P]), m.sb("p", [P, T4, T4 * P])
        mx = m.sb("mx", [P, T4, T4])
        pT = m.sb("pT", [P, 2, T4, P])
        rec, o_n = m.sb("rec", [P, H]), m.sb("o_n", [P, D])
        loads, zeros, ones = [], [kM[:, :, :, :, :]], [vx[:, :, :, DH:DH + 1]]
        if oproj:
            wo_sb = m.sb("wo", [P, KD, D])
            bo_sb = m.sb("bo", [P, D])
            loads += [(wo_sb[:, :, :], wo.rearrange("(k p) n -> p k n", p=P)), (bo_sb[:, :], bo.partition_broadcast(P))]
        if proj:
            qT, cT = m.sb("qT", [P, 2, KD, P]), m.sb("cT", [P, 2, KD, P])
            wq_sb, wk_sb, wv_sb = m.sb("wq", [P, KD, D]), m.sb("wk", [P, KD, D]), m.sb("wv", [P, KD, D])
            bv_sb = m.sb("bv", [P, D])
            bq_sb, bk_sb, bqs, bkm = m.sb("bq", [P, KD]), m.sb("bk", [P, KD]), m.sb("bqs", [P, KD]), m.sb("bkm", [P, KD, 2])
            loads += [(w_sb[:, :, :], w.rearrange("(k p) n -> p k n", p=P)) for w_sb, w in ((wq_sb, wq), (wk_sb, wk), (wv_sb, wv))]
            loads += [(bq_sb[:, :], bq), (bk_sb[:, :], bk), (bv_sb[:, :], bv.partition_broadcast(P))]
        if mask_kind == "int_qk":
            mask_in = m.sb("mask_in", [P, B, P], I32)
            loads.append((mask_in[:, :, :], mask.rearrange("b o q k -> (o q) b k")))
        elif mask_kind == "int_k":
            mask_in = m.sb("mask_in", [P, B, P], I32)
            loads.append((mask_in[:, :, :].rearrange("p b k -> p (b k)"), mask.rearrange("b x y k -> (x y b k)").partition_broadcast(P)))
        elif mask_kind == "inverted":
            mask_in, mask_q = m.sb("mask_in", [P, B, P], U8), m.sb("mask_q", [P, B], U8)
            qm = m.sb("qm", [P, B])
            inv = m.sb("inv", [P, P])
            loads += [(mask_in[:, :, :].rearrange("p b k -> p (b k)"), mask[0].rearrange("b k -> (b k)").partition_broadcast(P)),
                      (mask_q[:, :], mask[1])]
        norm_statistics(nc, layer, X, mean, rstd, 1.0 if proj else scale, loads, zeros, ones)

        PS = stack.enter_context(nc.psum_tensor(f"{layer}_ps", [P, 8, 512], F32))
        ps_s = PS[:, 0:4, :]
        ps_t = [PS[:, 4, :], PS[:, 5, :]]
        ps_v = PS[:, 6, 0:H * (DH + 1)].rearrange("p (h d) -> p h d", h=H)
        ps_q = PS[:, 7, :].rearrange("p (t s) -> p t s", t=2 * KD)
        half_b = PS[:, 7, D:2 * D]

        prepared = m.sem("prepared")
        ctx_in = [m.sem("ctx_in0"), m.sem("ctx_in1")]
        xn_ready, xo_done, xo_copied = m.sem("xn_ready"), m.sem("xo_done"), m.sem("xo_copied")
        kv_done, qo_done = m.sem("kv_done"), m.sem("qo_done")
        q_ready, k_ready_low, k_ready, v_ready = (m.sem(n) for n in ("q_ready", "k_ready_low", "k_ready", "v_ready"))
        s_done, biased, maxed, shifted, exped = (m.sem(n) for n in ("s_done", "biased", "maxed", "shifted", "exped"))
        pT_done, pT_copied, av_done, inverted, normed = (m.sem(n) for n in ("pT_done", "pT_copied", "av_done", "inverted", "normed"))
        bo_added, resid_done = m.sem("bo_added"), m.sem("resid_done")
        DMAS = KD if proj else HT + 1
        LAST = B - 1

        with nc.Block() as block:

            @block.vector
            def _(dve):
                c = Chain(dve, prepared)
                if mask_kind in ("int_qk", "int_k"):
                    c.do(nc.vector.tensor_scalar(bias[:, :, :], mask_in[:, :, :], 0.0, MASKED, ALU.is_equal, ALU.mult))
                elif mask_kind == "causal":
                    c.do(nc.vector.tensor_scalar(bias[:, 0, :], below[:, :], 0.0, MASKED, ALU.is_equal, ALU.mult))
                else:
                    c.do(nc.vector.tensor_scalar(inv[:, :], below[:, :], -999999.0, None, ALU.mult))
                    c.do(nc.vector.tensor_tensor(bias[:, :, :], mask_in[:, :, :], inv[:, :].unsqueeze(1).to_broadcast([P, B, P]), ALU.mult))
                    c.do(nc.vector.tensor_copy(qm[:, :], mask_q[:, :]))
                if proj:
                    c.do(nc.vector.tensor_scalar(bqs[:, :], bq_sb[:, :], scale, None, ALU.mult))
                    c.do(nc.vector.tensor_tensor(bkm[:, :, :], bk_sb[:, :].unsqueeze(2).to_broadcast([P, KD, 2]),
                                                 parity[:, :].unsqueeze(1).to_broadcast([P, KD, 2]), ALU.mult))

        def body(engine, run):
            run(-2, 0, True, False, False, False)
            run(-1, 1, True, True, False, False)
            run(0, 0, True, True, True, False)
            run(1, 1, True, True, True, True)
            with engine.Fori(1, (B - 2) // 2) as j:
                run(2 * j, 0, True, True, True, True)
                run(2 * j + 1, 1, True, True, True, True)
            run(LAST - 1, 0, False, True, True, True)
            run(LAST, 1, False, False, True, True)
            run(LAST + 1, 0, False, False, False, True)

        def known(i):
            return isinstance(i, int)

        def qo_count(i):
            return i + 3 if proj else i

        with nc.Block() as block:

            @block.sync
            def _(sp):
                def run(i, u, queries, scores, values, output):
                    if queries:
                        k = i + 2
                        if not known(i) or k >= 2:
                            if proj:
                                sp.wait_ge(kv_done, k)
                            else:
                                sp.wait_ge(s_done, T4 * (k - 1))
                                sp.wait_ge(v_ready, k - 1)
                        if proj:
                            for d in range(KD):
                                sp.dma_start(cT[:, u, d, :], ctxT[one(k), d * P:(d + 1) * P, :].rearrange("o p s -> (o p) s"))\
                                  .then_inc(ctx_in[u], 16)
                        else:
                            for g in range(HT):
                                sp.dma_start(kM[g * DH:(g + 1) * DH, u, :, g, :], ctxT[one(k), :, :].rearrange("o (t h r) s -> h (o r) t s", t=KD, r=DH)[g])\
                                  .then_inc(ctx_in[u], 16)
                            sp.dma_start(vraw[:, u, :], ctx[one(k), :, :].rearrange("o s d -> (o s) d")).then_inc(ctx_in[u], 16)
                body(sp, run)

            @block.gpsimd
            def _(pool):
                def run(i, u, queries, scores, values, output):
                    if queries and oproj:
                        k = i + 2
                        pool.wait_ge(xn_ready, k + 1)
                        nc.gpsimd.tensor_tensor(row(X, k), row(X, k), bo_sb[:, :], ALU.add).then_inc(bo_added, 1)
                    if scores:
                        k, w = i + 1, 1 - u
                        if not proj:
                            if known(i):
                                pool.wait_ge(ctx_in[w], 16 * DMAS * ((k - w) // 2 + 1))
                            else:
                                pool.wait_ge(ctx_in[w], 8 * DMAS * (k - w) + 16 * DMAS)
                            if not known(i) or k >= 2:
                                pool.wait_ge(av_done, T4 * (k - 1))
                            nc.gpsimd.tensor_tensor(vx[:, w, :, 0:DH], vraw[:, w, :].rearrange("p (h d) -> p h d", h=H),
                                                    vx[:, w, :, DH:DH + 1].to_broadcast([P, H, DH]), ALU.mult).then_inc(v_ready, 1)
                        for c in range(T4):
                            pool.wait_ge(maxed, T4 * k + c + 1)
                            tc_ = t_sb[:, c, :].rearrange("p (t s) -> p t s", t=T4)
                            nc.gpsimd.tensor_tensor(tc_, tc_, mx[:, c, :].unsqueeze(2).to_broadcast([P, T4, P]), ALU.subtract)\
                              .then_inc(shifted, 1)
                body(pool, run)

            @block.vector
            def _(dve):
                def run(i, u, queries, scores, values, output):
                    if queries:
                        k = i + 2
                        if not known(i) or k >= 2:
                            dve.wait_ge(xo_done, k - 1)
                        nc.vector.tensor_scalar(xn[:, u, :], row(X, k), col(mean, k), col(rstd, k), ALU.subtract, ALU.mult)\
                          .then_inc(xn_ready, 1)
                    if output:
                        k = i - 1
                        dve.wait_ge(av_done, T4 * (k + 1))
                        nc.vector.reciprocal(rec[:, :], ps_v[:, :, DH:DH + 1].rearrange("p h o -> p (h o)")).then_inc(inverted, 1)
                        dve.wait_ge(inverted, k + 1)
                        if not oproj and (not known(i) or k >= 1):
                            dve.wait_ge(resid_done, k)
                        nc.vector.tensor_tensor(o_n[:, :].rearrange("p (h d) -> p h d", h=H), ps_v[:, :, 0:DH],
                                                rec[:, :].unsqueeze(2).to_broadcast([P, H, DH]), ALU.mult).then_inc(normed, 1)

                    def add_bias(c, k=i + 1):
                        dve.wait_ge(s_done, T4 * k + c + 1)
                        if not known(i) or k >= 1:
                            dve.wait_ge(exped, T4 * (k - 1) + c + 1)
                        b = bias[:, 0, :] if NB == 1 else row(bias, k)
                        nc.vector.tensor_tensor(t_sb[:, c, :].rearrange("p (t s) -> p t s", t=T4),
                                                ps_s[:, c, :].rearrange("p (t s) -> p t s", t=T4),
                                                b.unsqueeze(1).to_broadcast([P, T4, P]), ALU.add).then_inc(biased, 1)

                    def maximum(c, k=i + 1):
                        dve.wait_ge(biased, T4 * k + c + 1)
                        nc.vector.tensor_reduce(mx[:, c, :], t_sb[:, c, :].rearrange("p (t s) -> p t s", t=T4),
                                                AXIS.X, ALU.max).then_inc(maxed, 1)
                    if scores:
                        add_bias(0)
                        add_bias(1)
                        maximum(0)
                        add_bias(2)
                        maximum(1)
                    if queries and proj:
                        dve.wait_ge(kv_done, i + 3)
                        for c in range(T4 // 2):
                            at = slice(c * HP, (c + 1) * HP)
                            for e in range(2):
                                last = nc.vector.scalar_tensor_tensor(kM[at, u, :, 2 * c + e, :], ps_q[at, 0:KD, :], parity[at, e:e + 1],
                                                                      bkm[at, :, e:e + 1].to_broadcast([HP, KD, P]), ALU.mult, ALU.add)
                        last.then_inc(k_ready_low, 1)
                    if scores:
                        add_bias(3)
                        maximum(2)
                    if scores and proj:
                        dve.wait_ge(kv_done, i + 3)
                        if queries:
                            dve.wait_ge(k_ready, i + 3)
                        if not known(i) or i >= 1:
                            dve.wait_ge(av_done, T4 * i)
                        nc.vector.tensor_tensor(vx[:, 1 - u, :, 0:DH], half_b.rearrange("p (h d) -> p h d", h=H),
                                                bv_sb[:, :].rearrange("p (h d) -> p h d", h=H), ALU.add).then_inc(v_ready, 1)
                    if scores:
                        maximum(3)
                    if queries and proj:
                        k = i + 2
                        dve.wait_ge(qo_done, qo_count(i))
                        if not known(i) or k >= 2:
                            dve.wait_ge(s_done, T4 * (k - 1))
                        nc.vector.scalar_tensor_tensor(qT[:, u, :, :], ps_q[:, 0:KD, :], float(scale),
                                                       bqs[:, :].unsqueeze(2).to_broadcast([P, KD, P]), ALU.mult, ALU.add)\
                          .then_inc(q_ready, 1)
                    if output:
                        k = i - 1
                        if oproj:
                            dve.wait_ge(qo_done, qo_count(i))
                            dve.wait_ge(bo_added, k + 1)
                            nc.vector.tensor_tensor(row(X, k), row(X, k), half_b, ALU.add).then_inc(resid_done, 1)
                        else:
                            dve.wait_ge(normed, k + 1)
                            nc.vector.scalar_tensor_tensor(row(X, k), o_n[:, :], col(qm, k), row(X, k), ALU.mult, ALU.add)\
                              .then_inc(resid_done, 1)
                body(dve, run)

            @block.scalar
            def _(act):
                def run(i, u, queries, scores, values, output):
                    def copy_pT(c):
                        n = T4 * i + c
                        act.wait_ge(pT_done, n + 1)
                        if not known(i) or n >= 2:
                            act.wait_ge(av_done, n - 1)
                        nc.scalar.activation(pT[:, c % 2, :, :], ps_t[c % 2].rearrange("p (t s) -> p t s", t=T4), ACT.Copy)\
                          .then_inc(pT_copied, 1)

                    def exponential(c, k=i + 1):
                        act.wait_ge(shifted, T4 * k + c + 1)
                        if not known(i) or k >= 1:
                            act.wait_ge(pT_done, T4 * (k - 1) + c + 1)
                        nc.scalar.activation(p_sb[:, c, :], t_sb[:, c, :], ACT.Exp).then_inc(exped, 1)
                    if values:
                        copy_pT(0)
                        copy_pT(1)
                    if queries or (output and oproj):
                        act.wait_ge(xo_done, i + 3)
                        parts = slice(0 if queries else KD, 2 * KD if output and oproj else KD)
                        nc.scalar.activation(xo[:, u, parts, :], ps_q[:, parts, :], ACT.Copy).then_inc(xo_copied, 1)
                    if scores:
                        exponential(0)
                    if queries and proj:
                        act.wait_ge(kv_done, i + 3)
                        for c in range(T4 // 2, T4):
                            at = slice(c * HP, (c + 1) * HP)
                            for t in range(KD):
                                for e in range(2):
                                    last = nc.scalar.activation(kM[at, u, t, 2 * c + e, :], ps_q[at, t, :], ACT.Identity,
                                                                bias=bkm[at, t, e:e + 1], scale=parity[at, e:e + 1])
                        last.then_inc(k_ready, 1)
                    if values:
                        copy_pT(2)
                    if scores:
                        exponential(1)
                    if values:
                        copy_pT(3)
                    if scores:
                        exponential(2)
                    if scores:
                        exponential(3)
                body(act, run)

            @block.tensor
            def _(pe):
                def project(w, src, u):
                    for t in range(KD):
                        for d in range(KD):
                            last = nc.tensor.matmul(ps_q[:, t, :], w[:, d, t * P:(t + 1) * P], src[:, u, d, :],
                                                    start=(d == 0), stop=(d == KD - 1))
                    return last

                def run(i, u, queries, scores, values, output):
                    def score(c, k=i + 1, w=1 - u):
                        if c == 0:
                            pe.wait_ge(q_ready if proj else xo_copied, k + 1)
                            if proj:
                                pe.wait_ge(k_ready, k + 1)
                                pe.wait_ge(k_ready_low, k + 1)
                            elif known(i):
                                pe.wait_ge(ctx_in[w], 16 * DMAS * ((k - w) // 2 + 1))
                            else:
                                pe.wait_ge(ctx_in[w], 8 * DMAS * (k - w) + 16 * DMAS)
                        if not known(i) or k >= 1:
                            pe.wait_ge(biased, T4 * (k - 1) + c + 1)
                        for t in range(KD):
                            last = nc.tensor.matmul(ps_s[:, c, t * 2 * P:(t + 1) * 2 * P], (qT if proj else xo)[:, w, t, :],
                                                    kM[:, w, t, 2 * c:2 * c + 2, :].rearrange("p e s -> p (e s)"), start=True, stop=True)
                        last.then_inc(s_done, 1)

                    def transpose_p(c):
                        n = T4 * i + c
                        pe.wait_ge(exped, n + 1)
                        if not known(i) or n >= 2:
                            pe.wait_ge(pT_copied, n - 1)
                        for t in range(T4):
                            last = nc.tensor.transpose(ps_t[c % 2][:, t * P:(t + 1) * P], p_sb[:, c, t * P:(t + 1) * P], ident[:, :])
                        last.then_inc(pT_done, 1)

                    def apply_v(c):
                        pe.wait_ge(pT_copied, T4 * i + c + 1)
                        if c == 0:
                            pe.wait_ge(v_ready, i + 1)
                            if not known(i) or i >= 1:
                                pe.wait_ge(normed, i)
                        for t in range(T4):
                            h = 8 * (t // 2) + 2 * c + t % 2
                            last = nc.tensor.matmul(ps_v[:, h, :], pT[:, c % 2, t, :], vx[:, u, h, :], start=True, stop=True)
                        last.then_inc(av_done, 1)

                    if scores:
                        score(0)
                    if values:
                        transpose_p(0)
                    if scores:
                        score(1)
                    if values:
                        transpose_p(1)
                    if queries or (output and oproj):
                        if oproj and (not known(i) or i >= 2):
                            pe.wait_ge(resid_done, i - 1)
                        if queries:
                            pe.wait_ge(xn_ready, i + 3)
                            for d in range(KD):
                                last = nc.tensor.transpose(ps_q[:, d, :], xn[:, u, d * P:(d + 1) * P], ident[:, :])
                        if output and oproj:
                            pe.wait_ge(normed, i)
                            for d in range(KD):
                                last = nc.tensor.transpose(ps_q[:, KD + d, :], o_n[:, d * P:(d + 1) * P], ident[:, :])
                        last.then_inc(xo_done, 1)
                    if scores:
                        score(2)
                    if values:
                        apply_v(0)
                    if proj and (queries or scores):
                        pe.wait_ge(xo_copied, i + 3)
                        if queries:
                            if known(i):
                                pe.wait_ge(ctx_in[u], 16 * DMAS * ((i + 2 - u) // 2 + 1))
                            else:
                                pe.wait_ge(ctx_in[u], 8 * DMAS * (i + 2 - u) + 16 * DMAS)
                            last = project(wk_sb, cT, u)
                        if scores:
                            for d in range(KD):
                                last = nc.tensor.matmul(half_b, cT[:, 1 - u, d, :], wv_sb[:, d, :], start=(d == 0), stop=(d == KD - 1))
                        last.then_inc(kv_done, 1)
                    if scores:
                        score(3)
                    if values:
                        transpose_p(2)
                        apply_v(1)
                        transpose_p(3)
                    if (queries and proj) or (output and oproj):
                        if proj and scores:
                            pe.wait_ge(v_ready, i + 2)
                        elif proj and queries:
                            pe.wait_ge(k_ready, i + 3)
                            pe.wait_ge(k_ready_low, i + 3)
                        else:
                            pe.wait_ge(xo_copied, i + 3)
                        if output and oproj:
                            for d in range(KD):
                                last = nc.tensor.matmul(half_b, xo[:, u, KD + d, :], wo_sb[:, d, :], start=(d == 0), stop=(d == KD - 1))
                        if queries and proj:
                            last = project(wq_sb, xo, u)
                        last.then_inc(qo_done, 1)
                    if values:
                        apply_v(2)
                        apply_v(3)
                body(pe, run)


def store(nc, X, out):
    with ExitStack() as stack:
        stored = stack.enter_context(nc.semaphore("stored"))
        with nc.Block() as block:

            @block.sync
            def _(sp):
                sp.dma_start(out.rearrange("b p d -> p b d"), X[:, :, :]).then_inc(stored, 16)
                sp.wait_ge(stored, 16)


def norm_and_product(nc, layer, X, ident, mean, rstd, small, logits, XT=None, base=None, small_bias=None, base_bias=None):
    N = small.shape[2]
    with ExitStack() as stack:
        m = Pool(nc, stack, layer + "_np")
        xn, xs = m.sb("xn", [P, 2, D]), m.sb("xs", [P, 2, KD, P])
        PS = stack.enter_context(nc.psum_tensor(f"{layer}_np_ps", [P, 8, 512], F32))
        xn_ready, x_done, x_copied, kept = m.sem("xn_ready"), m.sem("x_done"), m.sem("x_copied"), m.sem("kept")
        l_done, l_read, b_done, b_added, bias_added = (m.sem(n) for n in ("l_done", "l_read", "b_done", "b_added", "bias_added"))

        def body(engine, run):
            run(-1, 1, True, False)
            run(0, 0, True, True)
            run(1, 1, True, True)
            with engine.Fori(1, B // 2 - 1) as j:
                run(2 * j, 0, True, True)
                run(2 * j + 1, 1, True, True)
            run(B - 2, 0, True, True)
            run(B - 1, 1, False, True)

        def known(i):
            return isinstance(i, int)

        with nc.Block() as block:

            @block.vector
            def _(dve):
                def run(i, u, ahead, now):
                    if ahead:
                        k = i + 1
                        if not known(i) or k >= 2:
                            dve.wait_ge(x_done, k - 1)
                        nc.vector.tensor_scalar(xn[:, 1 - u, :], row(X, k), col(mean, k), col(rstd, k), ALU.subtract, ALU.mult)\
                          .then_inc(xn_ready, 1)
                    if now:
                        if XT is not None:
                            dve.wait_ge(x_copied, i + 1)
                            nc.vector.tensor_copy(XT[:, :, one(i), :].rearrange("p k o s -> p k (o s)"), xs[:, u, :, :]).then_inc(kept, 1)
                        dve.wait_ge(l_done, i + 1)
                        if small_bias is None:
                            nc.vector.tensor_copy(row(logits, i), PS[:, 2 + u, 0:N]).then_inc(l_read, 1)
                        else:
                            nc.vector.tensor_tensor(row(logits, i), PS[:, 2 + u, 0:N], small_bias[:, :], ALU.add).then_inc(l_read, 1)
                        if base is not None:
                            dve.wait_ge(b_done, i + 1)
                            dve.wait_ge(bias_added, i + 1)
                            nc.vector.tensor_tensor(row(X, i), row(X, i), PS[:, 4 + u, 0:D], ALU.add).then_inc(b_added, 1)
                body(dve, run)

            @block.gpsimd
            def _(pool):
                if base is not None:
                    def run(i, u, ahead, now):
                        if ahead:
                            pool.wait_ge(xn_ready, i + 2)
                            nc.gpsimd.tensor_tensor(row(X, i + 1), row(X, i + 1), base_bias[:, :], ALU.add).then_inc(bias_added, 1)
                    body(pool, run)

            @block.scalar
            def _(act):
                def run(i, u, ahead, now):
                    if ahead:
                        k, w = i + 1, 1 - u
                        act.wait_ge(x_done, k + 1)
                        if not known(i) or k >= 2:
                            act.wait_ge(l_done, k - 1)
                            if base is not None:
                                act.wait_ge(b_done, k - 1)
                            if XT is not None:
                                act.wait_ge(kept, k - 1)
                        nc.scalar.activation(xs[:, w, :, :], PS[:, w, 0:D].rearrange("p (k s) -> p k s", k=KD), ACT.Copy)\
                          .then_inc(x_copied, 1)
                body(act, run)

            @block.tensor
            def _(pe):
                def run(i, u, ahead, now):
                    if ahead:
                        k, w = i + 1, 1 - u
                        pe.wait_ge(xn_ready, k + 1)
                        if not known(i) or k >= 2:
                            pe.wait_ge(x_copied, k - 1)
                        for d in range(KD):
                            last = nc.tensor.transpose(PS[:, w, d * P:(d + 1) * P], xn[:, w, d * P:(d + 1) * P], ident[:, :])
                        last.then_inc(x_done, 1)
                    if now:
                        pe.wait_ge(x_copied, i + 1)
                        if not known(i) or i >= 2:
                            pe.wait_ge(l_read, i - 1)
                        for d in range(KD):
                            last = nc.tensor.matmul(PS[:, 2 + u, 0:N], xs[:, u, d, :], small[:, d, :], start=(d == 0), stop=(d == KD - 1))
                        last.then_inc(l_done, 1)
                        if base is not None:
                            if not known(i) or i >= 2:
                                pe.wait_ge(b_added, i - 1)
                            for d in range(KD):
                                last = nc.tensor.matmul(PS[:, 4 + u, 0:D], xs[:, u, d, :], base[:, d, :], start=(d == 0), stop=(d == KD - 1))
                            last.then_inc(b_done, 1)
                body(pe, run)


def add_product(nc, layer, X, ident, coef, rows, K):
    with ExitStack() as stack:
        m = Pool(nc, stack, layer + "_ap")
        cs, cT = m.sb("cs", [P, 2, P]), m.sb("cT", [K, 2, P])
        cleared = m.sem("cleared")
        PS = stack.enter_context(nc.psum_tensor(f"{layer}_ap_ps", [P, 8, 512], F32))
        staged, t_done, t_copied, r_done, added = (m.sem(n) for n in ("staged", "t_done", "t_copied", "r_done", "added"))

        def body(engine, run):
            run(-1, 1, True, False)
            run(0, 0, True, True)
            run(1, 1, True, True)
            with engine.Fori(1, B // 2 - 1) as j:
                run(2 * j, 0, True, True)
                run(2 * j + 1, 1, True, True)
            run(B - 2, 0, True, True)
            run(B - 1, 1, False, True)

        def known(i):
            return isinstance(i, int)

        with nc.Block() as block:

            @block.gpsimd
            def _(pool):
                nc.gpsimd.memset(cs[:, :, :], 0.0).then_inc(cleared, 1)

            @block.vector
            def _(dve):
                dve.wait_ge(cleared, 1)

                def run(i, u, ahead, now):
                    if ahead:
                        k = i + 1
                        if not known(i) or k >= 2:
                            dve.wait_ge(t_done, k - 1)
                        nc.vector.tensor_copy(cs[:, 1 - u, 0:K], coef[:, one(k), 0:K].rearrange("p o k -> p (o k)")).then_inc(staged, 1)
                    if now:
                        dve.wait_ge(r_done, i + 1)
                        nc.vector.tensor_tensor(row(X, i), row(X, i), PS[:, 2 + u, 0:D], ALU.add).then_inc(added, 1)
                body(dve, run)

            @block.scalar
            def _(act):
                def run(i, u, ahead, now):
                    if ahead:
                        k, w = i + 1, 1 - u
                        act.wait_ge(t_done, k + 1)
                        if not known(i) or k >= 2:
                            act.wait_ge(r_done, k - 1)
                        nc.scalar.activation(cT[:, w, :], PS[0:K, w, 0:P], ACT.Copy).then_inc(t_copied, 1)
                body(act, run)

            @block.tensor
            def _(pe):
                def run(i, u, ahead, now):
                    if ahead:
                        k, w = i + 1, 1 - u
                        pe.wait_ge(staged, k + 1)
                        if not known(i) or k >= 2:
                            pe.wait_ge(t_copied, k - 1)
                        nc.tensor.transpose(PS[:, w, 0:P], cs[:, w, :], ident[:, :]).then_inc(t_done, 1)
                    if now:
                        pe.wait_ge(t_copied, i + 1)
                        if not known(i) or i >= 2:
                            pe.wait_ge(added, i - 1)
                        nc.tensor.matmul(PS[:, 2 + u, 0:D], cT[:, u, :], rows[0:K, :], start=True, stop=True).then_inc(r_done, 1)
                body(pe, run)


def spread(t, n):
    return t.unsqueeze(2).to_broadcast([P, B, n])


def select_top(nc, c, combine, numbers, hit, index, values, count, E):
    for j in range(count):
        c.do(nc.vector.tensor_tensor(hit, numbers, spread(index[:, :, j], E), ALU.is_equal))
        if values is not None:
            c.do(nc.vector.tensor_tensor(hit, hit, spread(values[:, :, j], E), ALU.mult))
        if j == 0:
            c.do(nc.vector.tensor_copy(combine, hit))
        else:
            c.do(nc.vector.tensor_tensor(combine, combine, hit, ALU.add))


def top_picks(nc, c, values8, index8, index_f, source):
    for b in range(B):
        last = nc.vector.max(values8[:, b, :], source[:, b, :])
        if b == B - 1:
            c.do(last)
        else:
            last.then_inc(c.sem, 1)
            c.n += 1
    for b in range(B):
        last = nc.vector.max_index(index8[:, b, :], values8[:, b, :], source[:, b, :])
        if b == B - 1:
            c.do(last)
        else:
            last.then_inc(c.sem, 1)
            c.n += 1
    c.do(nc.vector.tensor_copy(index_f[:, :, :], index8[:, :, :]))


def route_top2(nc, layer, logits, combine, E):
    with ExitStack() as stack:
        m = Pool(nc, stack, layer + "_route")
        n_i, n_f = m.sb("n_i", [P, B, E], I32), m.sb("n_f", [P, B, E])
        v8, i8, i8f, hit = m.sb("v8", [P, B, 8]), m.sb("i8", [P, B, 8], U32), m.sb("i8f", [P, B, 8]), m.sb("hit", [P, B, E])
        gap, e, p = m.sb("gap", [P, B]), m.sb("e", [P, B]), m.sb("p", [P, B, 2])
        numbered, chain, gap_ready, e_ready = (m.sem(n) for n in ("numbered", "chain", "gap_ready", "e_ready"))
        with nc.Block() as block:

            @block.gpsimd
            def _(pool):
                nc.gpsimd.iota(n_i[:, :, :], pattern=[[0, B], [1, E]], base=0, channel_multiplier=0).then_inc(numbered, 1)

            @block.scalar
            def _(act):
                act.wait_ge(gap_ready, 1)
                nc.scalar.activation(e[:, :], gap[:, :], ACT.Exp).then_inc(e_ready, 1)

            @block.vector
            def _(dve):
                c = Chain(dve, chain)
                dve.wait_ge(numbered, 1)
                c.do(nc.vector.tensor_copy(n_f[:, :, :], n_i[:, :, :]))
                top_picks(nc, c, v8, i8, i8f, logits)
                nc.vector.tensor_tensor(gap[:, :], v8[:, :, 1], v8[:, :, 0], ALU.subtract).then_inc(gap_ready, 1)
                dve.wait_ge(e_ready, 1)
                c.do(nc.vector.tensor_scalar(gap[:, :], e[:, :], 1.0, None, ALU.add))
                c.do(nc.vector.reciprocal(p[:, :, 0], gap[:, :]))
                c.do(nc.vector.tensor_tensor(p[:, :, 1], p[:, :, 0], e[:, :], ALU.mult))
                select_top(nc, c, combine[:, :, 0:E], n_f[:, :, :], hit[:, :, :], i8f, p, 2, E)


def softmax_rows(nc, c, dve, act_ready, e_ready, scores, top, N):
    c.do(nc.vector.tensor_reduce(top, scores, AXIS.X, ALU.max))
    nc.vector.tensor_tensor(scores, scores, spread(top, N), ALU.subtract).then_inc(act_ready, 1)
    dve.wait_ge(e_ready, 1)
    c.do(nc.vector.tensor_reduce(top, scores, AXIS.X, ALU.add))
    c.do(nc.vector.reciprocal(top, top))
    c.do(nc.vector.tensor_tensor(scores, scores, spread(top, N), ALU.mult))


def route_grouped(nc, layer, logits, combine, E, GROUPS, TOP_GROUPS, TOP):
    G = E // GROUPS
    assert G == 4 and GROUPS == 8
    with ExitStack() as stack:
        m = Pool(nc, stack, layer + "_route")
        n_i, n_f = m.sb("n_i", [P, B, E], I32), m.sb("n_f", [P, B, E])
        v8, i8, i8f, hit = m.sb("v8", [P, B, 8]), m.sb("i8", [P, B, 8], U32), m.sb("i8f", [P, B, 8]), m.sb("hit", [P, B, E])
        top, masked = m.sb("top", [P, B]), m.sb("masked", [P, B, E])
        hi, lo = m.sb("hi", [P, 2, B, GROUPS]), m.sb("lo", [P, 2, B, GROUPS])
        gs, keep = m.sb("gs", [P, B, GROUPS]), m.sb("keep", [P, B, GROUPS])
        numbered, chain, act_ready, e_ready = (m.sem(n) for n in ("numbered", "chain", "act_ready", "e_ready"))
        with nc.Block() as block:

            @block.gpsimd
            def _(pool):
                nc.gpsimd.iota(n_i[:, :, :], pattern=[[0, B], [1, E]], base=0, channel_multiplier=0).then_inc(numbered, 1)
                pool.wait_ge(numbered, 1)
                nc.gpsimd.memset(combine[:, :, E:], 1.0).then_inc(numbered, 1)

            @block.scalar
            def _(act):
                act.wait_ge(act_ready, 1)
                nc.scalar.activation(logits[:, :, :], logits[:, :, :], ACT.Exp).then_inc(e_ready, 1)

            @block.vector
            def _(dve):
                c = Chain(dve, chain)
                dve.wait_ge(numbered, 2)
                c.do(nc.vector.tensor_copy(n_f[:, :, :], n_i[:, :, :]))
                softmax_rows(nc, c, dve, act_ready, e_ready, logits[:, :, :], top[:, :], E)
                s = logits[:, :, :].rearrange("p b (g m) -> p b g m", m=G)
                for k in range(2):
                    c.do(nc.vector.tensor_tensor(hi[:, k], s[:, :, :, 2 * k], s[:, :, :, 2 * k + 1], ALU.max))
                    c.do(nc.vector.tensor_tensor(lo[:, k], s[:, :, :, 2 * k], s[:, :, :, 2 * k + 1], ALU.min))
                c.do(nc.vector.tensor_tensor(gs[:, :, :], hi[:, 0], hi[:, 1], ALU.max))
                c.do(nc.vector.tensor_tensor(keep[:, :, :], hi[:, 0], hi[:, 1], ALU.min))
                c.do(nc.vector.tensor_tensor(hi[:, 0], lo[:, 0], lo[:, 1], ALU.max))
                c.do(nc.vector.tensor_tensor(hi[:, 1], hi[:, 0], keep[:, :, :], ALU.max))
                c.do(nc.vector.tensor_tensor(gs[:, :, :], gs[:, :, :], hi[:, 1], ALU.add))
                top_picks(nc, c, v8, i8, i8f, gs)
                select_top(nc, c, keep[:, :, :], n_f[:, :, 0:GROUPS], hit[:, :, 0:GROUPS], i8f, None, TOP_GROUPS, GROUPS)
                m4 = masked[:, :, :].rearrange("p b (g m) -> p b g m", m=G)
                c.do(nc.vector.tensor_scalar(gs[:, :, :], keep[:, :, :], 1.0, -MASKED, ALU.subtract, ALU.mult))
                c.do(nc.vector.tensor_tensor(m4, s, keep[:, :, :].unsqueeze(3).to_broadcast([P, B, GROUPS, G]), ALU.mult))
                c.do(nc.vector.tensor_tensor(m4, m4, gs[:, :, :].unsqueeze(3).to_broadcast([P, B, GROUPS, G]), ALU.add))
                top_picks(nc, c, v8, i8, i8f, masked)
                select_top(nc, c, combine[:, :, 0:E], n_f[:, :, :], hit[:, :, :], i8f, v8, TOP, E)


def experts(nc, layer, X, XT, combine, blob, E, F, gated):
    FT = F // P
    HID = FT * (2 if gated else 1)
    NT = 512
    UNITS = B * P // NT
    SUB = NT // P
    W1, BI = KD * F * (2 if gated else 1), HID
    with ExitStack() as stack:
        m = Pool(nc, stack, layer + "_ex")
        wb = m.sb("w", [P, 2, blob.shape[2]])
        h = m.sb("h", [P, 2, FT, NT])
        sg = m.sb("sg", [P, 2, NT]) if gated else None
        PS = stack.enter_context(nc.psum_tensor(f"{layer}_ex_ps", [P, 8, 512], F32))
        w_in = [m.sem("w_in0"), m.sem("w_in1")]
        h_done, act_done, h_ready, y_done, added = (m.sem(n) for n in ("h_done", "act_done", "h_ready", "y_done", "added"))

        def hidden_bank(n, f):
            return HID * (n % 2) + f if gated else f

        def w1(u, f, d):
            return wb[:, u, (f * KD + d) * P:(f * KD + d + 1) * P]

        def bias(u, f):
            return wb[:, u, W1 + f:W1 + f + 1]

        def w2(u, f):
            return wb[:, u, W1 + BI + f * D:W1 + BI + (f + 1) * D]

        def xt(d, n):
            return XT[:, d, SUB * n:SUB * (n + 1), :].rearrange("p b s -> p (b s)")

        def body(engine, run):
            run(0, 0, True, False)
            run(1, 1, False, False)
            with engine.Fori(1, E // 2 - 1) as j:
                run(2 * j, 0, False, False)
                run(2 * j + 1, 1, False, False)
            run(E - 2, 0, False, False)
            run(E - 1, 1, False, True)

        def known(e):
            return isinstance(e, int)

        def loads_seen(e, u):
            return 8 * (e - u) + 16

        with nc.Block() as block:

            @block.sync
            def _(sp):
                def run(e, u, first, last):
                    if not known(e) or e >= 2:
                        sp.wait_ge(y_done, 2 * UNITS * (e - 1))
                    sp.dma_start(wb[:, u, :], blob[one(e), :, :].rearrange("o p n -> (o p) n")).then_inc(w_in[u], 16)
                body(sp, run)

            @block.tensor
            def _(pe):
                def hidden(e, u, n):
                    g = UNITS * e + n
                    if n == 0:
                        pe.wait_ge(w_in[u], loads_seen(e, u))
                    for f in range(HID):
                        if gated:
                            if not known(e) or g >= 2:
                                pe.wait_ge(act_done if f < FT else h_ready, g - 1)
                        elif not known(e) or g >= 1:
                            pe.wait_ge(h_ready, FT * (g - 1) + f + 1)
                        for d in range(KD):
                            last = nc.tensor.matmul(PS[:, hidden_bank(n, f), :], w1(u, f, d), xt(d, n), start=(d == 0), stop=(d == KD - 1))
                        last.then_inc(h_done, 1)

                def outputs(e, u, n):
                    g = UNITS * e + n
                    pe.wait_ge(h_ready, FT * (g + 1))
                    for s in range(SUB):
                        if s % 2 == 0 and (not known(e) or g >= 2):
                            pe.wait_ge(added, 2 * (g - 2) + s // 2 + 1)
                        for f in range(FT):
                            last = nc.tensor.matmul(PS[:, 4 + 2 * (n % 2) + s // 2, (s % 2) * D:(s % 2 + 1) * D],
                                                    h[:, n % 2, f, s * P:(s + 1) * P], w2(u, f), start=(f == 0), stop=(f == FT - 1))
                        if s % 2:
                            last.then_inc(y_done, 1)

                def run(e, u, first, last):
                    if first:
                        hidden(e, u, 0)
                    for n in range(UNITS):
                        if n < UNITS - 1:
                            hidden(e, u, n + 1)
                        elif not last:
                            hidden(e + 1, 1 - u, 0)
                        outputs(e, u, n)
                body(pe, run)

            @block.scalar
            def _(act):
                def run(e, u, first, last):
                    for n in range(UNITS):
                        g = UNITS * e + n
                        for f in range(FT):
                            act.wait_ge(h_done, HID * g + f + 1)
                            if gated:
                                if not known(e) or g >= 2:
                                    act.wait_ge(h_ready, g - 1)
                                nc.scalar.activation(sg[:, n % 2, :], PS[:, hidden_bank(n, f), :], ACT.Silu, bias=bias(u, f))\
                                  .then_inc(act_done, 1)
                            else:
                                if f == 0 and (not known(e) or g >= 2):
                                    act.wait_ge(y_done, 2 * (g - 1))
                                nc.scalar.activation(h[:, n % 2, f, :], PS[:, hidden_bank(n, f), :], ACT.Gelu, bias=bias(u, f))\
                                  .then_inc(h_ready, 1)
                body(act, run)

            @block.vector
            def _(dve):
                def gate(e, u, n):
                    g = UNITS * e + n
                    dve.wait_ge(h_done, HID * (g + 1))
                    dve.wait_ge(act_done, g + 1)
                    if not known(e) or g >= 2:
                        dve.wait_ge(y_done, 2 * (g - 1))
                    nc.vector.scalar_tensor_tensor(h[:, n % 2, 0, :], PS[:, hidden_bank(n, 1), :], bias(u, 1), sg[:, n % 2, :],
                                                   ALU.add, ALU.mult).then_inc(h_ready, 1)

                def run(e, u, first, last):
                    if gated and first:
                        gate(e, u, 0)
                    for n in range(UNITS):
                        g = UNITS * e + n
                        if gated:
                            if n < UNITS - 1:
                                gate(e, u, n + 1)
                            elif not last:
                                gate(e + 1, 1 - u, 0)
                        for s in range(SUB):
                            b = SUB * n + s
                            if s % 2 == 0:
                                dve.wait_ge(y_done, 2 * g + s // 2 + 1)
                            acc = nc.vector.scalar_tensor_tensor(
                                X[:, b, :], PS[:, 4 + 2 * (n % 2) + s // 2, (s % 2) * D:(s % 2 + 1) * D],
                                combine[:, b, one(e)], X[:, b, :], ALU.mult, ALU.add)
                            if s % 2:
                                acc.then_inc(added, 1)
                body(dve, run)


def mixture(nc, layer, X, ident, router, router_bias, b2, blob, E, F, gated):
    shared = 2 if gated else 0
    with ExitStack() as stack:
        m = Pool(nc, stack, layer)
        mean, rstd = m.sb("mean", [P, B]), m.sb("rstd", [P, B])
        XT = m.sb("XT", [P, KD, B, P])
        logits, combine = m.sb("logits", [P, B, E]), m.sb("combine", [P, B, E + shared])
        rw = m.sb("rw", [P, KD, E])
        rows = b2.shape[0]
        b2_sb = m.sb("b2", [rows, D])
        loads = [(rw[:, :, :], router.rearrange("(k p) e -> p k e", p=P)), (b2_sb[:, :], b2)]
        rb = None
        if router_bias is not None:
            rb = m.sb("rb", [P, E])
            loads.append((rb[:, :], router_bias.partition_broadcast(P)))
        norm_statistics(nc, layer, X, mean, rstd, 1.0, loads)
        norm_and_product(nc, layer, X, ident, mean, rstd, rw, logits, XT=XT, small_bias=rb)
        if gated:
            route_grouped(nc, layer, logits, combine, E, 8, 4, 4)
        else:
            route_top2(nc, layer, logits, combine, E)
        add_product(nc, layer, X, ident, combine, b2_sb, rows)
        experts(nc, layer, X, XT, combine, blob, E + shared, F, gated)


def lora(nc, layer, X, ident, small, small_bias, base, base_bias, loraB, E, R, scaling):
    with ExitStack() as stack:
        m = Pool(nc, stack, layer)
        mean, rstd = m.sb("mean", [P, B]), m.sb("rstd", [P, B])
        sm, bs = m.sb("small", [P, KD, E + R]), m.sb("base", [P, KD, D])
        smb, bsb, lb = m.sb("small_bias", [P, E + R]), m.sb("base_bias", [P, D]), m.sb("loraB", [E * R, D])
        both, gate, gate16 = m.sb("both", [P, B, E + R]), m.sb("gate", [P, B, E]), m.sb("gate16", [P, B, E], BF16)
        top, outer = m.sb("top", [P, B]), m.sb("outer", [P, B, E * R])
        loads = [(sm[:, :, 0:E], small[0].rearrange("(k p) e -> p k e", p=P)),
                 (sm[:, :, E:], small[1].rearrange("(k p) e -> p k e", p=P)),
                 (smb[:, 0:E], small_bias.partition_broadcast(P)),
                 (bs[:, :, :], base.rearrange("(k p) e -> p k e", p=P)),
                 (bsb[:, :], base_bias.partition_broadcast(P)),
                 (lb[:, :], loraB.rearrange("e r n -> (e r) n"))]
        norm_statistics(nc, layer, X, mean, rstd, 1.0, loads, zeros=[smb[:, :]])
        norm_and_product(nc, layer, X, ident, mean, rstd, sm, both, base=bs, small_bias=smb, base_bias=bsb)
        chain, act_ready, e_ready = m.sem("chain"), m.sem("act_ready"), m.sem("e_ready")
        with nc.Block() as block:

            @block.scalar
            def _(act):
                act.wait_ge(act_ready, 1)
                nc.scalar.activation(gate[:, :, :], gate[:, :, :], ACT.Exp).then_inc(e_ready, 1)

            @block.vector
            def _(dve):
                c = Chain(dve, chain)
                c.do(nc.vector.tensor_copy(gate[:, :, :], both[:, :, 0:E]))
                softmax_rows(nc, c, dve, act_ready, e_ready, gate[:, :, :], top[:, :], E)
                c.do(nc.vector.tensor_copy(gate16[:, :, :], gate[:, :, :]))
                c.do(nc.vector.tensor_scalar(gate[:, :, :], gate16[:, :, :], float(scaling), None, ALU.mult))
                for r in range(R):
                    c.do(nc.vector.tensor_tensor(outer[:, :, :].rearrange("p b (e r) -> p b e r", r=R)[:, :, :, r],
                                                 gate[:, :, :], spread(both[:, :, E + r], E), ALU.mult))
        add_product(nc, layer, X, ident, outer, lb, E * R)


MAGIC = 1.5 * 2.0 ** 23
QMAX = 32767.0
WBLOCK, WQMAX = 32, 7.0
SIG = 65536.0


def quantized_ffn(nc, layer, X, ident, w_gate, w_up, w_down, F):
    FT = F // P
    NT = 512
    NN = B * P // NT
    CH = 1024
    NC = FT * B * P // CH
    with ExitStack() as stack:
        m = Pool(nc, stack, layer)
        mean, rstd = m.sb("mean", [P, B]), m.sb("rstd", [P, B])
        G, U = m.sb("G", [P, FT, B * P]), m.sb("U", [P, FT, B * P])
        XQ = m.sb("XQ", [P, KD, B, P])
        wT = [m.sb(f"wT{k}", [P, KD * F]) for k in range(3)]
        big, step, inv = m.sb("big", [P, 5]), m.sb("step", [P, 5]), m.sb("inv", [P, 5])
        part = m.sb("part", [P, 5])
        magic = m.sb("magic", [P, 1])
        found, reduced, scaled, chain = m.sem("found"), m.sem("reduced"), m.sem("scaled"), m.sem("chain")
        RMAX = bass.bass_isa.ReduceOp.absmax

        def all_tokens(pool, k):
            pool.wait_ge(found, k + 1)
            nc.gpsimd.partition_all_reduce(big[:, k:k + 1], part[:, k:k + 1], P, RMAX).then_inc(reduced, 1)

        def steps(dve, c, k, factor):
            dve.wait_ge(reduced, k + 1)
            c.do(nc.vector.tensor_scalar(step[:, k:k + 1], big[:, k:k + 1], factor / QMAX, 1e-12, ALU.mult, ALU.max))
            c.do(nc.vector.reciprocal(inv[:, k:k + 1], step[:, k:k + 1]))
            c.do(nc.vector.tensor_scalar(inv[:, k:k + 1], inv[:, k:k + 1], factor, None, ALU.mult))

        with ExitStack() as early:
            me = Pool(nc, early, layer)
            wn = [me.sb(f"wn{k}", [P, KD * F]) for k in range(3)]
            wa, wi = me.sb("wa", [P, KD * F // WBLOCK]), me.sb("wi", [P, KD * F // WBLOCK])
            XN = me.sb("XN", [P, B, D])
            xq = me.sb("xq", [P, 2, D])
            loads = [(wn[0][:, :].rearrange("p (t n) -> p t n", t=FT), w_gate.rearrange("(t p) n -> p t n", p=P)),
                     (wn[1][:, :].rearrange("p (t n) -> p t n", t=FT), w_up.rearrange("(t p) n -> p t n", p=P)),
                     (wn[2][:, :].rearrange("p (t n) -> p t n", t=KD), w_down.rearrange("(t p) n -> p t n", p=P))]
            norm_statistics(nc, layer, X, mean, rstd, 1.0, loads)

            PS = early.enter_context(nc.psum_tensor(f"{layer}_q_ps", [P, 8, 512], F32))
            normed, w_ready, wt_done, wt_copied = me.sem("normed"), me.sem("w_ready"), me.sem("wt_done"), me.sem("wt_copied")
            rounded, x_done, x_copied = me.sem("rounded"), me.sem("x_done"), me.sem("x_copied")
            with nc.Block() as block:

                @block.gpsimd
                def _(pool):
                    nc.gpsimd.memset(magic[:, :], MAGIC)
                    all_tokens(pool, 0)

                @block.vector
                def _(dve):
                    c = Chain(dve, chain)
                    with dve.Fori(0, B) as b:
                        nc.vector.tensor_scalar(row(XN, b), row(X, b), col(mean, b), col(rstd, b), ALU.subtract, ALU.mult)\
                          .then_inc(normed, 1)
                    dve.wait_ge(normed, B)
                    nc.vector.tensor_reduce(part[:, 0:1], XN[:, :, :].rearrange("p b d -> p (b d)"), AXIS.X, ALU.max,
                                            apply_absolute_value=True).then_inc(found, 1)
                    for k in range(3):
                        w = wn[k][:, :].rearrange("p (a n) -> p a n", n=WBLOCK)
                        NB = KD * F // WBLOCK
                        if k:
                            dve.wait_ge(w_ready, k)
                        c.do(nc.vector.tensor_reduce(wa[:, :], w, AXIS.X, ALU.max, apply_absolute_value=True))
                        c.do(nc.vector.tensor_scalar(wa[:, :], wa[:, :], 1.0 / WQMAX, 1e-12, ALU.mult, ALU.max))
                        c.do(nc.vector.reciprocal(wi[:, :], wa[:, :]))
                        c.do(nc.vector.tensor_tensor(w, w, wi[:, :].unsqueeze(2).to_broadcast([P, NB, WBLOCK]), ALU.mult))
                        c.do(nc.vector.tensor_scalar(w, w, MAGIC, MAGIC, ALU.add, ALU.subtract))
                        c.do(nc.vector.tensor_scalar(w, w, -WQMAX - 1.0, WQMAX, ALU.max, ALU.min))
                        nc.vector.tensor_tensor(w, w, wa[:, :].unsqueeze(2).to_broadcast([P, NB, WBLOCK]), ALU.mult).then_inc(w_ready, 1)
                    steps(dve, c, 0, 1.0)

                @block.tensor
                def _(pe):
                    for k in range(3):
                        pe.wait_ge(w_ready, k + 1)
                        for q in range(KD * FT):
                            g = 3 * k + q // 4
                            if q % 4 == 0 and g >= 8:
                                pe.wait_ge(wt_copied, g - 7)
                            if k < 2:
                                d, f = divmod(q, FT)
                                src = wn[k][:, f * D + d * P:f * D + (d + 1) * P]
                            else:
                                f, o = divmod(q, KD)
                                src = wn[k][:, o * F + f * P:o * F + (f + 1) * P]
                            t = nc.tensor.transpose(PS[:, g % 8, (q % 4) * P:(q % 4 + 1) * P], src, ident[:, :])
                            if q % 4 == 3:
                                t.then_inc(wt_done, 1)

                @block.scalar
                def _(act):
                    for g in range(9):
                        act.wait_ge(wt_done, g + 1)
                        nc.scalar.activation(wT[g // 3][:, (g % 3) * 512:(g % 3 + 1) * 512], PS[:, g % 8, :], ACT.Copy).then_inc(wt_copied, 1)

            with nc.Block() as block:

                @block.vector
                def _(dve):
                    def run(i, u):
                        if not isinstance(i, int):
                            dve.wait_ge(x_done, i - 1)
                        nc.vector.tensor_scalar(row(XN, i), row(XN, i), inv[:, 0:1], MAGIC, ALU.mult, ALU.add).then_inc(rounded, 1)
                        dve.wait_ge(rounded, 3 * i + 1)
                        nc.vector.tensor_scalar(xq[:, u, :], row(XN, i), MAGIC + QMAX, MAGIC - QMAX - 1.0, ALU.min, ALU.max).then_inc(rounded, 1)
                        dve.wait_ge(rounded, 3 * i + 2)
                        nc.vector.tensor_scalar(xq[:, u, :], xq[:, u, :], MAGIC, None, ALU.subtract).then_inc(rounded, 1)
                    run(0, 0)
                    run(1, 1)
                    with dve.Fori(1, B // 2) as j:
                        run(2 * j, 0)
                        run(2 * j + 1, 1)

                @block.tensor
                def _(pe):
                    def run(i, u):
                        pe.wait_ge(rounded, 3 * i + 3)
                        if not isinstance(i, int):
                            pe.wait_ge(x_copied, i - 1)
                        for d in range(KD):
                            last = nc.tensor.transpose(PS[:, u, d * P:(d + 1) * P], xq[:, u, d * P:(d + 1) * P], ident[:, :])
                        last.then_inc(x_done, 1)
                    run(0, 0)
                    run(1, 1)
                    with pe.Fori(1, B // 2) as j:
                        run(2 * j, 0)
                        run(2 * j + 1, 1)

                @block.gpsimd
                def _(pool):
                    pool.nop()

                @block.scalar
                def _(act):
                    for i in range(B):
                        act.wait_ge(x_done, i + 1)
                        nc.scalar.activation(XQ[:, :, i, :], PS[:, i % 2, 0:D].rearrange("p (k s) -> p k s", k=KD), ACT.Copy)\
                          .then_inc(x_copied, 1)

        with ExitStack() as middle:
            mm = Pool(nc, middle, layer)
            BANKS = 6
            PS = middle.enter_context(nc.psum_tensor(f"{layer}_m_ps", [P, 8, 512], F32))
            am, am_all = mm.sb("am", [P, 2, FT]), mm.sb("am_all", [P, 2, FT])
            p_done, p_read, am_done, am_kept = mm.sem("p_done"), mm.sem("p_read"), mm.sem("am_done"), mm.sem("am_kept")
            PER = 2 * FT
            with nc.Block() as block:

                @block.tensor
                def _(pe):
                    def run(n):
                        for q in range(PER):
                            k, f = divmod(q, FT)
                            if not isinstance(n, int) or q >= BANKS:
                                pe.wait_ge(p_read, PER * n + q - BANKS + 1)
                            for d in range(KD):
                                rhs = XQ[:, d, bass.ds(n * (NT // P), NT // P), :].rearrange("p b s -> p (b s)")
                                last = nc.tensor.matmul(PS[:, q % BANKS, :], wT[k][:, d * F + f * P:d * F + (f + 1) * P], rhs,
                                                        start=(d == 0), stop=(d == KD - 1))
                            last.then_inc(p_done, 1)
                    run(0)
                    with pe.Fori(1, NN) as n:
                        run(n)

                @block.vector
                def _(dve):
                    def run(n):
                        for q in range(PER):
                            k, f = divmod(q, FT)
                            dst = (G, U)[k]
                            dve.wait_ge(p_done, PER * n + q + 1)
                            if q == 0 and not isinstance(n, int):
                                dve.wait_ge(am_kept, n)
                            nc.vector.tensor_reduce(am[:, k, f:f + 1], PS[:, q % BANKS, :], AXIS.X, ALU.max,
                                                    apply_absolute_value=True).then_inc(am_done, 1)
                            nc.vector.tensor_scalar(dst[:, f, bass.ds(n * NT, NT)], PS[:, q % BANKS, :], step[:, 0:1], None, ALU.mult)\
                              .then_inc(p_read, 1)
                        dve.wait_ge(am_done, PER * n + PER)
                        if isinstance(n, int):
                            nc.vector.tensor_copy(am_all[:, :, :], am[:, :, :]).then_inc(am_kept, 1)
                        else:
                            nc.vector.tensor_tensor(am_all[:, :, :], am_all[:, :, :], am[:, :, :], ALU.max).then_inc(am_kept, 1)
                    run(0)
                    with dve.Fori(1, NN) as n:
                        run(n)
                    c = Chain(dve, mm.sem("chain1"))
                    dve.wait_ge(am_kept, NN)
                    c.do(nc.vector.tensor_reduce(part[:, 1:3], am_all[:, :, :], AXIS.X, ALU.max))
                    for k in range(2):
                        nc.vector.tensor_scalar(part[:, 1 + k:2 + k], part[:, 1 + k:2 + k], step[:, 0:1], None, ALU.mult).then_inc(found, 1)
                    steps(dve, c, 1, 1.0)
                    steps(dve, c, 2, 1.0)

                @block.gpsimd
                def _(pool):
                    all_tokens(pool, 1)
                    all_tokens(pool, 2)

        def chunk(t, i):
            return t[:, :, :].rearrange("p f s -> p (f s)")[:, bass.ds(i * CH, CH)]

        with ExitStack() as late:
            ml = Pool(nc, late, layer)
            gq, sg = ml.sb("gq", [P, 2, CH]), ml.sb("sg", [P, 2, CH])
            on_grid, clipped, q_ready, sg_ready, sg_clipped, prod = (ml.sem(n) for n in ("on_grid", "clipped", "q_ready", "sg_ready", "sg_clipped", "prod"))
            with nc.Block() as block:

                @block.scalar
                def _(act):
                    with act.Fori(0, NC) as i:
                        nc.scalar.activation(chunk(G, i), chunk(G, i), ACT.Identity, bias=magic[:, :], scale=inv[:, 1:2]).then_inc(on_grid, 1)

                    def run(i, u):
                        act.wait_ge(q_ready, i + 1)
                        if not isinstance(i, int):
                            act.wait_ge(prod, i - 1)
                        nc.scalar.activation(sg[:, u, :], gq[:, u, :], ACT.Sigmoid, scale=step[:, 1:2]).then_inc(sg_ready, 1)
                        act.wait_ge(sg_ready, 2 * i + 1)
                        nc.scalar.activation(sg[:, u, :], sg[:, u, :], ACT.Identity, bias=magic[:, :], scale=SIG).then_inc(sg_ready, 1)
                    run(0, 0)
                    run(1, 1)
                    with act.Fori(1, NC // 2) as j:
                        run(2 * j, 0)
                        run(2 * j + 1, 1)
                    with act.Fori(0, NC) as i:
                        nc.scalar.activation(chunk(U, i), chunk(U, i), ACT.Identity, bias=magic[:, :], scale=inv[:, 2:3]).then_inc(on_grid, 1)

                @block.vector
                def _(dve):
                    def to_integers(i, u):
                        if not isinstance(i, int):
                            dve.wait_ge(prod, i - 1)
                        dve.wait_ge(on_grid, i + 1)
                        nc.vector.tensor_scalar(gq[:, u, :], chunk(G, i), MAGIC + QMAX, MAGIC - QMAX - 1.0, ALU.min, ALU.max)\
                          .then_inc(clipped, 1)
                        dve.wait_ge(clipped, i + 1)
                        nc.vector.tensor_scalar(gq[:, u, :], gq[:, u, :], MAGIC, None, ALU.subtract).then_inc(q_ready, 1)

                    def product(i, u):
                        dve.wait_ge(sg_ready, 2 * i + 2)
                        nc.vector.tensor_scalar(sg[:, u, :], sg[:, u, :], MAGIC + SIG - 1.0, MAGIC, ALU.min, ALU.max).then_inc(sg_clipped, 1)
                        dve.wait_ge(sg_clipped, i + 1)
                        nc.vector.scalar_tensor_tensor(chunk(G, i), sg[:, u, :], MAGIC, gq[:, u, :], ALU.subtract, ALU.mult).then_inc(prod, 1)
                    to_integers(0, 0)
                    to_integers(1, 1)
                    with dve.Fori(1, NC // 2) as j:
                        product(2 * j - 2, 0)
                        to_integers(2 * j, 0)
                        product(2 * j - 1, 1)
                        to_integers(2 * j + 1, 1)
                    product(NC - 2, 0)
                    product(NC - 1, 1)
                    dve.wait_ge(prod, NC)
                    c = Chain(dve, ml.sem("chain3"))
                    c.do(nc.vector.tensor_reduce(part[:, 3:4], G[:, :, :].rearrange("p f s -> p (f s)"), AXIS.X, ALU.max,
                                                 apply_absolute_value=True))
                    nc.vector.tensor_scalar(part[:, 3:4], part[:, 3:4], step[:, 1:2], None, ALU.mult).then_inc(found, 1)
                    steps(dve, c, 3, 1.0 / SIG)
                    c.do(nc.vector.tensor_tensor(inv[:, 3:4], inv[:, 3:4], step[:, 1:2], ALU.mult))

                @block.gpsimd
                def _(pool):
                    all_tokens(pool, 3)

            grid2, low2, int2, up2, prod2 = (ml.sem(n) for n in ("grid2", "low2", "int2", "up2", "prod2"))
            with nc.Block() as block:

                @block.scalar
                def _(act):
                    with act.Fori(0, NC) as i:
                        nc.scalar.activation(chunk(G, i), chunk(G, i), ACT.Identity, bias=magic[:, :], scale=inv[:, 3:4]).then_inc(grid2, 1)

                @block.vector
                def _(dve):
                    with dve.Fori(0, NC) as i:
                        nc.vector.tensor_scalar(chunk(U, i), chunk(U, i), MAGIC + QMAX, MAGIC - QMAX - 1.0, ALU.min, ALU.max).then_inc(up2, 1)
                        dve.wait_ge(grid2, i + 1)
                        nc.vector.tensor_scalar(chunk(G, i), chunk(G, i), MAGIC + QMAX, MAGIC - QMAX - 1.0, ALU.min, ALU.max).then_inc(low2, 1)
                        dve.wait_ge(low2, i + 1)
                        nc.vector.tensor_scalar(chunk(G, i), chunk(G, i), MAGIC, None, ALU.subtract).then_inc(int2, 1)
                        dve.wait_ge(up2, i + 1)
                        dve.wait_ge(int2, i + 1)
                        nc.vector.scalar_tensor_tensor(chunk(G, i), chunk(U, i), MAGIC, chunk(G, i), ALU.subtract, ALU.mult).then_inc(prod2, 1)
                    dve.wait_ge(prod2, NC)
                    c = Chain(dve, ml.sem("chain2"))
                    c.do(nc.vector.tensor_reduce(part[:, 4:5], G[:, :, :].rearrange("p f s -> p (f s)"), AXIS.X, ALU.max,
                                                 apply_absolute_value=True))
                    c.do(nc.vector.tensor_tensor(part[:, 3:4], step[:, 2:3], step[:, 3:4], ALU.mult))
                    nc.vector.tensor_tensor(part[:, 4:5], part[:, 4:5], part[:, 3:4], ALU.mult).then_inc(found, 1)
                    steps(dve, c, 4, 1.0)
                    c.do(nc.vector.tensor_tensor(inv[:, 4:5], inv[:, 4:5], part[:, 3:4], ALU.mult))

                @block.gpsimd
                def _(pool):
                    all_tokens(pool, 4)

            PS = late.enter_context(nc.psum_tensor(f"{layer}_d_ps", [P, 8, 512], F32))
            ob = ml.sb("ob", [P, 2, FT, P])
            grid3, low3, int3, d_done, d_added = (ml.sem(n) for n in ("grid3", "low3", "int3", "d_done", "d_added"))

            def tokens(t, i):
                return t[:, :, bass.ds(i * P, P)]

            with nc.Block() as block:

                @block.scalar
                def _(act):
                    with act.Fori(0, B) as i:
                        nc.scalar.activation(tokens(G, i), tokens(G, i), ACT.Identity, bias=magic[:, :], scale=inv[:, 4:5]).then_inc(grid3, 1)

                @block.vector
                def _(dve):
                    def integers(i, u):
                        if not isinstance(i, int):
                            dve.wait_ge(d_done, i - 1)
                        dve.wait_ge(grid3, i + 1)
                        nc.vector.tensor_scalar(ob[:, u, :, :], tokens(G, i), MAGIC + QMAX, MAGIC - QMAX - 1.0, ALU.min, ALU.max)\
                          .then_inc(low3, 1)
                        dve.wait_ge(low3, i + 1)
                        nc.vector.tensor_scalar(ob[:, u, :, :], ob[:, u, :, :], MAGIC, None, ALU.subtract).then_inc(int3, 1)

                    def add(i, u):
                        dve.wait_ge(d_done, i + 1)
                        nc.vector.scalar_tensor_tensor(row(X, i), PS[:, u, 0:D], step[:, 4:5], row(X, i), ALU.mult, ALU.add)\
                          .then_inc(d_added, 1)
                    integers(0, 0)
                    integers(1, 1)
                    with dve.Fori(1, B // 2) as j:
                        add(2 * j - 2, 0)
                        integers(2 * j, 0)
                        add(2 * j - 1, 1)
                        integers(2 * j + 1, 1)
                    add(B - 2, 0)
                    add(B - 1, 1)

                @block.tensor
                def _(pe):
                    def run(i, u):
                        pe.wait_ge(int3, i + 1)
                        if not isinstance(i, int):
                            pe.wait_ge(d_added, i - 1)
                        for f in range(FT):
                            last = nc.tensor.matmul(PS[:, u, 0:D], ob[:, u, f, :], wT[2][:, f * D:(f + 1) * D], start=(f == 0), stop=(f == FT - 1))
                        last.then_inc(d_done, 1)
                    run(0, 0)
                    run(1, 1)
                    with pe.Fori(1, B // 2) as j:
                        run(2 * j, 0)
                        run(2 * j + 1, 1)
def program(nc, a, out):
    with ExitStack() as stack:
        X = stack.enter_context(nc.sbuf_tensor("X", [P, B, D], F32))
        ident = stack.enter_context(nc.sbuf_tensor("ident", [P, P], F32))
        below = stack.enter_context(nc.sbuf_tensor("below", [P, P], F32))
        parity = stack.enter_context(nc.sbuf_tensor("parity", [P, 2], F32))
        constants(nc, a["x"], a["parity"], X, ident, below, parity)
        ctx, ctxT = a["ctx"], a["ctxT"]
        attention(nc, "a0", X, ident, below, parity, ctx, ctxT, 1 / 16, "int_qk", a["mask_qk"], wo=a["L0_woT"], bo=a["L0_bo"])
        mixture(nc, "f0", X, ident, a["L0_router"], None, a["L0_b2"], a["L0_blob"], 8, 512, False)
        attention(nc, "a1", X, ident, below, parity, ctx, ctxT, 1 / 4, "inverted", (a["mask_bool"], a["mask_boolT"]))
        quantized_ffn(nc, "f1", X, ident, a["L1_gate"], a["L1_up"], a["L1_down"], 768)
        attention(nc, "a2", X, ident, below, parity, ctx, ctxT, 1 / 4, "causal", wq=a["L2_wq"], bq=a["L2_bq_heads"], wk=a["L2_wq"], bk=a["L2_bq_heads"],
                  wv=a["L2_wq"], bv=a["L2_bq"], wo=a["L2_wo"], bo=a["L2_bo"])
        lora(nc, "f2", X, ident, (a["L2_router"], a["L2_loraA"]), a["L2_router_b"], a["L2_base"], a["L2_base_b"], a["L2_loraB"], 8, 8, 2.0)
        attention(nc, "a3", X, ident, below, parity, ctx, ctxT, 1 / 4, "int_k", a["mask_k"], wq=a["L3_wq"], bq=a["L3_bq_heads"], wk=a["L3_wk"],
                  bk=a["L3_bk_heads"], wv=a["L3_wv"], bv=a["L3_bv"], wo=a["L3_wo"], bo=a["L3_bo"])
        mixture(nc, "f3", X, ident, a["L3_gw"], a["L3_gb"], a["L3_b2"], a["L3_blob"], 32, 128, True)
        store(nc, X, out)


def blob_of(ins, biases, w2):
    E, F, _ = w2.shape
    parts = [np.transpose(np.asarray(w).reshape(E, KD, P, F // P, P), (0, 2, 3, 1, 4)).reshape(E, P, KD * F) for w in ins]
    parts += [np.transpose(np.asarray(b).reshape(E, F // P, P), (0, 2, 1)) for b in biases]
    parts.append(np.transpose(np.asarray(w2).reshape(E, F // P, P, D), (0, 2, 1, 3)).reshape(E, P, F // P * D))
    return np.concatenate(parts, axis=2)


def by_tile(b):
    return np.transpose(np.asarray(b).reshape(KD, P))


def with_shared(routed, shared, axis):
    halves = np.split(np.asarray(shared), 2, axis=axis - 1)
    return np.concatenate([routed, np.stack(halves)])


def kernel(x, ctx_1024, mask_Bx1xSxS2_ik1, mask_BxS2_bf1, mask_Bx1x1xS2_ik0, **w):
    import concourse.bacc as bacc
    from concourse.bass_utils import run_bass_kernel_spmd

    laid = {
        "x": x, "ctx": ctx_1024, "ctxT": np.transpose(ctx_1024, (0, 2, 1)),
        "parity": np.stack([(np.arange(P) // DH) % 2 == e for e in range(2)], 1).astype(np.float32),
        "mask_qk": mask_Bx1xSxS2_ik1, "mask_k": mask_Bx1x1xS2_ik0,
        "mask_bool": np.ascontiguousarray(mask_BxS2_bf1).view(np.uint8),
        "mask_boolT": np.ascontiguousarray(np.transpose(mask_BxS2_bf1)).view(np.uint8),
        "L0_woT": np.transpose(w["L0_xattn_W_out"]), "L0_bo": w["L0_xattn_b_out"],
        "L1_gate": w["L1_ffn_w_gate"], "L1_up": w["L1_ffn_w_up"], "L1_down": w["L1_ffn_w_down"],
        "L2_wq": w["L2_xattn_Wq"], "L2_bq": w["L2_xattn_bq"], "L2_wo": w["L2_xattn_Wo"], "L2_bo": w["L2_xattn_bo"],
        "L2_base": np.transpose(w["L2_ffn_base_w"]), "L2_base_b": w["L2_ffn_base_b"], "L2_loraA": w["L2_ffn_lora_A"],
        "L2_loraB": w["L2_ffn_lora_B"], "L2_router": np.transpose(w["L2_ffn_router_w"]), "L2_router_b": w["L2_ffn_router_b"],
        "L3_wq": w["L3_xattn_Wq"], "L3_bq_heads": by_tile(w["L3_xattn_bq"]), "L3_wk": w["L3_xattn_Wk"],
        "L3_bk_heads": by_tile(w["L3_xattn_bk"]), "L2_bq_heads": by_tile(w["L2_xattn_bq"]),
        "L3_wv": w["L3_xattn_Wv"], "L3_bv": w["L3_xattn_bv"], "L3_wo": w["L3_xattn_Wo"], "L3_bo": w["L3_xattn_bo"],
        "L3_gw": w["L3_ffn_gw"], "L3_gb": w["L3_ffn_gb"],
        "L3_b2": np.concatenate([w["L3_ffn_b2"], np.reshape(w["L3_ffn_sb2"], (1, D))]),
        "L3_blob": blob_of([with_shared(w["L3_ffn_w1"], w["L3_ffn_sw1"], 2), with_shared(w["L3_ffn_w3"], w["L3_ffn_sw3"], 2)],
                           [with_shared(w["L3_ffn_b1"], w["L3_ffn_sb1"], 1), with_shared(w["L3_ffn_b3"], w["L3_ffn_sb3"], 1)],
                           with_shared(w["L3_ffn_w2"], w["L3_ffn_sw2"], 1)),
        "L0_router": np.transpose(w["L0_ffn_router_w"]), "L0_b2": w["L0_ffn_b2"],
        "L0_blob": blob_of([np.transpose(w["L0_ffn_w1"], (0, 2, 1))], [w["L0_ffn_b1"]], np.transpose(w["L0_ffn_w2"], (0, 2, 1))),
    }
    nc = bacc.Bacc("TRN2", target_bir_lowering=False, num_devices=1)
    arrays, aps = {}, {}
    for name, value in laid.items():
        value = np.ascontiguousarray(value)
        arrays[f"in_{name}"] = value
        aps[name] = nc.dram_tensor(f"in_{name}", value.shape, mybir.dt.from_np(value.dtype), kind="ExternalInput").ap()
    out = nc.dram_tensor("out", x.shape, F32, kind="ExternalOutput").ap()
    program(nc, aps, out)
    return run_bass_kernel_spmd(nc, [arrays], core_ids=[0]).results[0]["out"]
```

```python
import numpy as np
from contextlib import ExitStack

import concourse.bass as bass
from concourse import mybir

F32 = mybir.dt.float32
I32 = mybir.dt.int32
U32 = mybir.dt.uint32
U8 = mybir.dt.uint8
BF16 = mybir.dt.bfloat16
F16 = mybir.dt.float16
ALU = mybir.AluOpType
ACT = mybir.ActivationFunctionType
AXIS = mybir.AxisListType

B, S, D = 16, 128, 256
P = 128
KD = D // P
H, DH = 16, 16
HT = P // DH
T4 = 4
HP = P // T4
EPS = 1e-5
MAGIC = 1.5 * 2.0 ** 23
MASKED = -1e30


def one(i):
    return bass.ds(i, 1)


def row(t, i):
    return t[:, one(i), :].rearrange("p o d -> p (o d)")


def col(t, i):
    return t[:, one(i)]


class Chain:

    def __init__(self, eng, sem):
        self.eng, self.sem, self.n = eng, sem, 0

    def do(self, ins):
        self.n += 1
        ins.then_inc(self.sem, 1)
        self.eng.wait_ge(self.sem, self.n)


class Pool:

    def __init__(self, nc, stack, layer):
        self.nc, self.stack, self.layer, self.sems = nc, stack, layer, []
        stack.callback(self.clear)

    def sb(self, name, shape, dtype=F32):
        return self.stack.enter_context(self.nc.sbuf_tensor(f"{self.layer}_{name}", shape, dtype))

    def sem(self, name):
        self.sems.append(self.stack.enter_context(self.nc.semaphore(f"{self.layer}_{name}")))
        return self.sems[-1]

    def clear(self):
        if self.sems:
            with self.nc.Block() as block:

                @block.gpsimd
                def _(pool):
                    for s in self.sems:
                        pool.sem_clear(s)


def constants(nc, x_dram, parity_dram, X, ident, below, parity):
    with ExitStack() as stack:
        m = Pool(nc, stack, "const")
        loaded, filled, made = m.sem("loaded"), m.sem("filled"), m.sem("made")
        with nc.Block() as block:

            @block.sync
            def _(sp):
                sp.dma_start(X[:, :, :], x_dram.rearrange("b p d -> p b d")).then_inc(loaded, 16)
                sp.dma_start(parity[:, :], parity_dram).then_inc(loaded, 16)
                sp.wait_ge(loaded, 32)

            @block.gpsimd
            def _(pool):
                nc.gpsimd.memset(ident[:, :], 1.0).then_inc(filled, 1)
                nc.gpsimd.memset(below[:, :], 1.0).then_inc(filled, 1)
                pool.wait_ge(filled, 2)
                nc.gpsimd.affine_select(out=ident[:, :], in_=ident[:, :], compare_op=ALU.is_equal, fill=0.0,
                                        base=0, pattern=[[-1, P]], channel_multiplier=1).then_inc(made, 1)
                nc.gpsimd.affine_select(out=below[:, :], in_=below[:, :], compare_op=ALU.is_ge, fill=0.0,
                                        base=0, pattern=[[-1, P]], channel_multiplier=1).then_inc(made, 1)
                pool.wait_ge(made, 2)


def norm_statistics(nc, layer, X, mean, rstd, scale, loads, zeros=(), ones=()):
    with ExitStack() as stack:
        m = Pool(nc, stack, layer + "_stats")
        raw = m.sb("raw", [P, B, 6])
        t = [m.sb(f"t{k}", [P, B]) for k in range(5)]
        halves, chain, var_ready, root_ready = (m.sem(n) for n in ("halves", "chain", "var_ready", "root_ready"))
        filled, loaded = m.sem("filled"), m.sem("loaded")
        even, odd = raw[:, :, 0:3], raw[:, :, 3:6]
        with nc.Block() as block:

            @block.gpsimd
            def _(pool):
                for z in zeros:
                    nc.gpsimd.memset(z, 0.0).then_inc(filled, 1)
                for z in ones:
                    nc.gpsimd.memset(z, 1.0).then_inc(filled, 1)
                if zeros or ones:
                    pool.wait_ge(filled, len(zeros) + len(ones))

            @block.sync
            def _(sp):
                if zeros or ones:
                    sp.wait_ge(filled, len(zeros) + len(ones))
                for dst, src in loads:
                    sp.dma_start(dst, src).then_inc(loaded, 16)
                if loads:
                    sp.wait_ge(loaded, 16 * len(loads))

            @block.vector
            def _(dve):
                with dve.Fori(0, B // 8) as j:
                    for k in range(8):
                        nc.vector.bn_stats(out=row(raw, 8 * j + k), in_=row(X, 8 * j + k)).then_inc(halves, 1)
                dve.wait_ge(halves, B)
                c = Chain(dve, chain)
                me, mo = even[:, :, 1:2].rearrange("p b o -> p (b o)"), odd[:, :, 1:2].rearrange("p b o -> p (b o)")
                ve, vo = even[:, :, 2:3].rearrange("p b o -> p (b o)"), odd[:, :, 2:3].rearrange("p b o -> p (b o)")
                c.do(nc.vector.tensor_tensor(t[0][:, :], me, mo, ALU.add))
                c.do(nc.vector.tensor_tensor(t[1][:, :], me, mo, ALU.subtract))
                c.do(nc.vector.tensor_scalar(mean[:, :], t[0][:, :], 0.5, None, ALU.mult))
                c.do(nc.vector.tensor_tensor(t[2][:, :], ve, vo, ALU.add))
                c.do(nc.vector.scalar_tensor_tensor(t[3][:, :], t[1][:, :], 0.25, t[1][:, :], ALU.mult, ALU.mult))
                c.do(nc.vector.scalar_tensor_tensor(t[0][:, :], t[2][:, :], 1.0 / D, t[3][:, :], ALU.mult, ALU.add))
                nc.vector.tensor_scalar(t[1][:, :], t[0][:, :], EPS, None, ALU.add).then_inc(var_ready, 1)
                dve.wait_ge(root_ready, 1)
                c.do(nc.vector.reciprocal(t[3][:, :], t[2][:, :]))
                c.do(nc.vector.tensor_tensor(t[0][:, :], t[3][:, :], t[3][:, :], ALU.mult))
                c.do(nc.vector.tensor_tensor(t[4][:, :], t[0][:, :], t[1][:, :], ALU.mult))
                c.do(nc.vector.tensor_scalar(t[0][:, :], t[4][:, :], -0.5, 1.5, ALU.mult, ALU.add))
                c.do(nc.vector.scalar_tensor_tensor(rstd[:, :], t[3][:, :], float(scale), t[0][:, :], ALU.mult, ALU.mult))

            @block.scalar
            def _(act):
                act.wait_ge(var_ready, 1)
                nc.scalar.activation(t[2][:, :], t[1][:, :], ACT.Sqrt).then_inc(root_ready, 1)


def attention(nc, layer, X, ident, below, parity, ctx, ctxT, scale, mask_kind, mask=None, wq=None, bq=None, wk=None,
              bk=None, wv=None, bv=None, wo=None, bo=None):
    proj = wq is not None
    oproj = wo is not None
    with ExitStack() as stack:
        m = Pool(nc, stack, layer)
        mean, rstd = m.sb("mean", [P, B]), m.sb("rstd", [P, B])
        xn = m.sb("xn", [P, 2, D])
        xo = m.sb("xo", [P, 2, 2 * KD, P])
        kM = m.sb("kM", [P, 2, KD, HT, P])
        vraw = m.sb("vraw", [P, 2, D])
        vx = m.sb("vx", [P, 2, H, DH + 1])
        NB = 1 if mask_kind == "causal" else B
        bias = m.sb("bias", [P, NB, P])
        t_sb, p_sb = m.sb("t", [P, T4, T4 * P]), m.sb("p", [P, T4, T4 * P])
        mx = m.sb("mx", [P, T4, T4])
        pT = m.sb("pT", [P, 2, T4, P])
        rec, o_n = m.sb("rec", [P, H]), m.sb("o_n", [P, D])
        loads, zeros, ones = [], [kM[:, :, :, :, :]], [vx[:, :, :, DH:DH + 1]]
        if oproj:
            wo_sb = m.sb("wo", [P, KD, D])
            bo_sb = m.sb("bo", [P, D])
            loads += [(wo_sb[:, :, :], wo.rearrange("(k p) n -> p k n", p=P)), (bo_sb[:, :], bo.partition_broadcast(P))]
        if proj:
            qT, cT = m.sb("qT", [P, 2, KD, P]), m.sb("cT", [P, 2, KD, P])
            wq_sb, wk_sb, wv_sb = m.sb("wq", [P, KD, D]), m.sb("wk", [P, KD, D]), m.sb("wv", [P, KD, D])
            bv_sb = m.sb("bv", [P, D])
            bq_sb, bk_sb, bqs, bkm = m.sb("bq", [P, KD]), m.sb("bk", [P, KD]), m.sb("bqs", [P, KD]), m.sb("bkm", [P, KD, 2])
            loads += [(w_sb[:, :, :], w.rearrange("(k p) n -> p k n", p=P)) for w_sb, w in ((wq_sb, wq), (wk_sb, wk), (wv_sb, wv))]
            loads += [(bq_sb[:, :], bq), (bk_sb[:, :], bk), (bv_sb[:, :], bv.partition_broadcast(P))]
        if mask_kind == "int_qk":
            mask_in = m.sb("mask_in", [P, B, P], I32)
            loads.append((mask_in[:, :, :], mask.rearrange("b o q k -> (o q) b k")))
        elif mask_kind == "int_k":
            mask_in = m.sb("mask_in", [P, B, P], I32)
            loads.append((mask_in[:, :, :].rearrange("p b k -> p (b k)"), mask.rearrange("b x y k -> (x y b k)").partition_broadcast(P)))
        elif mask_kind == "inverted":
            mask_in, mask_q = m.sb("mask_in", [P, B, P], U8), m.sb("mask_q", [P, B], U8)
            qm = m.sb("qm", [P, B])
            inv = m.sb("inv", [P, P])
            loads += [(mask_in[:, :, :].rearrange("p b k -> p (b k)"), mask[0].rearrange("b k -> (b k)").partition_broadcast(P)),
                      (mask_q[:, :], mask[1])]
        norm_statistics(nc, layer, X, mean, rstd, 1.0 if proj else scale, loads, zeros, ones)

        PS = stack.enter_context(nc.psum_tensor(f"{layer}_ps", [P, 8, 512], F32))
        ps_s = PS[:, 0:4, :]
        ps_t = [PS[:, 4, :], PS[:, 5, :]]
        ps_v = PS[:, 6, 0:H * (DH + 1)].rearrange("p (h d) -> p h d", h=H)
        ps_q = PS[:, 7, :].rearrange("p (t s) -> p t s", t=2 * KD)
        half_b = PS[:, 7, D:2 * D]

        prepared = m.sem("prepared")
        ctx_in = [m.sem("ctx_in0"), m.sem("ctx_in1")]
        xn_ready, xo_done, xo_copied = m.sem("xn_ready"), m.sem("xo_done"), m.sem("xo_copied")
        kv_done, qo_done = m.sem("kv_done"), m.sem("qo_done")
        q_ready, k_ready_low, k_ready, v_ready = (m.sem(n) for n in ("q_ready", "k_ready_low", "k_ready", "v_ready"))
        s_done, biased, maxed, shifted, exped = (m.sem(n) for n in ("s_done", "biased", "maxed", "shifted", "exped"))
        pT_done, pT_copied, av_done, inverted, normed = (m.sem(n) for n in ("pT_done", "pT_copied", "av_done", "inverted", "normed"))
        bo_added, resid_done = m.sem("bo_added"), m.sem("resid_done")
        DMAS = KD if proj else HT + 1
        LAST = B - 1
        SHARE = 3

        with nc.Block() as block:

            @block.vector
            def _(dve):
                c = Chain(dve, prepared)
                if mask_kind in ("int_qk", "int_k"):
                    c.do(nc.vector.tensor_scalar(bias[:, :, :], mask_in[:, :, :], 0.0, MASKED, ALU.is_equal, ALU.mult))
                elif mask_kind == "causal":
                    c.do(nc.vector.tensor_scalar(bias[:, 0, :], below[:, :], 0.0, MASKED, ALU.is_equal, ALU.mult))
                else:
                    c.do(nc.vector.tensor_scalar(inv[:, :], below[:, :], -999999.0, None, ALU.mult))
                    c.do(nc.vector.tensor_tensor(bias[:, :, :], mask_in[:, :, :], inv[:, :].unsqueeze(1).to_broadcast([P, B, P]), ALU.mult))
                    c.do(nc.vector.tensor_copy(qm[:, :], mask_q[:, :]))
                if proj:
                    c.do(nc.vector.tensor_scalar(bqs[:, :], bq_sb[:, :], scale, None, ALU.mult))
                    c.do(nc.vector.tensor_tensor(bkm[:, :, :], bk_sb[:, :].unsqueeze(2).to_broadcast([P, KD, 2]),
                                                 parity[:, :].unsqueeze(1).to_broadcast([P, KD, 2]), ALU.mult))

        def body(engine, run):
            run(-2, 0, True, False, False, False)
            run(-1, 1, True, True, False, False)
            run(0, 0, True, True, True, False)
            run(1, 1, True, True, True, True)
            with engine.Fori(1, (B - 2) // 2) as j:
                run(2 * j, 0, True, True, True, True)
                run(2 * j + 1, 1, True, True, True, True)
            run(LAST - 1, 0, False, True, True, True)
            run(LAST, 1, False, False, True, True)
            run(LAST + 1, 0, False, False, False, True)

        def known(i):
            return isinstance(i, int)

        def qo_count(i):
            return i + 3 if proj else i

        with nc.Block() as block:

            @block.sync
            def _(sp):
                def run(i, u, queries, scores, values, output):
                    if queries:
                        k = i + 2
                        if not known(i) or k >= 2:
                            if proj:
                                sp.wait_ge(kv_done, k)
                            else:
                                sp.wait_ge(s_done, T4 * (k - 1))
                                sp.wait_ge(v_ready, k - 1)
                        if proj:
                            for d in range(KD):
                                sp.dma_start(cT[:, u, d, :], ctxT[one(k), d * P:(d + 1) * P, :].rearrange("o p s -> (o p) s"))\
                                  .then_inc(ctx_in[u], 16)
                        else:
                            for g in range(HT):
                                sp.dma_start(kM[g * DH:(g + 1) * DH, u, :, g, :], ctxT[one(k), :, :].rearrange("o (t h r) s -> h (o r) t s", t=KD, r=DH)[g])\
                                  .then_inc(ctx_in[u], 16)
                            sp.dma_start(vraw[:, u, :], ctx[one(k), :, :].rearrange("o s d -> (o s) d")).then_inc(ctx_in[u], 16)
                body(sp, run)

            @block.gpsimd
            def _(pool):
                def run(i, u, queries, scores, values, output):
                    if queries and oproj:
                        k = i + 2
                        pool.wait_ge(xn_ready, k + 1)
                        nc.gpsimd.tensor_tensor(row(X, k), row(X, k), bo_sb[:, :], ALU.add).then_inc(bo_added, 1)
                    if scores:
                        k, w = i + 1, 1 - u
                        if not proj:
                            if known(i):
                                pool.wait_ge(ctx_in[w], 16 * DMAS * ((k - w) // 2 + 1))
                            else:
                                pool.wait_ge(ctx_in[w], 8 * DMAS * (k - w) + 16 * DMAS)
                            if not known(i) or k >= 2:
                                pool.wait_ge(av_done, T4 * (k - 1))
                            nc.gpsimd.tensor_tensor(vx[:, w, :, 0:DH], vraw[:, w, :].rearrange("p (h d) -> p h d", h=H),
                                                    vx[:, w, :, DH:DH + 1].to_broadcast([P, H, DH]), ALU.mult).then_inc(v_ready, 1)
                        for c in range(T4):
                            pool.wait_ge(maxed, T4 * k + c + 1)
                            tc_ = t_sb[:, c, :].rearrange("p (t s) -> p t s", t=T4)
                            nc.gpsimd.tensor_tensor(tc_, tc_, mx[:, c, :].unsqueeze(2).to_broadcast([P, T4, P]), ALU.subtract)\
                              .then_inc(shifted, 1)
                body(pool, run)

            @block.vector
            def _(dve):
                def run(i, u, queries, scores, values, output):
                    if queries:
                        k = i + 2
                        if not known(i) or k >= 2:
                            dve.wait_ge(xo_done, k - 1)
                        nc.vector.tensor_scalar(xn[:, u, :], row(X, k), col(mean, k), col(rstd, k), ALU.subtract, ALU.mult)\
                          .then_inc(xn_ready, 1)
                    if output:
                        k = i - 1
                        dve.wait_ge(av_done, T4 * (k + 1))
                        nc.vector.reciprocal(rec[:, :], ps_v[:, :, DH:DH + 1].rearrange("p h o -> p (h o)")).then_inc(inverted, 1)
                        dve.wait_ge(inverted, k + 1)
                        if not oproj and (not known(i) or k >= 1):
                            dve.wait_ge(resid_done, k)
                        nc.vector.tensor_tensor(o_n[:, :].rearrange("p (h d) -> p h d", h=H), ps_v[:, :, 0:DH],
                                                rec[:, :].unsqueeze(2).to_broadcast([P, H, DH]), ALU.mult).then_inc(normed, 1)

                    def add_bias(c, k=i + 1):
                        dve.wait_ge(s_done, T4 * k + c + 1)
                        if not known(i) or k >= 1:
                            dve.wait_ge(exped, T4 * (k - 1) + c + 1)
                        b = bias[:, 0, :] if NB == 1 else row(bias, k)
                        nc.vector.tensor_tensor(t_sb[:, c, :].rearrange("p (t s) -> p t s", t=T4),
                                                ps_s[:, c, :].rearrange("p (t s) -> p t s", t=T4),
                                                b.unsqueeze(1).to_broadcast([P, T4, P]), ALU.add).then_inc(biased, 1)

                    def maximum(c, k=i + 1):
                        dve.wait_ge(biased, T4 * k + c + 1)
                        nc.vector.tensor_reduce(mx[:, c, :], t_sb[:, c, :].rearrange("p (t s) -> p t s", t=T4),
                                                AXIS.X, ALU.max).then_inc(maxed, 1)
                    if scores:
                        add_bias(0)
                        add_bias(1)
                        maximum(0)
                        add_bias(2)
                        maximum(1)
                    if queries and proj:
                        dve.wait_ge(kv_done, i + 3)
                        for c in range(SHARE):
                            at = slice(c * HP, (c + 1) * HP)
                            for e in range(2):
                                last = nc.vector.scalar_tensor_tensor(kM[at, u, :, 2 * c + e, :], ps_q[at, 0:KD, :], parity[at, e:e + 1],
                                                                      bkm[at, :, e:e + 1].to_broadcast([HP, KD, P]), ALU.mult, ALU.add)
                        last.then_inc(k_ready_low, 1)
                    if scores and proj:
                        dve.wait_ge(kv_done, i + 3)
                        if queries:
                            dve.wait_ge(k_ready, i + 3)
                        if not known(i) or i >= 1:
                            dve.wait_ge(av_done, T4 * i)
                        nc.vector.tensor_tensor(vx[:, 1 - u, :, 0:DH], half_b.rearrange("p (h d) -> p h d", h=H),
                                                bv_sb[:, :].rearrange("p (h d) -> p h d", h=H), ALU.add).then_inc(v_ready, 1)
                    if scores:
                        add_bias(3)
                        maximum(2)
                        maximum(3)
                    if queries and proj:
                        k = i + 2
                        dve.wait_ge(qo_done, qo_count(i))
                        if not known(i) or k >= 2:
                            dve.wait_ge(s_done, T4 * (k - 1))
                        nc.vector.scalar_tensor_tensor(qT[:, u, :, :], ps_q[:, 0:KD, :], float(scale),
                                                       bqs[:, :].unsqueeze(2).to_broadcast([P, KD, P]), ALU.mult, ALU.add)\
                          .then_inc(q_ready, 1)
                    if output:
                        k = i - 1
                        if oproj:
                            dve.wait_ge(qo_done, qo_count(i))
                            dve.wait_ge(bo_added, k + 1)
                            nc.vector.tensor_tensor(row(X, k), row(X, k), half_b, ALU.add).then_inc(resid_done, 1)
                        else:
                            dve.wait_ge(normed, k + 1)
                            nc.vector.scalar_tensor_tensor(row(X, k), o_n[:, :], col(qm, k), row(X, k), ALU.mult, ALU.add)\
                              .then_inc(resid_done, 1)
                body(dve, run)

            @block.scalar
            def _(act):
                def run(i, u, queries, scores, values, output):
                    def copy_pT(c):
                        n = T4 * i + c
                        act.wait_ge(pT_done, n + 1)
                        if not known(i) or n >= 2:
                            act.wait_ge(av_done, n - 1)
                        nc.scalar.activation(pT[:, c % 2, :, :], ps_t[c % 2].rearrange("p (t s) -> p t s", t=T4), ACT.Copy)\
                          .then_inc(pT_copied, 1)

                    def exponential(c, k=i + 1):
                        act.wait_ge(shifted, T4 * k + c + 1)
                        if not known(i) or k >= 1:
                            act.wait_ge(pT_done, T4 * (k - 1) + c + 1)
                        nc.scalar.activation(p_sb[:, c, :], t_sb[:, c, :], ACT.Exp).then_inc(exped, 1)
                    if values:
                        copy_pT(0)
                        copy_pT(1)
                    if queries or (output and oproj):
                        act.wait_ge(xo_done, i + 3)
                        parts = slice(0 if queries else KD, 2 * KD if output and oproj else KD)
                        nc.scalar.activation(xo[:, u, parts, :], ps_q[:, parts, :], ACT.Copy).then_inc(xo_copied, 1)
                    if scores:
                        exponential(0)
                    if queries and proj:
                        act.wait_ge(kv_done, i + 3)
                        for c in range(SHARE, T4):
                            at = slice(c * HP, (c + 1) * HP)
                            for t in range(KD):
                                for e in range(2):
                                    last = nc.scalar.activation(kM[at, u, t, 2 * c + e, :], ps_q[at, t, :], ACT.Identity,
                                                                bias=bkm[at, t, e:e + 1], scale=parity[at, e:e + 1])
                        last.then_inc(k_ready, 1)
                    if values:
                        copy_pT(2)
                    if scores:
                        exponential(1)
                    if values:
                        copy_pT(3)
                    if scores:
                        exponential(2)
                    if scores:
                        exponential(3)
                body(act, run)

            @block.tensor
            def _(pe):
                def project(w, src, u):
                    for t in range(KD):
                        for d in range(KD):
                            last = nc.tensor.matmul(ps_q[:, t, :], w[:, d, t * P:(t + 1) * P], src[:, u, d, :],
                                                    start=(d == 0), stop=(d == KD - 1))
                    return last

                def run(i, u, queries, scores, values, output):
                    def score(c, k=i + 1, w=1 - u):
                        if c == 0:
                            pe.wait_ge(q_ready if proj else xo_copied, k + 1)
                            if proj:
                                pe.wait_ge(k_ready, k + 1)
                                pe.wait_ge(k_ready_low, k + 1)
                            elif known(i):
                                pe.wait_ge(ctx_in[w], 16 * DMAS * ((k - w) // 2 + 1))
                            else:
                                pe.wait_ge(ctx_in[w], 8 * DMAS * (k - w) + 16 * DMAS)
                        if not known(i) or k >= 1:
                            pe.wait_ge(biased, T4 * (k - 1) + c + 1)
                        for t in range(KD):
                            last = nc.tensor.matmul(ps_s[:, c, t * 2 * P:(t + 1) * 2 * P], (qT if proj else xo)[:, w, t, :],
                                                    kM[:, w, t, 2 * c:2 * c + 2, :].rearrange("p e s -> p (e s)"), start=True, stop=True)
                        last.then_inc(s_done, 1)

                    def transpose_p(c):
                        n = T4 * i + c
                        pe.wait_ge(exped, n + 1)
                        if not known(i) or n >= 2:
                            pe.wait_ge(pT_copied, n - 1)
                        for t in range(T4):
                            last = nc.tensor.transpose(ps_t[c % 2][:, t * P:(t + 1) * P], p_sb[:, c, t * P:(t + 1) * P], ident[:, :])
                        last.then_inc(pT_done, 1)

                    def apply_v(c):
                        pe.wait_ge(pT_copied, T4 * i + c + 1)
                        if c == 0:
                            pe.wait_ge(v_ready, i + 1)
                            if not known(i) or i >= 1:
                                pe.wait_ge(normed, i)
                        for t in range(T4):
                            h = 8 * (t // 2) + 2 * c + t % 2
                            last = nc.tensor.matmul(ps_v[:, h, :], pT[:, c % 2, t, :], vx[:, u, h, :], start=True, stop=True)
                        last.then_inc(av_done, 1)

                    if scores:
                        score(0)
                    if values:
                        transpose_p(0)
                    if scores:
                        score(1)
                    if values:
                        transpose_p(1)
                    if queries or (output and oproj):
                        if oproj and (not known(i) or i >= 2):
                            pe.wait_ge(resid_done, i - 1)
                        if queries:
                            pe.wait_ge(xn_ready, i + 3)
                            for d in range(KD):
                                last = nc.tensor.transpose(ps_q[:, d, :], xn[:, u, d * P:(d + 1) * P], ident[:, :])
                        if output and oproj:
                            pe.wait_ge(normed, i)
                            for d in range(KD):
                                last = nc.tensor.transpose(ps_q[:, KD + d, :], o_n[:, d * P:(d + 1) * P], ident[:, :])
                        last.then_inc(xo_done, 1)
                    if scores:
                        score(2)
                    if values:
                        apply_v(0)
                    if proj and (queries or scores):
                        pe.wait_ge(xo_copied, i + 3)
                        if queries:
                            if known(i):
                                pe.wait_ge(ctx_in[u], 16 * DMAS * ((i + 2 - u) // 2 + 1))
                            else:
                                pe.wait_ge(ctx_in[u], 8 * DMAS * (i + 2 - u) + 16 * DMAS)
                            last = project(wk_sb, cT, u)
                        if scores:
                            for d in range(KD):
                                last = nc.tensor.matmul(half_b, cT[:, 1 - u, d, :], wv_sb[:, d, :], start=(d == 0), stop=(d == KD - 1))
                        last.then_inc(kv_done, 1)
                    if scores:
                        score(3)
                    if values:
                        transpose_p(2)
                        apply_v(1)
                        transpose_p(3)
                        apply_v(2)
                    if (queries and proj) or (output and oproj):
                        if proj and scores:
                            pe.wait_ge(v_ready, i + 2)
                        elif proj and queries:
                            pe.wait_ge(k_ready, i + 3)
                            pe.wait_ge(k_ready_low, i + 3)
                        else:
                            pe.wait_ge(xo_copied, i + 3)
                        if output and oproj:
                            for d in range(KD):
                                last = nc.tensor.matmul(half_b, xo[:, u, KD + d, :], wo_sb[:, d, :], start=(d == 0), stop=(d == KD - 1))
                        if queries and proj:
                            last = project(wq_sb, xo, u)
                        last.then_inc(qo_done, 1)
                    if values:
                        apply_v(3)
                body(pe, run)


def store(nc, X, out):
    with ExitStack() as stack:
        stored = stack.enter_context(nc.semaphore("stored"))
        with nc.Block() as block:

            @block.sync
            def _(sp):
                sp.dma_start(out.rearrange("b p d -> p b d"), X[:, :, :]).then_inc(stored, 16)
                sp.wait_ge(stored, 16)


def norm_and_product(nc, layer, X, ident, mean, rstd, small, logits, XT=None, base=None, small_bias=None, base_bias=None, rows_out=None):
    N = small.shape[2]
    G = 2
    STEPS = B // G
    with ExitStack() as stack:
        m = Pool(nc, stack, layer + "_np")
        xn, xs = m.sb("xn", [P, 2, G, D]), m.sb("xs", [P, 2, G, KD, P])
        PS = stack.enter_context(nc.psum_tensor(f"{layer}_np_ps", [P, 8, 512], F32))
        xn_ready, x_done, x_copied, kept = m.sem("xn_ready"), m.sem("x_done"), m.sem("x_copied"), m.sem("kept")
        out_stored = [m.sem("out_stored0"), m.sem("out_stored1")]
        l_done, l_read, b_done, b_added, bias_added = (m.sem(n) for n in ("l_done", "l_read", "b_done", "b_added", "bias_added"))

        def body(engine, run):
            run(-1, 1, True, False)
            run(0, 0, True, True)
            run(1, 1, True, True)
            with engine.Fori(1, STEPS // 2 - 1) as j:
                run(2 * j, 0, True, True)
                run(2 * j + 1, 1, True, True)
            run(STEPS - 2, 0, True, True)
            run(STEPS - 1, 1, False, True)

        def later(i, n):
            return not isinstance(i, int) or i >= n

        def batches(t, i):
            return t[:, bass.ds(G * i, G), :]

        with nc.Block() as block:

            @block.sync
            def _(sp):
                if rows_out is not None:
                    def run(i, u, ahead, now):
                        if ahead:
                            k = i + 1
                            sp.wait_ge(xn_ready, k + 1)
                            sp.dma_start(rows_out[bass.ds(k * G * S, G * S), :].rearrange("(b p) d -> p b d", b=G), xn[:, 1 - u, :, :])\
                              .then_inc(out_stored[1 - u], 16)
                    body(sp, run)
                    for stored in out_stored:
                        sp.wait_ge(stored, 8 * STEPS)

            @block.vector
            def _(dve):
                def run(i, u, ahead, now):
                    if ahead:
                        k, w = i + 1, 1 - u
                        if later(k, 2):
                            dve.wait_ge(x_done, k - 1)
                            if rows_out is not None:
                                dve.wait_ge(out_stored[w], 8 * (k - w))
                        for g in range(G):
                            last = nc.vector.tensor_scalar(xn[:, w, g, :], row(X, G * k + g), col(mean, G * k + g), col(rstd, G * k + g),
                                                           ALU.subtract, ALU.mult)
                        last.then_inc(xn_ready, 1)
                    if now:
                        if XT is not None:
                            dve.wait_ge(x_copied, i + 1)
                            nc.vector.tensor_copy(XT[:, :, bass.ds(G * i, G), :].rearrange("p k g s -> p g k s"), xs[:, u, :, :, :])\
                              .then_inc(kept, 1)
                        dve.wait_ge(l_done, i + 1)
                        products = PS[:, 2 + u, 0:G * N].rearrange("p (g n) -> p g n", g=G)
                        if small_bias is None:
                            nc.vector.tensor_copy(batches(logits, i), products).then_inc(l_read, 1)
                        else:
                            nc.vector.tensor_tensor(batches(logits, i), products, small_bias[:, :].unsqueeze(1).to_broadcast([P, G, N]),
                                                    ALU.add).then_inc(l_read, 1)
                        if base is not None:
                            dve.wait_ge(b_done, i + 1)
                            dve.wait_ge(bias_added, i + 1)
                            nc.vector.tensor_tensor(batches(X, i), batches(X, i), PS[:, 4 + u, :].rearrange("p (g d) -> p g d", g=G), ALU.add)\
                              .then_inc(b_added, 1)
                body(dve, run)

            @block.gpsimd
            def _(pool):
                if base is not None:
                    def run(i, u, ahead, now):
                        if ahead:
                            pool.wait_ge(xn_ready, i + 2)
                            nc.gpsimd.tensor_tensor(batches(X, i + 1), batches(X, i + 1), base_bias[:, :].unsqueeze(1).to_broadcast([P, G, D]), ALU.add)\
                              .then_inc(bias_added, 1)
                    body(pool, run)

            @block.scalar
            def _(act):
                def run(i, u, ahead, now):
                    if ahead:
                        k, w = i + 1, 1 - u
                        act.wait_ge(x_done, k + 1)
                        if later(k, 2):
                            act.wait_ge(l_done, k - 1)
                            if base is not None:
                                act.wait_ge(b_done, k - 1)
                            if XT is not None:
                                act.wait_ge(kept, k - 1)
                        nc.scalar.activation(xs[:, w, :, :, :], PS[:, w, :].rearrange("p (g k s) -> p g k s", g=G, k=KD), ACT.Copy)\
                          .then_inc(x_copied, 1)
                body(act, run)

            @block.tensor
            def _(pe):
                def run(i, u, ahead, now):
                    if ahead:
                        k, w = i + 1, 1 - u
                        pe.wait_ge(xn_ready, k + 1)
                        if later(k, 2):
                            pe.wait_ge(x_copied, k - 1)
                        for g in range(G):
                            for d in range(KD):
                                last = nc.tensor.transpose(PS[:, w, (g * KD + d) * P:(g * KD + d + 1) * P], xn[:, w, g, d * P:(d + 1) * P], ident[:, :])
                        last.then_inc(x_done, 1)
                    if now:
                        pe.wait_ge(x_copied, i + 1)
                        if later(i, 2):
                            pe.wait_ge(l_read, i - 1)
                        for g in range(G):
                            for d in range(KD):
                                last = nc.tensor.matmul(PS[:, 2 + u, g * N:(g + 1) * N], xs[:, u, g, d, :], small[:, d, :], start=(d == 0), stop=(d == KD - 1))
                        last.then_inc(l_done, 1)
                        if base is not None:
                            if later(i, 2):
                                pe.wait_ge(b_added, i - 1)
                            for g in range(G):
                                for d in range(KD):
                                    last = nc.tensor.matmul(PS[:, 4 + u, g * D:(g + 1) * D], xs[:, u, g, d, :], base[:, d, :], start=(d == 0), stop=(d == KD - 1))
                            last.then_inc(b_done, 1)
                body(pe, run)


def add_product(nc, layer, X, ident, coef, rows, K):
    G = 4
    with ExitStack() as stack:
        m = Pool(nc, stack, layer + "_ap")
        cs, cT = m.sb("cs", [P, B, P]), m.sb("cT", [K, 2, G * P])
        PS = stack.enter_context(nc.psum_tensor(f"{layer}_ap_ps", [P, 8, 512], F32))
        cleared, staged, t_done, t_copied, r_done, added = (m.sem(n) for n in ("cleared", "staged", "t_done", "t_copied", "r_done", "added"))
        with nc.Block() as block:

            @block.gpsimd
            def _(pool):
                nc.gpsimd.memset(cs[:, :, K:], 0.0).then_inc(cleared, 1)

            @block.vector
            def _(dve):
                nc.vector.tensor_copy(cs[:, :, 0:K], coef[:, :, 0:K]).then_inc(staged, 1)
                for i in range(B // G):
                    for k in range(G // 2):
                        b = G * i + 2 * k
                        dve.wait_ge(r_done, G // 2 * i + k + 1)
                        nc.vector.tensor_tensor(X[:, b:b + 2, :], X[:, b:b + 2, :], PS[:, 2 + 2 * (i % 2) + k, :].rearrange("p (b d) -> p b d", b=2),
                                                ALU.add).then_inc(added, 1)

            @block.scalar
            def _(act):
                for i in range(B // G):
                    act.wait_ge(t_done, i + 1)
                    if i >= 2:
                        act.wait_ge(r_done, G // 2 * (i - 1))
                    nc.scalar.activation(cT[:, i % 2, :], PS[0:K, i % 2, :], ACT.Copy).then_inc(t_copied, 1)

            @block.tensor
            def _(pe):
                def transposes(i):
                    if i >= 2:
                        pe.wait_ge(t_copied, i - 1)
                    for k in range(G):
                        last = nc.tensor.transpose(PS[:, i % 2, k * P:(k + 1) * P], cs[:, G * i + k, :], ident[:, :])
                    last.then_inc(t_done, 1)
                pe.wait_ge(cleared, 1)
                pe.wait_ge(staged, 1)
                transposes(0)
                for i in range(B // G):
                    if i + 1 < B // G:
                        transposes(i + 1)
                    pe.wait_ge(t_copied, i + 1)
                    if i >= 2:
                        pe.wait_ge(added, G // 2 * (i - 1))
                    for k in range(G):
                        last = nc.tensor.matmul(PS[:, 2 + 2 * (i % 2) + k // 2, (k % 2) * D:(k % 2 + 1) * D], cT[:, i % 2, k * P:(k + 1) * P],
                                                rows[0:K, :], start=True, stop=True)
                        if k % 2:
                            last.then_inc(r_done, 1)


def spread(t, n):
    return t.unsqueeze(2).to_broadcast([P, B, n])


def select_top(nc, c, combine, numbers, hit, index, values, count, E):
    for j in range(count):
        c.do(nc.vector.tensor_tensor(hit, numbers, spread(index[:, :, j], E), ALU.is_equal))
        if values is not None:
            c.do(nc.vector.tensor_tensor(hit, hit, spread(values[:, :, j], E), ALU.mult))
        if j == 0:
            c.do(nc.vector.tensor_copy(combine, hit))
        else:
            c.do(nc.vector.tensor_tensor(combine, combine, hit, ALU.add))


def top_picks(nc, c, values8, index8, index_f, source):
    for b in range(B):
        last = nc.vector.max(values8[:, b, :], source[:, b, :])
        if b == B - 1:
            c.do(last)
        else:
            last.then_inc(c.sem, 1)
            c.n += 1
    for b in range(B):
        last = nc.vector.max_index(index8[:, b, :], values8[:, b, :], source[:, b, :])
        if b == B - 1:
            c.do(last)
        else:
            last.then_inc(c.sem, 1)
            c.n += 1
    c.do(nc.vector.tensor_copy(index_f[:, :, :], index8[:, :, :]))


def route_top2(nc, layer, logits, combine, chosen, share, E, background, arrived):
    with ExitStack() as stack:
        m = Pool(nc, stack, layer + "_route")
        n_i, n_f = m.sb("n_i", [P, B, E], I32), m.sb("n_f", [P, B, E])
        v8, i8, i8f, hit = m.sb("v8", [P, B, 8]), m.sb("i8", [P, B, 8], U32), m.sb("i8f", [P, B, 8]), m.sb("hit", [P, B, E])
        gap, e, p = m.sb("gap", [P, B]), m.sb("e", [P, B]), m.sb("p", [P, B, 2])
        numbered, chain, gap_ready, e_ready = (m.sem(n) for n in ("numbered", "chain", "gap_ready", "e_ready"))
        with nc.Block() as block:

            @block.gpsimd
            def _(pool):
                nc.gpsimd.iota(n_i[:, :, :], pattern=[[0, B], [1, E]], base=0, channel_multiplier=0).then_inc(numbered, 1)

            @block.scalar
            def _(act):
                act.wait_ge(gap_ready, 1)
                nc.scalar.activation(e[:, :], gap[:, :], ACT.Exp).then_inc(e_ready, 1)
                for dst, src in background:
                    act.dma_start(dst, src).then_inc(arrived, 16)

            @block.vector
            def _(dve):
                c = Chain(dve, chain)
                dve.wait_ge(numbered, 1)
                c.do(nc.vector.tensor_copy(n_f[:, :, :], n_i[:, :, :]))
                top_picks(nc, c, v8, i8, i8f, logits)
                nc.vector.tensor_tensor(gap[:, :], v8[:, :, 1], v8[:, :, 0], ALU.subtract).then_inc(gap_ready, 1)
                dve.wait_ge(e_ready, 1)
                c.do(nc.vector.tensor_scalar(gap[:, :], e[:, :], 1.0, None, ALU.add))
                c.do(nc.vector.reciprocal(p[:, :, 0], gap[:, :]))
                c.do(nc.vector.tensor_tensor(p[:, :, 1], p[:, :, 0], e[:, :], ALU.mult))
                select_top(nc, c, combine[:, :, 0:E], n_f[:, :, :], hit[:, :, :], i8f, p, 2, E)
                c.do(nc.vector.tensor_copy(chosen[:, :, :], i8f[:, :, 0:2]))
                c.do(nc.vector.tensor_copy(share[:, :, :], p[:, :, :]))


def softmax_rows(nc, c, dve, act_ready, e_ready, scores, top, N):
    c.do(nc.vector.tensor_reduce(top, scores, AXIS.X, ALU.max))
    nc.vector.tensor_tensor(scores, scores, spread(top, N), ALU.subtract).then_inc(act_ready, 1)
    dve.wait_ge(e_ready, 1)
    c.do(nc.vector.tensor_reduce(top, scores, AXIS.X, ALU.add))
    c.do(nc.vector.reciprocal(top, top))
    c.do(nc.vector.tensor_tensor(scores, scores, spread(top, N), ALU.mult))


def route_grouped(nc, layer, logits, combine, chosen, share, E, GROUPS, TOP_GROUPS, TOP, background, arrived):
    G = E // GROUPS
    assert G == 4 and GROUPS == 8
    with ExitStack() as stack:
        m = Pool(nc, stack, layer + "_route")
        n_i, n_f = m.sb("n_i", [P, B, E], I32), m.sb("n_f", [P, B, E])
        v8, i8, i8f, hit = m.sb("v8", [P, B, 8]), m.sb("i8", [P, B, 8], U32), m.sb("i8f", [P, B, 8]), m.sb("hit", [P, B, E])
        top, masked = m.sb("top", [P, B]), m.sb("masked", [P, B, E])
        hi, lo = m.sb("hi", [P, 2, B, GROUPS]), m.sb("lo", [P, 2, B, GROUPS])
        gs, keep = m.sb("gs", [P, B, GROUPS]), m.sb("keep", [P, B, GROUPS])
        numbered, chain, act_ready, e_ready = (m.sem(n) for n in ("numbered", "chain", "act_ready", "e_ready"))
        with nc.Block() as block:

            @block.gpsimd
            def _(pool):
                nc.gpsimd.iota(n_i[:, :, :], pattern=[[0, B], [1, E]], base=0, channel_multiplier=0).then_inc(numbered, 1)
                pool.wait_ge(numbered, 1)
                nc.gpsimd.memset(combine[:, :, E:], 1.0).then_inc(numbered, 1)

            @block.scalar
            def _(act):
                act.wait_ge(act_ready, 1)
                nc.scalar.activation(logits[:, :, :], logits[:, :, :], ACT.Exp).then_inc(e_ready, 1)
                for dst, src in background:
                    act.dma_start(dst, src).then_inc(arrived, 16)

            @block.vector
            def _(dve):
                c = Chain(dve, chain)
                dve.wait_ge(numbered, 2)
                c.do(nc.vector.tensor_copy(n_f[:, :, :], n_i[:, :, :]))
                softmax_rows(nc, c, dve, act_ready, e_ready, logits[:, :, :], top[:, :], E)
                s = logits[:, :, :].rearrange("p b (g m) -> p b g m", m=G)
                for k in range(2):
                    c.do(nc.vector.tensor_tensor(hi[:, k], s[:, :, :, 2 * k], s[:, :, :, 2 * k + 1], ALU.max))
                    c.do(nc.vector.tensor_tensor(lo[:, k], s[:, :, :, 2 * k], s[:, :, :, 2 * k + 1], ALU.min))
                c.do(nc.vector.tensor_tensor(gs[:, :, :], hi[:, 0], hi[:, 1], ALU.max))
                c.do(nc.vector.tensor_tensor(keep[:, :, :], hi[:, 0], hi[:, 1], ALU.min))
                c.do(nc.vector.tensor_tensor(hi[:, 0], lo[:, 0], lo[:, 1], ALU.max))
                c.do(nc.vector.tensor_tensor(hi[:, 1], hi[:, 0], keep[:, :, :], ALU.max))
                c.do(nc.vector.tensor_tensor(gs[:, :, :], gs[:, :, :], hi[:, 1], ALU.add))
                top_picks(nc, c, v8, i8, i8f, gs)
                select_top(nc, c, keep[:, :, :], n_f[:, :, 0:GROUPS], hit[:, :, 0:GROUPS], i8f, None, TOP_GROUPS, GROUPS)
                m4 = masked[:, :, :].rearrange("p b (g m) -> p b g m", m=G)
                c.do(nc.vector.tensor_scalar(gs[:, :, :], keep[:, :, :], 1.0, -MASKED, ALU.subtract, ALU.mult))
                c.do(nc.vector.tensor_tensor(m4, s, keep[:, :, :].unsqueeze(3).to_broadcast([P, B, GROUPS, G]), ALU.mult))
                c.do(nc.vector.tensor_tensor(m4, m4, gs[:, :, :].unsqueeze(3).to_broadcast([P, B, GROUPS, G]), ALU.add))
                top_picks(nc, c, v8, i8, i8f, masked)
                select_top(nc, c, combine[:, :, 0:E], n_f[:, :, :], hit[:, :, :], i8f, v8, TOP, E)
                c.do(nc.vector.tensor_copy(chosen[:, :, :], i8f[:, :, 0:TOP]))
                c.do(nc.vector.tensor_copy(share[:, :, :], v8[:, :, 0:TOP]))


def experts(nc, layer, X, XT, combine, blob, E, F, gated):
    FT = F // P
    HID = FT * (2 if gated else 1)
    NT = 512
    UNITS = B * P // NT
    SUB = NT // P
    W1, BI = KD * F * (2 if gated else 1), HID
    with ExitStack() as stack:
        m = Pool(nc, stack, layer + "_ex")
        wb = m.sb("w", [P, 2, blob.shape[2]])
        h = m.sb("h", [P, 2, FT, NT])
        sg = m.sb("sg", [P, 2, NT]) if gated else None
        PS = stack.enter_context(nc.psum_tensor(f"{layer}_ex_ps", [P, 8, 512], F32))
        w_in = [m.sem("w_in0"), m.sem("w_in1")]
        h_done, act_done, h_ready, y_done, added = (m.sem(n) for n in ("h_done", "act_done", "h_ready", "y_done", "added"))

        def hidden_bank(n, f):
            return HID * (n % 2) + f if gated else f

        def w1(u, f, d):
            return wb[:, u, (f * KD + d) * P:(f * KD + d + 1) * P]

        def bias(u, f):
            return wb[:, u, W1 + f:W1 + f + 1]

        def w2(u, f):
            return wb[:, u, W1 + BI + f * D:W1 + BI + (f + 1) * D]

        def xt(d, n):
            return XT[:, d, SUB * n:SUB * (n + 1), :].rearrange("p b s -> p (b s)")

        def body(engine, run):
            run(0, 0, True, False)
            if E > 2:
                run(1, 1, False, False)
                with engine.Fori(1, E // 2 - 1) as j:
                    run(2 * j, 0, False, False)
                    run(2 * j + 1, 1, False, False)
                run(E - 2, 0, False, False)
            run(E - 1, 1, False, True)

        def known(e):
            return isinstance(e, int)

        def loads_seen(e, u):
            return 8 * (e - u) + 16

        with nc.Block() as block:

            @block.sync
            def _(sp):
                def run(e, u, first, last):
                    if not known(e) or e >= 2:
                        sp.wait_ge(y_done, 2 * UNITS * (e - 1))
                    sp.dma_start(wb[:, u, :], blob[one(e), :, :].rearrange("o p n -> (o p) n")).then_inc(w_in[u], 16)
                body(sp, run)

            @block.tensor
            def _(pe):
                def hidden(e, u, n):
                    g = UNITS * e + n
                    if n == 0:
                        pe.wait_ge(w_in[u], loads_seen(e, u))
                    for f in range(HID):
                        if gated:
                            if not known(e) or g >= 2:
                                pe.wait_ge(act_done if f < FT else h_ready, g - 1)
                        elif not known(e) or g >= 1:
                            pe.wait_ge(h_ready, FT * (g - 1) + f + 1)
                        for d in range(KD):
                            last = nc.tensor.matmul(PS[:, hidden_bank(n, f), :], w1(u, f, d), xt(d, n), start=(d == 0), stop=(d == KD - 1))
                        last.then_inc(h_done, 1)

                def outputs(e, u, n):
                    g = UNITS * e + n
                    pe.wait_ge(h_ready, FT * (g + 1))
                    for s in range(SUB):
                        if s % 2 == 0 and (not known(e) or g >= 2):
                            pe.wait_ge(added, 2 * (g - 2) + s // 2 + 1)
                        for f in range(FT):
                            last = nc.tensor.matmul(PS[:, 4 + 2 * (n % 2) + s // 2, (s % 2) * D:(s % 2 + 1) * D],
                                                    h[:, n % 2, f, s * P:(s + 1) * P], w2(u, f), start=(f == 0), stop=(f == FT - 1))
                        if s % 2:
                            last.then_inc(y_done, 1)

                def run(e, u, first, last):
                    if first:
                        hidden(e, u, 0)
                    for n in range(UNITS):
                        if n < UNITS - 1:
                            hidden(e, u, n + 1)
                        elif not last:
                            hidden(e + 1, 1 - u, 0)
                        outputs(e, u, n)
                body(pe, run)

            @block.scalar
            def _(act):
                def run(e, u, first, last):
                    for n in range(UNITS):
                        g = UNITS * e + n
                        for f in range(FT):
                            act.wait_ge(h_done, HID * g + f + 1)
                            if gated:
                                if not known(e) or g >= 2:
                                    act.wait_ge(h_ready, g - 1)
                                nc.scalar.activation(sg[:, n % 2, :], PS[:, hidden_bank(n, f), :], ACT.Silu, bias=bias(u, f))\
                                  .then_inc(act_done, 1)
                            else:
                                if f == 0 and (not known(e) or g >= 2):
                                    act.wait_ge(y_done, 2 * (g - 1))
                                nc.scalar.activation(h[:, n % 2, f, :], PS[:, hidden_bank(n, f), :], ACT.Gelu, bias=bias(u, f))\
                                  .then_inc(h_ready, 1)
                body(act, run)

            @block.vector
            def _(dve):
                def gate(e, u, n):
                    g = UNITS * e + n
                    dve.wait_ge(h_done, HID * (g + 1))
                    dve.wait_ge(act_done, g + 1)
                    if not known(e) or g >= 2:
                        dve.wait_ge(y_done, 2 * (g - 1))
                    nc.vector.scalar_tensor_tensor(h[:, n % 2, 0, :], PS[:, hidden_bank(n, 1), :], bias(u, 1), sg[:, n % 2, :],
                                                   ALU.add, ALU.mult).then_inc(h_ready, 1)

                def run(e, u, first, last):
                    if gated and first:
                        gate(e, u, 0)
                    for n in range(UNITS):
                        g = UNITS * e + n
                        if gated:
                            if n < UNITS - 1:
                                gate(e, u, n + 1)
                            elif not last:
                                gate(e + 1, 1 - u, 0)
                        for s in range(SUB):
                            b = SUB * n + s
                            if s % 2 == 0:
                                dve.wait_ge(y_done, 2 * g + s // 2 + 1)
                            acc = nc.vector.scalar_tensor_tensor(
                                X[:, b, :], PS[:, 4 + 2 * (n % 2) + s // 2, (s % 2) * D:(s % 2 + 1) * D],
                                combine[:, b, one(e)], X[:, b, :], ALU.mult, ALU.add)
                            if s % 2:
                                acc.then_inc(added, 1)
                body(dve, run)


def assign_slots(nc, layer, combine, chosen, slot, token, tile_expert, below, ident, E, K, TILES):
    with ExitStack() as stack:
        m = Pool(nc, stack, layer + "_slots")
        picked = m.sb("picked", [P, B, E], BF16)
        before, every = m.sb("before", [P, P], BF16), m.sb("every", [P, P], BF16)
        every_f, place = m.sb("every_f", [P, P]), m.sb("place", [P, 1])
        n_i, n_f = m.sb("n_i", [P, B, E], I32), m.sb("n_f", [P, B, E])
        across_i, across = m.sb("across_i", [P, P], I32), m.sb("across", [P, P])
        id_i, ids = m.sb("id_i", [P, B], I32), m.sb("ids", [P, B])
        position, hit = m.sb("position", [P, B, E]), m.sb("hit", [P, B, E])
        tiles, ends, ends2, t = (m.sb(n, [P, E]) for n in ("tiles", "ends", "ends2", "t"))
        tile_of, place_of = m.sb("tile_of", [P, B, K]), m.sb("place_of", [P, B, K])
        diagonal = m.sb("diagonal", [P, P])
        in_place, in_tile = m.sb("in_place", [P, 2, K, P], F16), m.sb("in_tile", [P, 2, K, TILES], F16)
        PS = stack.enter_context(nc.psum_tensor(f"{layer}_slots_ps", [P, 8, 512], F32))
        numbered, chain, sides_ready, ranked, te_ready, te_done = (
            m.sem(n) for n in ("numbered", "chain", "sides_ready", "ranked", "te_ready", "te_done"))
        slots_ready, place_ready, tile_ready, entered = (m.sem(n) for n in ("slots_ready", "place_ready", "tile_ready", "entered"))
        ranks = PS[:, 0, 0:B * E].rearrange("p (b e) -> p b e", b=B)
        counts, te, table = PS[:, 1, 0:E], PS[:, 2, 0:P], PS[:, 3, 0:TILES]
        with nc.Block() as block:

            @block.gpsimd
            def _(pool):
                nc.gpsimd.iota(n_i[:, :, :], pattern=[[0, B], [1, E]], base=0, channel_multiplier=0).then_inc(numbered, 1)
                nc.gpsimd.iota(across_i[:, :], pattern=[[1, P]], base=0, channel_multiplier=0).then_inc(numbered, 1)
                nc.gpsimd.iota(id_i[:, :], pattern=[[S, B]], base=0, channel_multiplier=1).then_inc(numbered, 1)
                nc.gpsimd.memset(every[:, :], 1.0).then_inc(numbered, 1)
                nc.gpsimd.memset(every_f[:, :], 1.0).then_inc(numbered, 1)

            @block.vector
            def _(dve):
                c = Chain(dve, chain)
                nc.vector.tensor_scalar(picked[:, :, :], combine[:, :, 0:E], 0.0, None, ALU.is_gt).then_inc(sides_ready, 1)
                nc.vector.tensor_scalar(before[:, :], below[:, :], -1.0, 1.0, ALU.mult, ALU.add).then_inc(sides_ready, 1)
                dve.wait_ge(numbered, 5)
                c.do(nc.vector.tensor_copy(n_f[:, :, :], n_i[:, :, :]))
                c.do(nc.vector.tensor_copy(across[:, :], across_i[:, :]))
                c.do(nc.vector.tensor_copy(ids[:, :], id_i[:, :]))
                dve.wait_ge(ranked, 1)

                def rounded(out, x, scale, offset):
                    c.do(nc.vector.tensor_scalar(out, x, scale, offset, ALU.mult, ALU.add))
                    c.do(nc.vector.tensor_scalar(out, out, MAGIC, None, ALU.add))
                    c.do(nc.vector.tensor_scalar(out, out, MAGIC, None, ALU.subtract))
                rounded(tiles[:, :], counts, 1.0 / P, 63.5 / P)
                src, dst, step = tiles, ends, 1
                while step < E:
                    c.do(nc.vector.tensor_tensor(dst[:, step:], src[:, step:], src[:, 0:E - step], ALU.add))
                    c.do(nc.vector.tensor_copy(dst[:, 0:step], src[:, 0:step]))
                    src, dst, step = dst, (ends2 if dst is ends else ends), 2 * step
                c.do(nc.vector.tensor_tensor(t[:, :], src[:, :], ids[:, 0:1].to_broadcast([P, E]), ALU.is_le))
                c.do(nc.vector.tensor_reduce(place[:, :], t[:, :], AXIS.X, ALU.add))
                c.do(nc.vector.tensor_scalar(place[:, :], place[:, :], float(E - 1), None, ALU.min))
                nc.vector.tensor_scalar(diagonal[:, :], ident[:, :], place[:, 0:1], None, ALU.mult).then_inc(te_ready, 1)
                c.do(nc.vector.tensor_tensor(t[:, :], src[:, :], tiles[:, :], ALU.subtract))
                c.do(nc.vector.tensor_scalar(t[:, :], t[:, :], float(P), None, ALU.mult))
                c.do(nc.vector.tensor_tensor(position[:, :, :], ranks, t[:, :].unsqueeze(1).to_broadcast([P, B, E]), ALU.add))
                for k in range(K):
                    c.do(nc.vector.tensor_tensor(hit[:, :, :], n_f[:, :, :], spread(chosen[:, :, k], E), ALU.is_equal))
                    c.do(nc.vector.tensor_tensor(hit[:, :, :], hit[:, :, :], position[:, :, :], ALU.mult))
                    c.do(nc.vector.tensor_reduce(slot[:, :, k], hit[:, :, :], AXIS.X, ALU.add))
                rounded(tile_of[:, :, :], slot[:, :, :], 1.0 / P, -63.5 / P)
                nc.vector.scalar_tensor_tensor(place_of[:, :, :], tile_of[:, :, :], -float(P), slot[:, :, :], ALU.mult, ALU.add)\
                  .then_inc(slots_ready, 1)
                dve.wait_ge(te_done, 1)
                nc.vector.tensor_copy(tile_expert[0:1, :], te[0:1, 0:TILES]).then_inc(chain, 1)
                dve.wait_ge(slots_ready, 1)

                def run(b, u):
                    if not isinstance(b, int) or b >= 2:
                        dve.wait_ge(entered, b - 1)
                    nc.vector.tensor_tensor(in_place[:, u, :, :], across[:, :].unsqueeze(1).to_broadcast([P, K, P]),
                                            row(place_of, b).unsqueeze(2).to_broadcast([P, K, P]), ALU.is_equal).then_inc(place_ready, 1)
                    for k in range(K):
                        last = nc.vector.tensor_scalar(in_tile[:, u, k, :], across[:, 0:TILES], row(tile_of, b)[:, k:k + 1], col(ids, b),
                                                       ALU.is_equal, ALU.mult)
                    last.then_inc(tile_ready, 1)
                run(0, 0)
                run(1, 1)
                with dve.Fori(1, B // 2) as j:
                    run(2 * j, 0)
                    run(2 * j + 1, 1)
                dve.wait_ge(entered, B)
                nc.vector.tensor_copy(token[:, :], table).then_inc(chain, 1)

            @block.tensor
            def _(pe):
                pe.wait_ge(sides_ready, 2)
                pe.wait_ge(numbered, 5)
                nc.tensor.matmul(PS[:, 0, 0:B * E], before[:, :], picked[:, :, :].rearrange("p b e -> p (b e)"), start=True, stop=False)
                for b in range(B - 1):
                    nc.tensor.matmul(PS[:, 0, (b + 1) * E:B * E], every[:, :],
                                     picked[:, b, :].unsqueeze(1).to_broadcast([P, B - 1 - b, E]), start=False, stop=(b == B - 2))
                for b in range(B):
                    last = nc.tensor.matmul(counts, every[:, :], picked[:, b, :], start=(b == 0), stop=(b == B - 1))
                last.then_inc(ranked, 1)
                pe.wait_ge(te_ready, 1)
                nc.tensor.matmul(te, every_f[:, :], diagonal[:, :], start=True, stop=True).then_inc(te_done, 1)

                def run(b, u, first, last_one):
                    pe.wait_ge(place_ready, b + 1)
                    pe.wait_ge(tile_ready, b + 1)
                    for k in range(K):
                        last = nc.tensor.matmul(table, in_place[:, u, k, :], in_tile[:, u, k, :], start=(first and k == 0),
                                                stop=(last_one and k == K - 1))
                    last.then_inc(entered, 1)
                run(0, 0, True, False)
                run(1, 1, False, False)
                with pe.Fori(1, B // 2 - 1) as j:
                    run(2 * j, 0, False, False)
                    run(2 * j + 1, 1, False, False)
                run(B - 2, 0, False, False)
                run(B - 1, 1, False, True)


def routed_experts(nc, layer, rows_in, rows_out, gathered, token, tile_expert, w_in, bias, w_out, arrived, loads, ident, E, F, gated, TILES):
    FT, FG = F // P, F * (2 if gated else 1)
    NG = 8
    with ExitStack() as stack:
        m = Pool(nc, stack, layer + "_re")
        index, turn = m.sb("index", [P, NG], I32), m.sb("turn", [P, TILES])
        xg, xT, hin = m.sb("xg", [P, NG, D]), m.sb("xT", [P, 2, KD, P]), m.sb("hin", [P, 2, FG])
        sg = m.sb("sg", [P, 2, F]) if gated else None
        h, hT, y = m.sb("h", [P, 2, F]), m.sb("hT", [P, 2, FT, P]), m.sb("y", [P, NG, D])
        PS = stack.enter_context(nc.psum_tensor(f"{layer}_re_ps", [P, 8, 512], F32))
        stored = [m.sem(f"stored{k}") for k in range(NG)]
        index_ready, x_done, x_copied, h_done, h_biased = (m.sem(n) for n in ("index_ready", "x_done", "x_copied", "h_done", "h_biased"))
        act_done, h_ready, hT_done, hT_copied, y_done, y_copied = (
            m.sem(n) for n in ("act_done", "h_ready", "hT_done", "hT_copied", "y_done", "y_copied"))

        def body(engine, run, reads=None):
            def group(first, count):
                held, loop = {}, not isinstance(first, int)

                def read(at, n):
                    lo = at if loop else max(at, -first)
                    hi = at + n if loop else min(at + n, TILES - first)
                    if hi > lo:
                        _, values = nc.values_load_multi_w_load_instructions(tile_expert[0:1, bass.ds(first + lo, hi - lo)], engines=[reads[0]],
                                                                             min_val=0, max_val=E - 1)
                        held.update(zip(range(lo, hi), values))
                if reads:
                    read(reads[1], 2 - reads[1])
                for k in range(count):
                    run(first + k, (k if loop else first + k) % NG, lambda d, k=k: held[k + d])
                    if reads and k + 1 < count:
                        read(k + 2, 1)
            group(-2, 2)
            group(0, NG)
            with engine.Fori(1, TILES // NG - 1) as j:
                group(NG * j, NG)
            group(TILES - NG, NG)
            group(TILES, 2)

        def inside(i, d):
            return not isinstance(i, int) or 0 <= i + d < TILES

        def later(i, d, n):
            return not isinstance(i, int) or i + d >= n

        def uses(k, r):
            return 16 // NG * (k - r) + 16

        with nc.Block() as block:

            @block.gpsimd
            def _(pool):
                def gather(k, r):
                    pool.wait_ge(index_ready, k + 1)
                    nc.gpsimd.tensor_tensor(col(turn, k), ident[:, 0:1], ident[:, 0:1], ALU.add)
                    pool.indirect_dma_start(xg[:, r, :], None, rows_in[:, :], bass.IndirectOffsetOnAxis(ap=index[:, r:r + 1], axis=0))\
                        .then_inc(gathered[r], 16)
                for k in range(NG):
                    gather(k, k)
                with pool.Fori(1, TILES // NG) as j:
                    for k in range(NG):
                        gather(NG * j + k, k)

            @block.sync
            def _(sp):
                def store(k, r):
                    sp.wait_ge(y_copied, k + 1)
                    sp.dma_start(rows_out[bass.ds(k * P, P), :], y[:, r, :]).then_inc(stored[r], 16)
                for k in range(NG):
                    store(k, k)
                with sp.Fori(1, TILES // NG) as j:
                    for k in range(NG):
                        store(NG * j + k, k)
                for r in range(NG):
                    sp.wait_ge(stored[r], 16 * (TILES // NG))

            @block.vector
            def _(dve):
                dve.wait_ge(arrived, 16 * loads)

                def take_index(k, r):
                    nc.vector.tensor_copy(index[:, r:r + 1], col(token, k)).then_inc(index_ready, 1)
                for k in range(NG - 2):
                    take_index(k, k)

                def run(i, r, expert):
                    if inside(i, NG):
                        if later(i, NG, NG):
                            dve.wait_ge(x_done, i + 1)
                        take_index(i + NG, r)
                    if inside(i, 0) and gated:
                        u = r % 2
                        dve.wait_ge(act_done, i + 1)
                        if later(i, 0, 2):
                            dve.wait_ge(hT_done, i - 1)
                        nc.vector.tensor_tensor(h[:, u, :], sg[:, u, :], hin[:, u, F:], ALU.mult).then_inc(h_ready, 1)
                    if inside(i, 1):
                        k, u = i + 1, (r + 1) % 2
                        dve.wait_ge(h_done, k + 1)
                        if later(i, 1, 2):
                            dve.wait_ge(h_ready, k - 1)
                        nc.vector.tensor_tensor(hin[:, u, :], PS[:, 2 + u, 0:FG], row(bias, expert(1)), ALU.add).then_inc(h_biased, 1)
                    if inside(i, -2):
                        k, q, u = i - 2, (r - 2) % NG, r % 2
                        dve.wait_ge(y_done, k + 1)
                        if later(i, -2, NG):
                            dve.wait_ge(stored[q], uses(k - NG, q))
                        nc.vector.tensor_copy(y[:, q, :], PS[:, 6 + u, 0:D]).then_inc(y_copied, 1)
                body(dve, run, (mybir.EngineType.DVE, 1))

            @block.scalar
            def _(act):
                def run(i, r, expert):
                    if inside(i, 2):
                        k, u = i + 2, r % 2
                        act.wait_ge(x_done, k + 1)
                        if later(i, 2, 2):
                            act.wait_ge(h_done, k - 1)
                        nc.scalar.activation(xT[:, u, :, :], PS[:, u, 0:D].rearrange("p (k s) -> p k s", k=KD), ACT.Copy)\
                          .then_inc(x_copied, 1)
                    if inside(i, -1):
                        k, u = i - 1, (r - 1) % 2
                        act.wait_ge(hT_done, k + 1)
                        if later(i, -1, 2):
                            act.wait_ge(y_done, k - 1)
                        nc.scalar.activation(hT[:, u, :, :], PS[:, 4 + u, 0:F].rearrange("p (f s) -> p f s", f=FT), ACT.Copy)\
                          .then_inc(hT_copied, 1)
                    if inside(i, 1):
                        k, u = i + 1, (r + 1) % 2
                        act.wait_ge(h_biased, k + 1)
                        if gated:
                            if later(i, 1, 2):
                                act.wait_ge(h_ready, k - 1)
                            nc.scalar.activation(sg[:, u, :], hin[:, u, 0:F], ACT.Silu).then_inc(act_done, 1)
                        else:
                            if later(i, 1, 2):
                                act.wait_ge(hT_done, k - 1)
                            nc.scalar.activation(h[:, u, :], hin[:, u, :], ACT.Gelu).then_inc(h_ready, 1)
                body(act, run)

            @block.tensor
            def _(pe):
                pe.wait_ge(arrived, 16 * loads)

                def run(i, r, expert):
                    if inside(i, 2):
                        k, q, u = i + 2, (r + 2) % NG, r % 2
                        pe.wait_ge(gathered[q], uses(k, q))
                        if later(i, 2, 2):
                            pe.wait_ge(x_copied, k - 1)
                        for d in range(KD):
                            last = nc.tensor.transpose(PS[:, u, d * P:(d + 1) * P], xg[:, q, d * P:(d + 1) * P], ident[:, :])
                        last.then_inc(x_done, 1)
                    if inside(i, -1):
                        k, u = i - 1, (r - 1) % 2
                        pe.wait_ge(h_ready, k + 1)
                        if later(i, -1, 2):
                            pe.wait_ge(hT_copied, k - 1)
                        for f in range(FT):
                            last = nc.tensor.transpose(PS[:, 4 + u, f * P:(f + 1) * P], h[:, u, f * P:(f + 1) * P], ident[:, :])
                        last.then_inc(hT_done, 1)
                    if inside(i, 1):
                        k, u = i + 1, (r + 1) % 2
                        pe.wait_ge(x_copied, k + 1)
                        if later(i, 1, 2):
                            pe.wait_ge(h_biased, k - 1)
                        for d in range(KD):
                            last = nc.tensor.matmul(PS[:, 2 + u, 0:FG], xT[:, u, d, :], w_in[:, one(expert(1)), d, :].rearrange("p o n -> p (o n)"),
                                                    start=(d == 0), stop=(d == KD - 1))
                        last.then_inc(h_done, 1)
                    if inside(i, -2):
                        k, u = i - 2, r % 2
                        pe.wait_ge(hT_copied, k + 1)
                        if later(i, -2, 2):
                            pe.wait_ge(y_copied, k - 1)
                        for f in range(FT):
                            last = nc.tensor.matmul(PS[:, 6 + u, 0:D], hT[:, u, f, :], w_out[:, one(expert(-2)), f, :].rearrange("p o n -> p (o n)"),
                                                    start=(f == 0), stop=(f == FT - 1))
                        last.then_inc(y_done, 1)
                body(pe, run, (mybir.EngineType.PE, -2))


def collect(nc, layer, X, ident, gathered, rows, slot, share, K):
    NB = 8 // K
    with ExitStack() as stack:
        m = Pool(nc, stack, layer + "_collect")
        index, turn, y = m.sb("index", [P, NB, K], I32), m.sb("turn", [P, B]), m.sb("y", [P, NB, K, D])
        index_ready, added = m.sem("index_ready"), m.sem("added")
        with nc.Block() as block:

            @block.gpsimd
            def _(pool):
                def run(b, u):
                    pool.wait_ge(index_ready, b + 1)
                    nc.gpsimd.tensor_tensor(col(turn, b), ident[:, 0:1], ident[:, 0:1], ALU.add)
                    for k in range(K):
                        pool.indirect_dma_start(y[:, u, k, :], None, rows[:, :], bass.IndirectOffsetOnAxis(ap=index[:, u, k:k + 1], axis=0))\
                            .then_inc(gathered[u], 16)
                for u in range(NB):
                    run(u, u)
                with pool.Fori(1, B // NB) as j:
                    for u in range(NB):
                        run(NB * j + u, u)

            @block.vector
            def _(dve):
                def take_index(b, u):
                    if not isinstance(b, int) or b >= NB:
                        dve.wait_ge(added, K * (b - NB + 1))
                    nc.vector.tensor_copy(index[:, u, :], row(slot, b)).then_inc(index_ready, 1)

                def sums(b, u):
                    dve.wait_ge(gathered[u], 16 * K // NB * (b - u) + 16 * K)
                    for k in range(K):
                        if k or not isinstance(b, int) or b:
                            dve.wait_ge(added, K * b + k)
                        nc.vector.scalar_tensor_tensor(row(X, b), y[:, u, k, :], row(share, b)[:, k:k + 1], row(X, b), ALU.mult, ALU.add)\
                          .then_inc(added, 1)
                for u in range(NB):
                    take_index(u, u)
                for u in range(NB):
                    sums(u, u)
                    take_index(NB + u, u)
                with dve.Fori(1, B // NB - 1) as j:
                    for u in range(NB):
                        sums(NB * j + u, u)
                        take_index(NB * j + NB + u, u)
                for u in range(NB):
                    sums(B - NB + u, u)


def mixture(nc, layer, X, ident, below, gathered, router, router_bias, b2, weights, shared_blob, E, F, K, gated):
    w_in, bias, w_out = weights
    FT, FG = F // P, F * (2 if gated else 1)
    shared = 2 if gated else 0
    TILES = -(-((B * S * K + E * (P - 1)) // P) // 8) * 8
    rows_in = nc.dram_tensor(f"{layer}_rows_in", (B * S, D), F32, kind="Internal").ap()
    rows_out = nc.dram_tensor(f"{layer}_rows_out", (TILES * P, D), F32, kind="Internal").ap()
    with ExitStack() as stack:
        m = Pool(nc, stack, layer)
        arrived = m.sem("arrived")
        w_in_sb, bias_sb, w_out_sb = m.sb("w_in", [P, E, KD, FG]), m.sb("bias", [P, E, FG]), m.sb("w_out", [P, E, FT, D])
        combine = m.sb("combine", [P, B, E + shared])
        chosen, share, slot = m.sb("chosen", [P, B, K]), m.sb("share", [P, B, K]), m.sb("slot", [P, B, K])
        token, tile_expert = m.sb("token", [P, TILES]), m.sb("tile_expert", [1, TILES], I32)
        rows = b2.shape[0]
        b2_sb = m.sb("b2", [rows, D])
        GROUP = E // 8
        background = [(bias_sb[:, :, :].rearrange("p e f -> p (e f)"), bias.partition_broadcast(P))]
        for g in range(0, E, GROUP):
            background.append((w_in_sb[:, g:g + GROUP, :, :], w_in[:, g:g + GROUP, :, :]))
            background.append((w_out_sb[:, g:g + GROUP, :, :], w_out[:, g:g + GROUP, :, :]))
        with ExitStack() as early:
            me = Pool(nc, early, layer + "_r")
            mean, rstd = me.sb("mean", [P, B]), me.sb("rstd", [P, B])
            XT = me.sb("XT", [P, KD, B, P]) if shared else None
            logits, rw = me.sb("logits", [P, B, E]), me.sb("rw", [P, KD, E])
            loads = [(rw[:, :, :], router.rearrange("(k p) e -> p k e", p=P)), (b2_sb[:, :], b2)]
            rb = None
            if router_bias is not None:
                rb = me.sb("rb", [P, E])
                loads.append((rb[:, :], router_bias.partition_broadcast(P)))
            norm_statistics(nc, layer, X, mean, rstd, 1.0, loads)
            norm_and_product(nc, layer, X, ident, mean, rstd, rw, logits, XT=XT, small_bias=rb, rows_out=rows_in)
            if gated:
                route_grouped(nc, layer, logits, combine, chosen, share, E, 8, 4, K, background, arrived)
            else:
                route_top2(nc, layer, logits, combine, chosen, share, E, background, arrived)
            add_product(nc, layer, X, ident, combine, b2_sb, rows)
            assign_slots(nc, layer, combine, chosen, slot, token, tile_expert, below, ident, E, K, TILES)
            if shared:
                experts(nc, layer, X, XT, combine[:, :, E:], shared_blob, shared, F, gated)
        routed_experts(nc, layer, rows_in, rows_out, gathered[4:], token, tile_expert, w_in_sb, bias_sb, w_out_sb, arrived, len(background),
                       ident, E, F, gated, TILES)
        collect(nc, layer, X, ident, gathered[0:4], rows_out, slot, share, K)


def lora(nc, layer, X, ident, small, small_bias, base, base_bias, loraB, E, R, scaling):
    with ExitStack() as stack:
        m = Pool(nc, stack, layer)
        mean, rstd = m.sb("mean", [P, B]), m.sb("rstd", [P, B])
        sm, bs = m.sb("small", [P, KD, E + R]), m.sb("base", [P, KD, D])
        smb, bsb, lb = m.sb("small_bias", [P, E + R]), m.sb("base_bias", [P, D]), m.sb("loraB", [E * R, D])
        both, gate, gate16 = m.sb("both", [P, B, E + R]), m.sb("gate", [P, B, E]), m.sb("gate16", [P, B, E], BF16)
        top, outer = m.sb("top", [P, B]), m.sb("outer", [P, B, E * R])
        loads = [(sm[:, :, 0:E], small[0].rearrange("(k p) e -> p k e", p=P)),
                 (sm[:, :, E:], small[1].rearrange("(k p) e -> p k e", p=P)),
                 (smb[:, 0:E], small_bias.partition_broadcast(P)),
                 (bs[:, :, :], base.rearrange("(k p) e -> p k e", p=P)),
                 (bsb[:, :], base_bias.partition_broadcast(P)),
                 (lb[:, :], loraB.rearrange("e r n -> (e r) n"))]
        norm_statistics(nc, layer, X, mean, rstd, 1.0, loads, zeros=[smb[:, :]])
        norm_and_product(nc, layer, X, ident, mean, rstd, sm, both, base=bs, small_bias=smb, base_bias=bsb)
        chain, act_ready, e_ready = m.sem("chain"), m.sem("act_ready"), m.sem("e_ready")
        with nc.Block() as block:

            @block.scalar
            def _(act):
                act.wait_ge(act_ready, 1)
                nc.scalar.activation(gate[:, :, :], gate[:, :, :], ACT.Exp).then_inc(e_ready, 1)

            @block.vector
            def _(dve):
                c = Chain(dve, chain)
                c.do(nc.vector.tensor_copy(gate[:, :, :], both[:, :, 0:E]))
                softmax_rows(nc, c, dve, act_ready, e_ready, gate[:, :, :], top[:, :], E)
                c.do(nc.vector.tensor_copy(gate16[:, :, :], gate[:, :, :]))
                c.do(nc.vector.tensor_scalar(gate[:, :, :], gate16[:, :, :], float(scaling), None, ALU.mult))
                for r in range(R):
                    c.do(nc.vector.tensor_tensor(outer[:, :, :].rearrange("p b (e r) -> p b e r", r=R)[:, :, :, r],
                                                 gate[:, :, :], spread(both[:, :, E + r], E), ALU.mult))
        add_product(nc, layer, X, ident, outer, lb, E * R)


QMAX = 32767.0
WBLOCK, WQMAX = 32, 7.0
SIG = 65536.0


def quantized_ffn(nc, layer, X, ident, w_gate, w_up, w_down, F):
    FT = F // P
    NT = 512
    NN = B * P // NT
    CH = 1024
    NC = FT * B * P // CH
    with ExitStack() as stack:
        m = Pool(nc, stack, layer)
        mean, rstd = m.sb("mean", [P, B]), m.sb("rstd", [P, B])
        G, U = m.sb("G", [P, FT, B * P]), m.sb("U", [P, FT, B * P])
        XQ = m.sb("XQ", [P, KD, B, P])
        wT = [m.sb(f"wT{k}", [P, KD * F]) for k in range(3)]
        big, step, inv = m.sb("big", [P, 5]), m.sb("step", [P, 5]), m.sb("inv", [P, 5])
        part = m.sb("part", [P, 5])
        magic = m.sb("magic", [P, 1])
        found, reduced, scaled, chain = m.sem("found"), m.sem("reduced"), m.sem("scaled"), m.sem("chain")
        RMAX = bass.bass_isa.ReduceOp.absmax

        def all_tokens(pool, k):
            pool.wait_ge(found, k + 1)
            nc.gpsimd.partition_all_reduce(big[:, k:k + 1], part[:, k:k + 1], P, RMAX).then_inc(reduced, 1)

        def steps(dve, c, k, factor):
            dve.wait_ge(reduced, k + 1)
            c.do(nc.vector.tensor_scalar(step[:, k:k + 1], big[:, k:k + 1], factor / QMAX, 1e-12, ALU.mult, ALU.max))
            c.do(nc.vector.reciprocal(inv[:, k:k + 1], step[:, k:k + 1]))
            c.do(nc.vector.tensor_scalar(inv[:, k:k + 1], inv[:, k:k + 1], factor, None, ALU.mult))

        with ExitStack() as early:
            me = Pool(nc, early, layer)
            wn = [me.sb(f"wn{k}", [P, KD * F]) for k in range(3)]
            wa, wi = me.sb("wa", [P, KD * F // WBLOCK]), me.sb("wi", [P, KD * F // WBLOCK])
            XN = me.sb("XN", [P, B, D])
            xq = me.sb("xq", [P, 2, D])
            loads = [(wn[0][:, :].rearrange("p (t n) -> p t n", t=FT), w_gate.rearrange("(t p) n -> p t n", p=P)),
                     (wn[1][:, :].rearrange("p (t n) -> p t n", t=FT), w_up.rearrange("(t p) n -> p t n", p=P)),
                     (wn[2][:, :].rearrange("p (t n) -> p t n", t=KD), w_down.rearrange("(t p) n -> p t n", p=P))]
            norm_statistics(nc, layer, X, mean, rstd, 1.0, loads)

            PS = early.enter_context(nc.psum_tensor(f"{layer}_q_ps", [P, 8, 512], F32))
            normed, w_ready, wt_done, wt_copied = me.sem("normed"), me.sem("w_ready"), me.sem("wt_done"), me.sem("wt_copied")
            rounded, x_done, x_copied = me.sem("rounded"), me.sem("x_done"), me.sem("x_copied")
            with nc.Block() as block:

                @block.gpsimd
                def _(pool):
                    nc.gpsimd.memset(magic[:, :], MAGIC)
                    all_tokens(pool, 0)

                @block.vector
                def _(dve):
                    c = Chain(dve, chain)
                    with dve.Fori(0, B // 4) as j:
                        for k in range(4):
                            b = 4 * j + k
                            nc.vector.tensor_scalar(row(XN, b), row(X, b), col(mean, b), col(rstd, b), ALU.subtract, ALU.mult)\
                              .then_inc(normed, 1)
                    dve.wait_ge(normed, B)
                    nc.vector.tensor_reduce(part[:, 0:1], XN[:, :, :].rearrange("p b d -> p (b d)"), AXIS.X, ALU.max,
                                            apply_absolute_value=True).then_inc(found, 1)
                    for k in range(3):
                        w = wn[k][:, :].rearrange("p (a n) -> p a n", n=WBLOCK)
                        NB = KD * F // WBLOCK
                        if k:
                            dve.wait_ge(w_ready, k)
                        c.do(nc.vector.tensor_reduce(wa[:, :], w, AXIS.X, ALU.max, apply_absolute_value=True))
                        c.do(nc.vector.tensor_scalar(wa[:, :], wa[:, :], 1.0 / WQMAX, 1e-12, ALU.mult, ALU.max))
                        c.do(nc.vector.reciprocal(wi[:, :], wa[:, :]))
                        c.do(nc.vector.tensor_tensor(w, w, wi[:, :].unsqueeze(2).to_broadcast([P, NB, WBLOCK]), ALU.mult))
                        c.do(nc.vector.tensor_scalar(w, w, MAGIC, MAGIC, ALU.add, ALU.subtract))
                        c.do(nc.vector.tensor_scalar(w, w, -WQMAX - 1.0, WQMAX, ALU.max, ALU.min))
                        nc.vector.tensor_tensor(w, w, wa[:, :].unsqueeze(2).to_broadcast([P, NB, WBLOCK]), ALU.mult).then_inc(w_ready, 1)
                    steps(dve, c, 0, 1.0)

                @block.tensor
                def _(pe):
                    for k in range(3):
                        pe.wait_ge(w_ready, k + 1)
                        for q in range(KD * FT):
                            g = 3 * k + q // 4
                            if q % 4 == 0 and g >= 8:
                                pe.wait_ge(wt_copied, g - 7)
                            if k < 2:
                                d, f = divmod(q, FT)
                                src = wn[k][:, f * D + d * P:f * D + (d + 1) * P]
                            else:
                                f, o = divmod(q, KD)
                                src = wn[k][:, o * F + f * P:o * F + (f + 1) * P]
                            t = nc.tensor.transpose(PS[:, g % 8, (q % 4) * P:(q % 4 + 1) * P], src, ident[:, :])
                            if q % 4 == 3:
                                t.then_inc(wt_done, 1)

                @block.scalar
                def _(act):
                    for g in range(9):
                        act.wait_ge(wt_done, g + 1)
                        nc.scalar.activation(wT[g // 3][:, (g % 3) * 512:(g % 3 + 1) * 512], PS[:, g % 8, :], ACT.Copy).then_inc(wt_copied, 1)

            with nc.Block() as block:

                @block.vector
                def _(dve):
                    def run(j):
                        pair, both = XN[:, bass.ds(2 * j, 2), :], xq[:, :, :]
                        nc.vector.tensor_scalar(pair, pair, inv[:, 0:1], MAGIC, ALU.mult, ALU.add).then_inc(rounded, 1)
                        if not isinstance(j, int):
                            dve.wait_ge(x_done, 2 * j)
                        dve.wait_ge(rounded, 3 * j + 1)
                        nc.vector.tensor_scalar(both, pair, MAGIC + QMAX, MAGIC - QMAX - 1.0, ALU.min, ALU.max).then_inc(rounded, 1)
                        dve.wait_ge(rounded, 3 * j + 2)
                        nc.vector.tensor_scalar(both, both, MAGIC, None, ALU.subtract).then_inc(rounded, 1)
                    run(0)
                    with dve.Fori(1, B // 2) as j:
                        run(j)

                @block.tensor
                def _(pe):
                    def run(i, u, j):
                        pe.wait_ge(rounded, 3 * j + 3)
                        if not isinstance(i, int):
                            pe.wait_ge(x_copied, i - 1)
                        for d in range(KD):
                            last = nc.tensor.transpose(PS[:, u, d * P:(d + 1) * P], xq[:, u, d * P:(d + 1) * P], ident[:, :])
                        last.then_inc(x_done, 1)
                    run(0, 0, 0)
                    run(1, 1, 0)
                    with pe.Fori(1, B // 2) as j:
                        run(2 * j, 0, j)
                        run(2 * j + 1, 1, j)

                @block.gpsimd
                def _(pool):
                    pool.nop()

                @block.scalar
                def _(act):
                    for i in range(B):
                        act.wait_ge(x_done, i + 1)
                        nc.scalar.activation(XQ[:, :, i, :], PS[:, i % 2, 0:D].rearrange("p (k s) -> p k s", k=KD), ACT.Copy)\
                          .then_inc(x_copied, 1)

        with ExitStack() as middle:
            mm = Pool(nc, middle, layer)
            BANKS = 6
            PS = middle.enter_context(nc.psum_tensor(f"{layer}_m_ps", [P, 8, 512], F32))
            am = mm.sb("am", [P, 2, NN, FT])
            p_done, p_read, am_done = mm.sem("p_done"), mm.sem("p_read"), mm.sem("am_done")
            PER = 2 * FT
            with nc.Block() as block:

                @block.tensor
                def _(pe):
                    def run(n):
                        for q in range(PER):
                            k, f = divmod(q, FT)
                            if not isinstance(n, int) or q >= BANKS:
                                pe.wait_ge(p_read, PER * n + q - BANKS + 1)
                            for d in range(KD):
                                rhs = XQ[:, d, bass.ds(n * (NT // P), NT // P), :].rearrange("p b s -> p (b s)")
                                last = nc.tensor.matmul(PS[:, q % BANKS, :], wT[k][:, d * F + f * P:d * F + (f + 1) * P], rhs,
                                                        start=(d == 0), stop=(d == KD - 1))
                            last.then_inc(p_done, 1)
                    run(0)
                    with pe.Fori(1, NN) as n:
                        run(n)

                @block.scalar
                def _(act):
                    for n in range(NN):
                        for q in range(PER):
                            k, f = divmod(q, FT)
                            act.wait_ge(p_done, PER * n + q + 1)
                            nc.scalar.activation((G, U)[k][:, f, n * NT:(n + 1) * NT], PS[:, q % BANKS, :], ACT.Identity, scale=step[:, 0:1])\
                              .then_inc(p_read, 1)

                @block.vector
                def _(dve):
                    for n in range(NN):
                        for k in range(2):
                            dve.wait_ge(p_read, PER * n + FT * (k + 1))
                            nc.vector.tensor_reduce(am[:, k, n, :], (G, U)[k][:, :, n * NT:(n + 1) * NT], AXIS.X, ALU.max,
                                                    apply_absolute_value=True).then_inc(am_done, 1)
                    c = Chain(dve, mm.sem("chain1"))
                    dve.wait_ge(am_done, 2 * NN)
                    nc.vector.tensor_reduce(part[:, 1:3], am[:, :, :, :].rearrange("p k n f -> p k (n f)"), AXIS.X, ALU.max).then_inc(found, 2)
                    steps(dve, c, 1, 1.0)
                    steps(dve, c, 2, 1.0)

                @block.gpsimd
                def _(pool):
                    all_tokens(pool, 1)
                    all_tokens(pool, 2)

        def chunk(t, i):
            return t[:, :, :].rearrange("p f s -> p (f s)")[:, bass.ds(i * CH, CH)]

        with ExitStack() as late:
            ml = Pool(nc, late, layer)
            gq, sg = ml.sb("gq", [P, 2, CH]), ml.sb("sg", [P, 2, CH])
            on_grid, clipped, q_ready, sg_ready, sg_clipped, prod = (ml.sem(n) for n in ("on_grid", "clipped", "q_ready", "sg_ready", "sg_clipped", "prod"))
            with nc.Block() as block:

                @block.scalar
                def _(act):
                    def grid(i):
                        nc.scalar.activation(chunk(G, i), chunk(G, i), ACT.Identity, bias=magic[:, :], scale=inv[:, 1:2]).then_inc(on_grid, 1)

                    def run(i, u):
                        act.wait_ge(q_ready, i + 1)
                        if not isinstance(i, int) or i >= 2:
                            act.wait_ge(prod, i - 1)
                        nc.scalar.activation(sg[:, u, :], gq[:, u, :], ACT.Sigmoid, scale=step[:, 1:2]).then_inc(sg_ready, 1)
                        act.wait_ge(sg_ready, 2 * i + 1)
                        nc.scalar.activation(sg[:, u, :], sg[:, u, :], ACT.Identity, bias=magic[:, :], scale=SIG).then_inc(sg_ready, 1)
                    grid(0)
                    grid(1)
                    run(0, 0)
                    grid(2)
                    run(1, 1)
                    grid(3)
                    with act.Fori(1, NC // 2 - 1) as j:
                        run(2 * j, 0)
                        grid(2 * j + 2)
                        run(2 * j + 1, 1)
                        grid(2 * j + 3)
                    run(NC - 2, 0)
                    run(NC - 1, 1)
                    with act.Fori(0, NC) as i:
                        nc.scalar.activation(chunk(U, i), chunk(U, i), ACT.Identity, bias=magic[:, :], scale=inv[:, 2:3]).then_inc(on_grid, 1)

                @block.vector
                def _(dve):
                    def to_integers(i, u):
                        if not isinstance(i, int):
                            dve.wait_ge(prod, i - 1)
                        dve.wait_ge(on_grid, i + 1)
                        nc.vector.tensor_scalar(gq[:, u, :], chunk(G, i), MAGIC + QMAX, MAGIC - QMAX - 1.0, ALU.min, ALU.max)\
                          .then_inc(clipped, 1)
                        dve.wait_ge(clipped, i + 1)
                        nc.vector.tensor_scalar(gq[:, u, :], gq[:, u, :], MAGIC, None, ALU.subtract).then_inc(q_ready, 1)

                    def product(i, u):
                        dve.wait_ge(sg_ready, 2 * i + 2)
                        nc.vector.tensor_scalar(sg[:, u, :], sg[:, u, :], MAGIC + SIG - 1.0, MAGIC, ALU.min, ALU.max).then_inc(sg_clipped, 1)
                        dve.wait_ge(sg_clipped, i + 1)
                        nc.vector.scalar_tensor_tensor(chunk(G, i), sg[:, u, :], MAGIC, gq[:, u, :], ALU.subtract, ALU.mult).then_inc(prod, 1)
                    to_integers(0, 0)
                    to_integers(1, 1)
                    with dve.Fori(1, NC // 2) as j:
                        product(2 * j - 2, 0)
                        to_integers(2 * j, 0)
                        product(2 * j - 1, 1)
                        to_integers(2 * j + 1, 1)
                    product(NC - 2, 0)
                    product(NC - 1, 1)
                    dve.wait_ge(prod, NC)
                    c = Chain(dve, ml.sem("chain3"))
                    c.do(nc.vector.tensor_reduce(part[:, 3:4], G[:, :, :].rearrange("p f s -> p (f s)"), AXIS.X, ALU.max,
                                                 apply_absolute_value=True))
                    nc.vector.tensor_scalar(part[:, 3:4], part[:, 3:4], step[:, 1:2], None, ALU.mult).then_inc(found, 1)
                    steps(dve, c, 3, 1.0 / SIG)
                    c.do(nc.vector.tensor_tensor(inv[:, 3:4], inv[:, 3:4], step[:, 1:2], ALU.mult))

                @block.gpsimd
                def _(pool):
                    all_tokens(pool, 3)

            grid2, low2, int2, up2, prod2 = (ml.sem(n) for n in ("grid2", "low2", "int2", "up2", "prod2"))
            with nc.Block() as block:

                @block.scalar
                def _(act):
                    with act.Fori(0, NC) as i:
                        nc.scalar.activation(chunk(G, i), chunk(G, i), ACT.Identity, bias=magic[:, :], scale=inv[:, 3:4]).then_inc(grid2, 1)

                @block.vector
                def _(dve):
                    with dve.Fori(0, NC // 2) as j:
                        for k in range(2):
                            i = 2 * j + k
                            nc.vector.tensor_scalar(chunk(U, i), chunk(U, i), MAGIC + QMAX, MAGIC - QMAX - 1.0, ALU.min, ALU.max).then_inc(up2, 1)
                        for k in range(2):
                            i = 2 * j + k
                            dve.wait_ge(grid2, i + 1)
                            nc.vector.tensor_scalar(chunk(G, i), chunk(G, i), MAGIC + QMAX, MAGIC - QMAX - 1.0, ALU.min, ALU.max).then_inc(low2, 1)
                        for k in range(2):
                            i = 2 * j + k
                            dve.wait_ge(low2, i + 1)
                            nc.vector.tensor_scalar(chunk(G, i), chunk(G, i), MAGIC, None, ALU.subtract).then_inc(int2, 1)
                        for k in range(2):
                            i = 2 * j + k
                            dve.wait_ge(up2, i + 1)
                            dve.wait_ge(int2, i + 1)
                            nc.vector.scalar_tensor_tensor(chunk(G, i), chunk(U, i), MAGIC, chunk(G, i), ALU.subtract, ALU.mult).then_inc(prod2, 1)
                    dve.wait_ge(prod2, NC)
                    c = Chain(dve, ml.sem("chain2"))
                    c.do(nc.vector.tensor_reduce(part[:, 4:5], G[:, :, :].rearrange("p f s -> p (f s)"), AXIS.X, ALU.max,
                                                 apply_absolute_value=True))
                    c.do(nc.vector.tensor_tensor(part[:, 3:4], step[:, 2:3], step[:, 3:4], ALU.mult))
                    nc.vector.tensor_tensor(part[:, 4:5], part[:, 4:5], part[:, 3:4], ALU.mult).then_inc(found, 1)
                    steps(dve, c, 4, 1.0)
                    c.do(nc.vector.tensor_tensor(inv[:, 4:5], inv[:, 4:5], part[:, 3:4], ALU.mult))

                @block.gpsimd
                def _(pool):
                    all_tokens(pool, 4)

            PS = late.enter_context(nc.psum_tensor(f"{layer}_d_ps", [P, 8, 512], F32))
            ob = ml.sb("ob", [P, 2, FT, P])
            grid3, low3, int3, d_done, d_added = (ml.sem(n) for n in ("grid3", "low3", "int3", "d_done", "d_added"))

            def tokens(t, i):
                return t[:, :, bass.ds(i * P, P)]

            with nc.Block() as block:

                @block.scalar
                def _(act):
                    with act.Fori(0, B) as i:
                        nc.scalar.activation(tokens(G, i), tokens(G, i), ACT.Identity, bias=magic[:, :], scale=inv[:, 4:5]).then_inc(grid3, 1)

                @block.vector
                def _(dve):
                    def integers(i, u):
                        if not isinstance(i, int):
                            dve.wait_ge(d_done, i - 1)
                        dve.wait_ge(grid3, i + 1)
                        nc.vector.tensor_scalar(ob[:, u, :, :], tokens(G, i), MAGIC + QMAX, MAGIC - QMAX - 1.0, ALU.min, ALU.max)\
                          .then_inc(low3, 1)
                        dve.wait_ge(low3, i + 1)
                        nc.vector.tensor_scalar(ob[:, u, :, :], ob[:, u, :, :], MAGIC, None, ALU.subtract).then_inc(int3, 1)

                    def add(i, u):
                        dve.wait_ge(d_done, i + 1)
                        nc.vector.scalar_tensor_tensor(row(X, i), PS[:, u, 0:D], step[:, 4:5], row(X, i), ALU.mult, ALU.add)\
                          .then_inc(d_added, 1)
                    integers(0, 0)
                    integers(1, 1)
                    with dve.Fori(1, B // 2) as j:
                        add(2 * j - 2, 0)
                        integers(2 * j, 0)
                        add(2 * j - 1, 1)
                        integers(2 * j + 1, 1)
                    add(B - 2, 0)
                    add(B - 1, 1)

                @block.tensor
                def _(pe):
                    def run(i, u):
                        pe.wait_ge(int3, i + 1)
                        if not isinstance(i, int):
                            pe.wait_ge(d_added, i - 1)
                        for f in range(FT):
                            last = nc.tensor.matmul(PS[:, u, 0:D], ob[:, u, f, :], wT[2][:, f * D:(f + 1) * D], start=(f == 0), stop=(f == FT - 1))
                        last.then_inc(d_done, 1)
                    run(0, 0)
                    run(1, 1)
                    with pe.Fori(1, B // 2) as j:
                        run(2 * j, 0)
                        run(2 * j + 1, 1)
def program(nc, a, out):
    with ExitStack() as stack:
        X = stack.enter_context(nc.sbuf_tensor("X", [P, B, D], F32))
        ident = stack.enter_context(nc.sbuf_tensor("ident", [P, P], F32))
        below = stack.enter_context(nc.sbuf_tensor("below", [P, P], F32))
        parity = stack.enter_context(nc.sbuf_tensor("parity", [P, 2], F32))
        gathered = [[stack.enter_context(nc.semaphore(f"{layer}_gathered{k}")) for k in range(12)] for layer in ("f0", "f3")]
        constants(nc, a["x"], a["parity"], X, ident, below, parity)
        ctx, ctxT = a["ctx"], a["ctxT"]
        attention(nc, "a0", X, ident, below, parity, ctx, ctxT, 1 / 16, "int_qk", a["mask_qk"], wo=a["L0_woT"], bo=a["L0_bo"])
        mixture(nc, "f0", X, ident, below, gathered[0], a["L0_router"], None, a["L0_b2"], (a["L0_w1"], a["L0_b1"], a["L0_w2"]), None, 8, 512, 2, False)
        attention(nc, "a1", X, ident, below, parity, ctx, ctxT, 1 / 4, "inverted", (a["mask_bool"], a["mask_boolT"]))
        quantized_ffn(nc, "f1", X, ident, a["L1_gate"], a["L1_up"], a["L1_down"], 768)
        attention(nc, "a2", X, ident, below, parity, ctx, ctxT, 1 / 4, "causal", wq=a["L2_wq"], bq=a["L2_bq_heads"], wk=a["L2_wq"], bk=a["L2_bq_heads"],
                  wv=a["L2_wq"], bv=a["L2_bq"], wo=a["L2_wo"], bo=a["L2_bo"])
        lora(nc, "f2", X, ident, (a["L2_router"], a["L2_loraA"]), a["L2_router_b"], a["L2_base"], a["L2_base_b"], a["L2_loraB"], 8, 8, 2.0)
        attention(nc, "a3", X, ident, below, parity, ctx, ctxT, 1 / 4, "int_k", a["mask_k"], wq=a["L3_wq"], bq=a["L3_bq_heads"], wk=a["L3_wk"],
                  bk=a["L3_bk_heads"], wv=a["L3_wv"], bv=a["L3_bv"], wo=a["L3_wo"], bo=a["L3_bo"])
        mixture(nc, "f3", X, ident, below, gathered[1], a["L3_gw"], a["L3_gb"], a["L3_b2"], (a["L3_w13"], a["L3_b13"], a["L3_w2"]), a["L3_shared"],
                32, 128, 4, True)
        store(nc, X, out)


def blob_of(ins, biases, w2):
    E, F, _ = w2.shape
    parts = [np.transpose(np.asarray(w).reshape(E, KD, P, F // P, P), (0, 2, 3, 1, 4)).reshape(E, P, KD * F) for w in ins]
    parts += [np.transpose(np.asarray(b).reshape(E, F // P, P), (0, 2, 1)) for b in biases]
    parts.append(np.transpose(np.asarray(w2).reshape(E, F // P, P, D), (0, 2, 1, 3)).reshape(E, P, F // P * D))
    return np.concatenate(parts, axis=2)


def by_tile(b):
    return np.transpose(np.asarray(b).reshape(KD, P))


def halves(shared, axis):
    return np.stack(np.split(np.asarray(shared), 2, axis=axis))


def by_feature(w):
    E, I, O = w.shape
    return np.transpose(np.asarray(w).reshape(E, I // P, P, O), (2, 0, 1, 3))


def kernel(x, ctx_1024, mask_Bx1xSxS2_ik1, mask_BxS2_bf1, mask_Bx1x1xS2_ik0, **w):
    import concourse.bacc as bacc
    from concourse.bass_utils import run_bass_kernel_spmd

    laid = {
        "x": x, "ctx": ctx_1024, "ctxT": np.transpose(ctx_1024, (0, 2, 1)),
        "parity": np.stack([(np.arange(P) // DH) % 2 == e for e in range(2)], 1).astype(np.float32),
        "mask_qk": mask_Bx1xSxS2_ik1, "mask_k": mask_Bx1x1xS2_ik0,
        "mask_bool": np.ascontiguousarray(mask_BxS2_bf1).view(np.uint8),
        "mask_boolT": np.ascontiguousarray(np.transpose(mask_BxS2_bf1)).view(np.uint8),
        "L0_woT": np.transpose(w["L0_xattn_W_out"]), "L0_bo": w["L0_xattn_b_out"],
        "L1_gate": w["L1_ffn_w_gate"], "L1_up": w["L1_ffn_w_up"], "L1_down": w["L1_ffn_w_down"],
        "L2_wq": w["L2_xattn_Wq"], "L2_bq": w["L2_xattn_bq"], "L2_wo": w["L2_xattn_Wo"], "L2_bo": w["L2_xattn_bo"],
        "L2_base": np.transpose(w["L2_ffn_base_w"]), "L2_base_b": w["L2_ffn_base_b"], "L2_loraA": w["L2_ffn_lora_A"],
        "L2_loraB": w["L2_ffn_lora_B"], "L2_router": np.transpose(w["L2_ffn_router_w"]), "L2_router_b": w["L2_ffn_router_b"],
        "L3_wq": w["L3_xattn_Wq"], "L3_bq_heads": by_tile(w["L3_xattn_bq"]), "L3_wk": w["L3_xattn_Wk"],
        "L3_bk_heads": by_tile(w["L3_xattn_bk"]), "L2_bq_heads": by_tile(w["L2_xattn_bq"]),
        "L3_wv": w["L3_xattn_Wv"], "L3_bv": w["L3_xattn_bv"], "L3_wo": w["L3_xattn_Wo"], "L3_bo": w["L3_xattn_bo"],
        "L3_gw": w["L3_ffn_gw"], "L3_gb": w["L3_ffn_gb"],
        "L3_b2": np.concatenate([w["L3_ffn_b2"], np.reshape(w["L3_ffn_sb2"], (1, D))]),
        "L3_w13": by_feature(np.concatenate([w["L3_ffn_w1"], w["L3_ffn_w3"]], 2)),
        "L3_b13": np.concatenate([w["L3_ffn_b1"], w["L3_ffn_b3"]], 1).reshape(-1), "L3_w2": by_feature(w["L3_ffn_w2"]),
        "L3_shared": blob_of([halves(w["L3_ffn_sw1"], 1), halves(w["L3_ffn_sw3"], 1)],
                             [halves(w["L3_ffn_sb1"], 0), halves(w["L3_ffn_sb3"], 0)], halves(w["L3_ffn_sw2"], 0)),
        "L0_router": np.transpose(w["L0_ffn_router_w"]), "L0_b2": w["L0_ffn_b2"],
        "L0_w1": by_feature(np.transpose(w["L0_ffn_w1"], (0, 2, 1))), "L0_b1": np.reshape(w["L0_ffn_b1"], -1),
        "L0_w2": by_feature(np.transpose(w["L0_ffn_w2"], (0, 2, 1))),
    }
    nc = bacc.Bacc("TRN2", target_bir_lowering=False, num_devices=1)
    arrays, aps = {}, {}
    for name, value in laid.items():
        value = np.ascontiguousarray(value)
        arrays[f"in_{name}"] = value
        aps[name] = nc.dram_tensor(f"in_{name}", value.shape, mybir.dt.from_np(value.dtype), kind="ExternalInput").ap()
    out = nc.dram_tensor("out", x.shape, F32, kind="ExternalOutput").ap()
    program(nc, aps, out)
    return run_bass_kernel_spmd(nc, [arrays], core_ids=[0]).results[0]["out"]
```
